# Optimizing a Trainium2 kernel written in Bass

```python
import numpy as np
import jax
import jax.numpy as jnp

def _softmax(x, axis=-1):
    return jax.nn.softmax(x, axis=axis)

def _gelu(x):
    return jax.nn.gelu(x, approximate=True)

def _silu(x):
    return jax.nn.silu(x)

def _sigmoid(x):
    return jax.nn.sigmoid(x)

def _layernorm(x, axis=-1, eps=1e-05):
    m = jnp.mean(x, axis=axis, keepdims=True)
    v = jnp.var(x, axis=axis, keepdims=True)
    return (x - m) / jnp.sqrt(v + eps)

def _scatter_add(tgt, idx, src, axis=0):
    return tgt.at[idx].add(src)

def _segment_sum(src, seg, n):
    return jax.ops.segment_sum(src, seg, n)
kernel_name = 'mk_flamingo_gated_d1_seqx_r4_26d503'

def setup_inputs(seed: int=0):
    np.random.seed(seed)
    _w = jnp.asarray

    def _rec_inputs():
        import jax
        import jax.numpy as jnp
        _rk = jax.random.key(seed)
        x = 4.136e-05 + 0.9999 * jax.random.normal(jax.random.fold_in(_rk, 1), (4, 512, 512), jnp.float32)
        _lenS = 512 - jax.random.randint(jax.random.fold_in(_rk, 7), (4,), 0, max(1, 512 // 4) + 1, jnp.int32)
        _lenS2 = 512 - jax.random.randint(jax.random.fold_in(_rk, 8), (4,), 0, max(1, 512 // 4) + 1, jnp.int32)
        _ctx_1024P = jax.random.normal(jax.random.fold_in(_rk, 11), (4, 16, 256), jnp.float32)
        _ctx_1024c = jax.random.dirichlet(jax.random.fold_in(_rk, 511), 0.3 * jnp.ones((16,), jnp.float32), (4, 512))
        _ctx_1024t = jnp.einsum('bsk,bkd->bsd', _ctx_1024c, _ctx_1024P)
        _ctx_1024t = _ctx_1024t * jax.lax.rsqrt(jnp.mean(jnp.square(_ctx_1024t)) + 1e-12) * 0.953939
        ctx_1024 = -0.000292821 + 1.00034 * (_ctx_1024t + 0.3 * jax.random.normal(jax.random.fold_in(_rk, 611), (4, 512, 256), jnp.float32))
        _g = jax.random.normal(jax.random.fold_in(_rk, 9001), (2, 1), jnp.float32)
        _g = jnp.sign(_g) * jnp.maximum(jnp.abs(_g), 1.0) + (_g == 0) * 1.0
        g_xattn = _g[0]
        g_ffn = _g[1]
        return (x, ctx_1024, g_xattn, g_ffn)
    x, ctx_1024, g_xattn, g_ffn = _rec_inputs()

    def _L0_xattn_setup():
        import jax, jax.numpy as jnp
        import numpy as np
        import math
        B, L, DM = (2, 512, 256)
        DS, DC, EXP = (16, 4, 2)
        DI = EXP * DM
        DR = math.ceil(DM / 16)
        DT_MIN, DT_MAX, DT_FLOOR = (0.001, 0.1, 0.0001)

        def _ssm_forward(hidden_states, z, in_proj_w, conv_w, conv_b, x_proj_w, dt_proj_w, dt_proj_b, A_log, D):
            b = hidden_states.shape[0]
            x = jnp.einsum('ed,bld->bel', in_proj_w, hidden_states)
            xp = jnp.pad(x, ((0, 0), (0, 0), (DC - 1, 0)))
            xc = jax.lax.conv_general_dilated(xp, conv_w[:, None, :], window_strides=(1,), padding='VALID', dimension_numbers=('NCH', 'OIH', 'NCH'), feature_group_count=DI)
            u = jax.nn.silu(xc + conv_b[None, :, None])
            x_dbl = jnp.einsum('ke,bel->bkl', x_proj_w, u)
            dt_lo = x_dbl[:, :DR]
            Bm = x_dbl[:, DR:DR + DS]
            Cm = x_dbl[:, DR + DS:]
            delta = jax.nn.softplus(jnp.einsum('er,brl->bel', dt_proj_w, dt_lo) + dt_proj_b[None, :, None])
            A = -jnp.exp(A_log)

            def step(state, xs):
                d_t, B_t, C_t, u_t = xs
                dA = jnp.exp(d_t[..., None] * A)
                state = state * dA + (d_t * u_t)[..., None] * B_t[:, None, :]
                y_t = jnp.einsum('ben,bn->be', state, C_t)
                return (state, y_t)
            xs = (jnp.moveaxis(delta, -1, 0), jnp.moveaxis(Bm, -1, 0), jnp.moveaxis(Cm, -1, 0), jnp.moveaxis(u, -1, 0))
            state0 = jnp.zeros((b, DI, DS), delta.dtype)
            _, ys = jax.lax.scan(step, state0, xs)
            y = jnp.moveaxis(ys, 0, -1)
            y = y + D[None, :, None] * u
            y = y * jax.nn.silu(z)
            return jnp.swapaxes(y, 1, 2)
        key = jax.random.key(seed)
        ks = jax.random.split(key, 8)
        hidden_states = jax.random.normal(ks[0], (B, L, DM), jnp.float32)
        z = jax.random.normal(ks[1], (B, DI, L), jnp.float32)
        in_proj_w = jax.random.normal(ks[2], (DI, DM), jnp.float32) * DM ** (-0.5)
        conv_w = jax.random.normal(ks[3], (DI, DC), jnp.float32) * DC ** (-0.5)
        conv_b = jnp.zeros((DI,), jnp.float32)
        x_proj_w = jax.random.normal(ks[4], (DR + 2 * DS, DI), jnp.float32) * DI ** (-0.5)
        dt_std = DR ** (-0.5)
        dt_proj_w = jax.random.uniform(ks[5], (DI, DR), jnp.float32, -dt_std, dt_std)
        dt = jnp.exp(jax.random.uniform(ks[6], (DI,), jnp.float32) * (math.log(DT_MAX) - math.log(DT_MIN)) + math.log(DT_MIN))
        dt = jnp.clip(dt, DT_FLOOR)
        dt_proj_b = dt + jnp.log(-jnp.expm1(-dt))
        A_log = jnp.log(jnp.broadcast_to(jnp.arange(1, DS + 1, dtype=jnp.float32), (DI, DS)))
        D = jnp.ones((DI,), jnp.float32)
        return dict(hidden_states=hidden_states, z=z, in_proj_w=in_proj_w, conv_w=conv_w, conv_b=conv_b, x_proj_w=x_proj_w, dt_proj_w=dt_proj_w, dt_proj_b=dt_proj_b, A_log=A_log, D=D)
    _L0_xattn_all = _L0_xattn_setup()
    _L0_xattn_in = {k: v for k, v in _L0_xattn_all.items() if k in ('in_proj_w', 'conv_w', 'conv_b', 'x_proj_w', 'dt_proj_w', 'dt_proj_b', 'A_log', 'D')}
    del _L0_xattn_all

    def _L0_ffn_setup():
        import jax, jax.numpy as jnp
        import numpy as np
        B, S, H, I, E, F, K, R, TOPK = (1, 256, 512, 352, 64, 8, 8, 8, 6)
        ISH = 2 * I

        def _fused_linear(x, W, qa, qb, scale, w):
            out = x @ W.T
            a = jnp.einsum('th,krh->tkr', x, qa)
            b = jnp.einsum('tkr,khr->tkh', a, qb)
            mix = jnp.einsum('tkh,tk->th', b, w)
            return out + scale[None, :] * mix

        def _moe_forward(hidden_states, gate_weight, inv_mapping, mask_up_W, gate_W, gate_qa, gate_qb, gate_scale, up_W, up_qa, up_qb, up_scale, down_W, down_qa, down_qb, down_scale, sh_gate_W, sh_up_W, sh_down_W):
            b, s, h = hidden_states.shape
            x = hidden_states.reshape(-1, h)
            T = x.shape[0]
            scores = jax.nn.softmax(x @ gate_weight.T, axis=-1)
            topk_w, topk_idx = jax.lax.top_k(scores, TOPK)
            w_dense = jnp.zeros((T, E), x.dtype).at[jnp.arange(T)[:, None], topk_idx].add(topk_w)
            flat = w_dense[:, inv_mapping]
            scalar = flat.sum(-1)
            soft = jax.nn.softmax(jnp.where(flat == 0, -1000000000.0, flat), axis=-1)

            def expert(muW, gW, gqa, gqb, gs, uW, uqa, uqb, us, dW, dqa, dqb, ds, w):
                xe = x + w @ muW.T
                gate = jax.nn.silu(_fused_linear(xe, gW, gqa, gqb, gs, w))
                up = _fused_linear(xe, uW, uqa, uqb, us, w)
                return _fused_linear(gate * up, dW, dqa, dqb, ds, w)
            outs = jax.vmap(expert, in_axes=(0,) * 13 + (1,))(mask_up_W, gate_W, gate_qa, gate_qb, gate_scale, up_W, up_qa, up_qb, up_scale, down_W, down_qa, down_qb, down_scale, soft)
            y = jnp.einsum('fth,tf->th', outs, scalar).reshape(b, s, h)
            sh = jax.nn.silu(hidden_states @ sh_gate_W.T) * (hidden_states @ sh_up_W.T) @ sh_down_W.T
            return y + sh
        key = jax.random.key(seed)
        ks = jax.random.split(key, 20)
        g = lambda k, shape, s=0.02: jax.random.normal(k, shape, jnp.float32) * s
        return {'hidden_states': jax.random.normal(ks[0], (B, S, H), jnp.float32), 'gate_weight': g(ks[1], (E, H)), 'inv_mapping': jnp.arange(E, dtype=jnp.int32).reshape(F, K), 'mask_up_W': g(ks[2], (F, H, K)), 'gate_W': g(ks[3], (F, I, H)), 'gate_qa': g(ks[4], (F, K, R, H)), 'gate_qb': g(ks[5], (F, K, I, R)), 'gate_scale': jnp.full((F, I), 0.1, jnp.float32), 'up_W': g(ks[6], (F, I, H)), 'up_qa': g(ks[7], (F, K, R, H)), 'up_qb': g(ks[8], (F, K, I, R)), 'up_scale': jnp.full((F, I), 0.1, jnp.float32), 'down_W': g(ks[9], (F, H, I)), 'down_qa': g(ks[10], (F, K, R, I)), 'down_qb': g(ks[11], (F, K, H, R)), 'down_scale': jnp.full((F, H), 0.1, jnp.float32), 'sh_gate_W': g(ks[12], (ISH, H)), 'sh_up_W': g(ks[13], (ISH, H)), 'sh_down_W': g(ks[14], (H, ISH))}
    _L0_ffn_all = _L0_ffn_setup()
    _L0_ffn_in = {k: v for k, v in _L0_ffn_all.items() if k in ('gate_weight', 'inv_mapping', 'mask_up_W', 'gate_W', 'gate_qa', 'gate_qb', 'gate_scale', 'up_W', 'up_qa', 'up_qb', 'up_scale', 'down_W', 'down_qa', 'down_qb', 'down_scale', 'sh_gate_W', 'sh_up_W', 'sh_down_W')}
    del _L0_ffn_all
    return {'x': x, 'ctx_1024': ctx_1024, 'g_xattn': g_xattn, 'g_ffn': g_ffn, 'L0_xattn_in_proj_w': _L0_xattn_in['in_proj_w'], 'L0_xattn_conv_w': _L0_xattn_in['conv_w'], 'L0_xattn_conv_b': _L0_xattn_in['conv_b'], 'L0_xattn_x_proj_w': _L0_xattn_in['x_proj_w'], 'L0_xattn_dt_proj_w': _L0_xattn_in['dt_proj_w'], 'L0_xattn_dt_proj_b': _L0_xattn_in['dt_proj_b'], 'L0_xattn_A_log': _L0_xattn_in['A_log'], 'L0_xattn_D': _L0_xattn_in['D'], 'L0_ffn_gate_weight': _L0_ffn_in['gate_weight'], 'L0_ffn_inv_mapping': _L0_ffn_in['inv_mapping'], 'L0_ffn_mask_up_W': _L0_ffn_in['mask_up_W'], 'L0_ffn_gate_W': _L0_ffn_in['gate_W'], 'L0_ffn_gate_qa': _L0_ffn_in['gate_qa'], 'L0_ffn_gate_qb': _L0_ffn_in['gate_qb'], 'L0_ffn_gate_scale': _L0_ffn_in['gate_scale'], 'L0_ffn_up_W': _L0_ffn_in['up_W'], 'L0_ffn_up_qa': _L0_ffn_in['up_qa'], 'L0_ffn_up_qb': _L0_ffn_in['up_qb'], 'L0_ffn_up_scale': _L0_ffn_in['up_scale'], 'L0_ffn_down_W': _L0_ffn_in['down_W'], 'L0_ffn_down_qa': _L0_ffn_in['down_qa'], 'L0_ffn_down_qb': _L0_ffn_in['down_qb'], 'L0_ffn_down_scale': _L0_ffn_in['down_scale'], 'L0_ffn_sh_gate_W': _L0_ffn_in['sh_gate_W'], 'L0_ffn_sh_up_W': _L0_ffn_in['sh_up_W'], 'L0_ffn_sh_down_W': _L0_ffn_in['sh_down_W']}

def reference(x, ctx_1024, g_xattn, g_ffn, L0_xattn_in_proj_w, L0_xattn_conv_w, L0_xattn_conv_b, L0_xattn_x_proj_w, L0_xattn_dt_proj_w, L0_xattn_dt_proj_b, L0_xattn_A_log, L0_xattn_D, L0_ffn_gate_weight, L0_ffn_inv_mapping, L0_ffn_mask_up_W, L0_ffn_gate_W, L0_ffn_gate_qa, L0_ffn_gate_qb, L0_ffn_gate_scale, L0_ffn_up_W, L0_ffn_up_qa, L0_ffn_up_qb, L0_ffn_up_scale, L0_ffn_down_W, L0_ffn_down_qa, L0_ffn_down_qb, L0_ffn_down_scale, L0_ffn_sh_gate_W, L0_ffn_sh_up_W, L0_ffn_sh_down_W):
    import jax
    import jax.numpy as jnp

    def _L0_xattn_ref(hidden_states, z, in_proj_w, conv_w, conv_b, x_proj_w, dt_proj_w, dt_proj_b, A_log, D):
        import jax, jax.numpy as jnp
        import numpy as np
        import math
        B, L, DM = (2, 512, 256)
        DS, DC, EXP = (16, 4, 2)
        DI = EXP * DM
        DR = math.ceil(DM / 16)
        DT_MIN, DT_MAX, DT_FLOOR = (0.001, 0.1, 0.0001)

        def _ssm_forward(hidden_states, z, in_proj_w, conv_w, conv_b, x_proj_w, dt_proj_w, dt_proj_b, A_log, D):
            b = hidden_states.shape[0]
            x = jnp.einsum('ed,bld->bel', in_proj_w, hidden_states)
            xp = jnp.pad(x, ((0, 0), (0, 0), (DC - 1, 0)))
            xc = jax.lax.conv_general_dilated(xp, conv_w[:, None, :], window_strides=(1,), padding='VALID', dimension_numbers=('NCH', 'OIH', 'NCH'), feature_group_count=DI)
            u = jax.nn.silu(xc + conv_b[None, :, None])
            x_dbl = jnp.einsum('ke,bel->bkl', x_proj_w, u)
            dt_lo = x_dbl[:, :DR]
            Bm = x_dbl[:, DR:DR + DS]
            Cm = x_dbl[:, DR + DS:]
            delta = jax.nn.softplus(jnp.einsum('er,brl->bel', dt_proj_w, dt_lo) + dt_proj_b[None, :, None])
            A = -jnp.exp(A_log)

            def step(state, xs):
                d_t, B_t, C_t, u_t = xs
                dA = jnp.exp(d_t[..., None] * A)
                state = state * dA + (d_t * u_t)[..., None] * B_t[:, None, :]
                y_t = jnp.einsum('ben,bn->be', state, C_t)
                return (state, y_t)
            xs = (jnp.moveaxis(delta, -1, 0), jnp.moveaxis(Bm, -1, 0), jnp.moveaxis(Cm, -1, 0), jnp.moveaxis(u, -1, 0))
            state0 = jnp.zeros((b, DI, DS), delta.dtype)
            _, ys = jax.lax.scan(step, state0, xs)
            y = jnp.moveaxis(ys, 0, -1)
            y = y + D[None, :, None] * u
            y = y * jax.nn.silu(z)
            return jnp.swapaxes(y, 1, 2)
        return _ssm_forward(hidden_states, z, in_proj_w, conv_w, conv_b, x_proj_w, dt_proj_w, dt_proj_b, A_log, D)

    def _L0_ffn_ref(hidden_states, gate_weight, inv_mapping, mask_up_W, gate_W, gate_qa, gate_qb, gate_scale, up_W, up_qa, up_qb, up_scale, down_W, down_qa, down_qb, down_scale, sh_gate_W, sh_up_W, sh_down_W):
        import jax, jax.numpy as jnp
        import numpy as np
        B, S, H, I, E, F, K, R, TOPK = (1, 256, 512, 352, 64, 8, 8, 8, 6)
        ISH = 2 * I

        def _fused_linear(x, W, qa, qb, scale, w):
            out = x @ W.T
            a = jnp.einsum('th,krh->tkr', x, qa)
            b = jnp.einsum('tkr,khr->tkh', a, qb)
            mix = jnp.einsum('tkh,tk->th', b, w)
            return out + scale[None, :] * mix

        def _moe_forward(hidden_states, gate_weight, inv_mapping, mask_up_W, gate_W, gate_qa, gate_qb, gate_scale, up_W, up_qa, up_qb, up_scale, down_W, down_qa, down_qb, down_scale, sh_gate_W, sh_up_W, sh_down_W):
            b, s, h = hidden_states.shape
            x = hidden_states.reshape(-1, h)
            T = x.shape[0]
            scores = jax.nn.softmax(x @ gate_weight.T, axis=-1)
            topk_w, topk_idx = jax.lax.top_k(scores, TOPK)
            w_dense = jnp.zeros((T, E), x.dtype).at[jnp.arange(T)[:, None], topk_idx].add(topk_w)
            flat = w_dense[:, inv_mapping]
            scalar = flat.sum(-1)
            soft = jax.nn.softmax(jnp.where(flat == 0, -1000000000.0, flat), axis=-1)

            def expert(muW, gW, gqa, gqb, gs, uW, uqa, uqb, us, dW, dqa, dqb, ds, w):
                xe = x + w @ muW.T
                gate = jax.nn.silu(_fused_linear(xe, gW, gqa, gqb, gs, w))
                up = _fused_linear(xe, uW, uqa, uqb, us, w)
                return _fused_linear(gate * up, dW, dqa, dqb, ds, w)
            outs = jax.vmap(expert, in_axes=(0,) * 13 + (1,))(mask_up_W, gate_W, gate_qa, gate_qb, gate_scale, up_W, up_qa, up_qb, up_scale, down_W, down_qa, down_qb, down_scale, soft)
            y = jnp.einsum('fth,tf->th', outs, scalar).reshape(b, s, h)
            sh = jax.nn.silu(hidden_states @ sh_gate_W.T) * (hidden_states @ sh_up_W.T) @ sh_down_W.T
            return y + sh
        return _moe_forward(hidden_states, gate_weight, inv_mapping, mask_up_W, gate_W, gate_qa, gate_qb, gate_scale, up_W, up_qa, up_qb, up_scale, down_W, down_qa, down_qb, down_scale, sh_gate_W, sh_up_W, sh_down_W)
    x = x + jnp.tanh(g_xattn[0]) * _L0_xattn_ref(ctx_1024, _layernorm(x, axis=-1), L0_xattn_in_proj_w, L0_xattn_conv_w, L0_xattn_conv_b, L0_xattn_x_proj_w, L0_xattn_dt_proj_w, L0_xattn_dt_proj_b, L0_xattn_A_log, L0_xattn_D)
    x = x + jnp.tanh(g_ffn[0]) * _L0_ffn_ref(_layernorm(x, axis=-1), L0_ffn_gate_weight, L0_ffn_inv_mapping, L0_ffn_mask_up_W, L0_ffn_gate_W, L0_ffn_gate_qa, L0_ffn_gate_qb, L0_ffn_gate_scale, L0_ffn_up_W, L0_ffn_up_qa, L0_ffn_up_qb, L0_ffn_up_scale, L0_ffn_down_W, L0_ffn_down_qa, L0_ffn_down_qb, L0_ffn_down_scale, L0_ffn_sh_gate_W, L0_ffn_sh_up_W, L0_ffn_sh_down_W)
    return x

_drawn_inputs = setup_inputs


def setup_inputs(seed=0):
    import zlib

    import numpy as np

    out = dict(_drawn_inputs(seed))
    spreads = {'L0_xattn_conv_b': (0.0, 0.281),
     'L0_xattn_D': (1.0, 0.2),
     'L0_ffn_gate_scale': (0.10000000149011612, 0.6),
     'L0_ffn_up_scale': (0.10000000149011612, 0.6),
     'L0_ffn_down_scale': (0.10000000149011612, 0.6)}
    factors = {'L0_xattn_dt_proj_w': 6.725,
     'L0_xattn_dt_proj_b': 2.942,
     'L0_ffn_gate_weight': 8.0,
     'L0_ffn_mask_up_W': 8.0,
     'L0_ffn_gate_W': 7.599,
     'L0_ffn_gate_qa': 8.0,
     'L0_ffn_gate_qb': 8.0,
     'L0_ffn_up_W': 7.536,
     'L0_ffn_up_qa': 8.0,
     'L0_ffn_up_qb': 8.0,
     'L0_ffn_down_W': 7.591,
     'L0_ffn_down_qa': 8.0,
     'L0_ffn_down_qb': 8.0}
    for name, (base, spread) in spreads.items():
        noise = np.random.default_rng([zlib.crc32(name.encode()), seed]).standard_normal(out[name].shape)
        drawn = base * np.exp(spread * noise) if base else spread * noise
        out[name] = jnp.asarray(drawn.astype(out[name].dtype))
    for name, factor in factors.items():
        out[name] = (out[name] * factor).astype(out[name].dtype)
    return out
```

```python
from contextlib import ExitStack

import concourse.bass as bass
from concourse import mybir

F32 = mybir.dt.float32
F32R = mybir.dt.float32r
I32 = mybir.dt.int32
ALU = mybir.AluOpType
ACT = mybir.ActivationFunctionType
AX_X = mybir.AxisListType.X

P = 128
B, L, H = 4, 512, 512
HC = H // P
LC = L // P
DM = 256
NS, DR, TAPS = 16, 16, 4
NF, NK, NR = 8, 8, 8
NE = NF * NK
KR = NK * NR
TOPK = 6
I = 352
IC = 3
IW = [min(P, I - P * m) for m in range(IC)]
NX = NF + 2
EPS = 1e-5
HALF = P // 2

GU = 2 * HC * I
D_W, D_QA, D_QB, D_S = 0, IC * H, IC * H + IC * P, IC * H + IC * P + H
D_SPLIT, D_ALL = D_S, D_S + H
PRE_IN, PRE_XP, PRE_DT = 0, 2 * H, D_QB
R_QA, R_QB, R_S = 0, HC * P, HC * P + I
R_MU, R_SEL = R_S + I, R_S + I + H
R_SPLIT, R_ALL = R_S, R_SEL + P
C_ID, C_MA, C_MB, C_E, C_AL, C_CW, C_CB, C_DB, C_D, C_GW, C_GX, C_GF, C_IO, C_ALL = (
    0, 128, 129, 130, 162, 226, 242, 246, 250, 254, 510, 511, 512, 513)


def gated_ssm_moe(nc, x, ctxT, gu, dd, pre, rr, cst, inv, out):
    with ExitStack() as ctx:
        def sb(name, shape, dt=F32):
            return ctx.enter_context(nc.sbuf_tensor(name, shape, dt))

        def sem(name):
            return ctx.enter_context(nc.semaphore(name))

        raw_gu = sb("raw_gu", [P, GU])
        raw_d = sb("raw_d", [P, D_ALL])
        raw_r = sb("raw_r", [P, R_ALL])
        gu_h, gu_l = sb("gu_h", [P, 2, HC, I], F32R), sb("gu_l", [P, 2, HC, I], F32R)
        d_h, d_l = sb("d_h", [P, D_SPLIT], F32R), sb("d_l", [P, D_SPLIT], F32R)
        r_h, r_l = sb("r_h", [P, R_SPLIT], F32R), sb("r_l", [P, R_SPLIT], F32R)
        mu = sb("mu", [P, H], F32R)
        r_sel = sb("r_sel", [P, P], F32R)
        cs = sb("cs", [P, C_ALL])
        inv_i, inv_f = sb("inv_i", [NE, NE], I32), sb("inv_f", [NE, NE])
        pm = sb("pm", [NE, NE])
        ones = sb("ones", [P, P])
        a_neg = sb("a_neg", [P, HC * NS])
        cwh, cbh = sb("cwh", [P, HC * TAPS]), sb("cbh", [P, HC])
        gw_h, gw_l = sb("gw_h", [P, HC, NE], F32R), sb("gw_l", [P, HC, NE], F32R)
        tgx, tgf = sb("tgx", [P, 1]), sb("tgf", [P, 1])
        x1 = sb("x1", [P, LC, H])
        xu = sb("xu", [P, LC, H])
        xnT = sb("xnT", [P, HC, L])
        xe_h, xe_l = sb("xe_h", [P, HC, L], F32R), sb("xe_l", [P, HC, L], F32R)
        xt = sb("xt", [P, 2, L])
        wr_n, wr_c = sb("wr_next", [P, L]), sb("wr_cur", [P, L])
        rnd = sb("rnd", [P, L], F32R)
        ws = sb("ws", [P, L], F32R)
        soft_s = sb("soft_s", [P, L], F32R)
        aw = sb("aw", [P, L])
        aw_h, aw_l = sb("aw_h", [P, L], F32R), sb("aw_l", [P, L], F32R)
        daw_s = sb("daw_s", [P, L], F32R)
        tt = sb("tt", [P, 2, L])
        hh, hl = sb("hh", [P, IC, L], F32R), sb("hl", [P, IC, L], F32R)
        delta, du = sb("delta", [P, HC, L]), sb("du", [P, HC, L])
        yx = sb("yx", [P, HC, L + TAPS - 1])
        y = yx[:, :, TAPS - 1:]
        s_st = sb("s_st", [P, L], F32R)
        b_rep, c_rep = sb("b_rep", [P, 2, L]), sb("c_rep", [P, L])
        sel = sb("sel", [P, 4, P], F32R)
        dA = sb("dA", [P, 2, L])
        wt = sb("wt", [P, 2, L])
        bst, mv = sb("bst", [P, LC, 6]), sb("mv", [P, LC, 2])
        st = sb("st", [P, 8, LC])
        mx = sb("mx", [P, LC])
        pad = sb("pad", [P, 16])
        sc = sb("sc", [P, LC, NE + 2])
        rep = xt[:, 0, 0:LC * (NE + 2)].rearrange("p (c n) -> p c n", c=LC)
        m8 = sb("m8", [P, LC, 8])
        wd = xt[:, 1, 0:LC * NE].rearrange("p (c n) -> p c n", c=LC)
        flat = tt[:, 0, 0:LC * NE].rearrange("p (g k) -> p g k", k=NK)
        fz = tt[:, 1, 0:LC * NE].rearrange("p (g k) -> p g k", k=NK)
        g1, g2 = sb("g1", [P, LC * NF]), sb("g2", [P, LC * NF])
        soft2 = wr_c[:].rearrange("p (c a n) -> p c a n", c=LC, a=2)
        wdT = aw[0:NE, :]
        scal = sb("scal", [P, LC, NF])

        def bank(name):
            return ctx.enter_context(nc.psum_tensor(name, [P, 512], F32))

        b_q, b_g0, b_u0, b_g1, b_u1, b_d0, b_d1, b_s = [bank("b_" + n) for n in
                                                         ("q", "g0", "u0", "g1", "u1", "d0", "d1", "s")]
        bg, bu, bd = [b_g0, b_g1, b_g0], [b_u0, b_u1, b_u0], [b_d0, b_d1]
        four = [b_g0, b_u0, b_g1, b_u1]

        ident = cs[:, C_ID:C_ID + P]

        dma_cst, dma_gu, dma_d, dma_r, dma_x, dma_ctx = (
            sem(n) for n in ("dma_cst", "dma_gu", "dma_d", "dma_r", "dma_x", "dma_ctx"))
        dma_out = sem("dma_out")
        set_dve, set_act = (
            sem(n) for n in ("set_dve", "set_act"))
        pool_scale_d, act_hi_d, pool_lo_d, pool_scale_r, act_hi_r, pool_lo_r = (
            sem(n) for n in ("pool_scale_d", "act_hi_d", "pool_lo_d", "pool_scale_r", "act_hi_r", "pool_lo_r"))
        act_hi_gu, pool_lo_g, pool_lo_u, act_mu, act_rsel, pool_mu = (
            sem(n) for n in ("act_hi_gu", "pool_lo_g", "pool_lo_u", "act_mu", "act_rsel", "pool_mu"))
        dve_mu = sem("dve_mu")
        pe_qa, pe_gu, pe_wr, pe_xe, pe_dqa, pe_dn = (
            sem(n) for n in ("pe_qa", "pe_gu", "pe_wr", "pe_xe", "pe_dqa", "pe_dn"))
        pe_rep, act_ws, dve_ws, act_wrc, dve_xt, act_xe = (
            sem(n) for n in ("pe_rep", "act_ws", "dve_ws", "act_wrc", "dve_xt", "act_xe"))
        dve_xe, dve_aw, act_aw, dve_awl, act_daw, dve_daw = (
            sem(n) for n in ("dve_xe", "dve_aw", "act_aw", "dve_awl", "act_daw", "dve_daw"))
        act_tanh, dve_g2, dve_h, act_hh, dve_hl, dve_dn = (
            sem(n) for n in ("act_tanh", "dve_g2", "dve_h", "act_hh", "dve_hl", "dve_dn"))
        dve_sel, act_rep, act_da, pool_dbu, dve_scan, dve_p = (
            sem(n) for n in ("dve_sel", "act_rep", "act_da", "pool_dbu", "dve_scan", "dve_p"))
        pool_y = sem("pool_y")
        act_ctx, dve_ctx, pe_in, act_xs, dve_cv, act_tc = (
            sem(n) for n in ("act_ctx", "dve_ctx", "pe_in", "act_xs", "dve_cv", "act_tc"))
        dve_u, act_u, dve_ul, pe_xd, act_rnd, act_s = (
            sem(n) for n in ("dve_u", "act_u", "dve_ul", "pe_xd", "act_rnd", "act_s"))
        dve_s, pe_dt, act_abs, act_relu, act_ev, dve_w = (
            sem(n) for n in ("dve_s", "pe_dt", "act_abs", "act_relu", "act_ev", "dve_w"))
        act_ln, dve_dl, dve_y = (
            sem(n) for n in ("act_ln", "dve_dl", "dve_y"))
        dve_stat, act_sqrt, dve_zh, act_tz, dve_z, dve_y3 = (
            sem(n) for n in ("dve_stat", "act_sqrt", "dve_zh", "act_tz", "dve_z", "dve_y3"))
        pe_yt, dve_x1 = (
            sem(n) for n in ("pe_yt", "dve_x1"))
        dve_xn, pe_xnT, act_xnT, act_xh, dve_xl, pe_lg = (
            sem(n) for n in ("dve_xn", "pe_xnT", "act_xnT", "act_xh", "dve_xl", "pe_lg"))
        dve_rt, act_ex, pe_wdT, act_wdT, pe_fl, dve_ft = (
            sem(n) for n in ("dve_rt", "act_ex", "pe_wdT", "act_wdT", "pe_fl", "dve_ft"))
        act_fe, pe_sT, act_sr, act_sT, dve_sT = (
            sem(n) for n in ("act_fe", "pe_sT", "act_sr", "act_sT", "dve_sT"))

        def a_(b, e):
            return NX * b + e

        def r_(b, e):
            return NF * b + e

        def x_(b, e):
            return (NF + 1) * b + e

        def d_loaded(b, e):
            return 11 * b + 2 + e + 1

        def d_split(b, e, last):
            return 11 * b + 2 + e + (0 if last else 1)

        def pre_split(nb):
            return 1 if isinstance(nb, int) and nb == 0 else 11 * (nb - 1) + 2

        PRIME = 2

        def ssm_tile(nb, e, j):
            return 64 * nb + 8 * e + j

        def ssm_rep(nb, e, k):
            return 32 * nb + 4 * e + k

        def col(t, i, n=1):
            return t[:, bass.ds(i, n)] if not isinstance(i, int) else t[:, i:i + n]

        ROUTE_STEPS, FLAT_STEPS, STAT_STEPS = 17, 11, 17
        SETUP_DVE, SETUP_ACT = 10, 4

        def three(w_h, w_l, v_h, v_l):
            return ((w_h, v_h), (w_h, v_l), (w_l, v_h))

        block = ctx.enter_context(nc.Block())

        @block.sync
        def _(sp):
            def load_gu(e):
                sp.dma_start(raw_gu[:], gu[e] if isinstance(e, int) else gu[bass.ds(e, 1)]
                             .rearrange("a p n -> (a p) n")).then_inc(dma_gu, 16)

            def load_d(e):
                sp.dma_start(raw_d[:], dd[e] if isinstance(e, int) else dd[bass.ds(e, 1)]
                             .rearrange("a p n -> (a p) n")).then_inc(dma_d, 16)

            def load_r(e):
                sp.dma_start(raw_r[:], rr[e] if isinstance(e, int) else rr[bass.ds(e, 1)]
                             .rearrange("a p n -> (a p) n")).then_inc(dma_r, 16)

            def load_pre():
                sp.dma_start(raw_d[:, 0:D_SPLIT], pre).then_inc(dma_d, 16)

            def of_batch(t, b):
                return t[b] if isinstance(b, int) else t[bass.ds(b, 1)].rearrange("a p n -> (a p) n")

            def load_x(b):
                src = x[b] if isinstance(b, int) else x[bass.ds(b, 1)].rearrange("a l h -> (a l) h")
                sp.dma_start(xu[:], src.rearrange("(c p) h -> p c h", p=P)).then_inc(dma_x, 16)

            def next_d(b, e, last):
                sp.wait_ge(pool_lo_d, d_split(b, e, last))
                if isinstance(e, int) and e == NX - 1:
                    if not last:
                        load_pre()
                else:
                    load_d(e + 1)

            def next_r(b, e, to):
                sp.wait_ge(pool_lo_r, r_(b, e) + 2)
                sp.wait_ge(dve_mu, r_(b, e) + 2)
                sp.wait_ge(act_rsel, r_(b, e) + 2)
                load_r(to)

            def next_gu(b, e, to):
                sp.wait_ge(pool_lo_u, a_(b, e) + 2)
                load_gu(to)

            sp.dma_start(cs[:], cst).then_inc(dma_cst, 16)
            sp.dma_start(inv_i[:], inv.partition_broadcast(NE)).then_inc(dma_cst, 16)
            sp.dma_start(dA[:], ctxT[0]).then_inc(dma_ctx, 16)
            load_pre()
            load_r(0)
            load_gu(0)
            sp.wait_ge(pool_lo_d, 1)
            load_pre()
            sp.wait_ge(dve_y, 1)
            load_x(0)
            sp.wait_ge(pool_lo_r, 1)
            sp.wait_ge(dve_mu, 1)
            sp.wait_ge(act_rsel, 1)
            load_r(1)
            sp.wait_ge(pool_lo_u, 1)
            load_gu(1)

            def batch(b, last):
                if not last:
                    sp.wait_ge(dve_scan, PRIME + 64 * (b + 1))
                    sp.dma_start(dA[:], of_batch(ctxT, b + 1)).then_inc(dma_ctx, 16)
                    sp.wait_ge(pool_lo_d, pre_split(b + 1))
                else:
                    sp.wait_ge(dma_d, 16 * (11 * b + 2))
                load_d(0)
                if not last:
                    sp.wait_ge(pe_xnT, HC * (b + 1))
                    load_x(b + 1)
                with sp.Fori(0, NF - 2) as e:
                    next_d(b, e, last)
                    next_r(b, e, e + 2)
                    next_gu(b, e, e + 2)
                for e in range(NF - 2, NX):
                    next_d(b, e, last)
                    if e < NF and not last:
                        next_r(b, e, e + 2 - NF)
                    if e + 2 < NX:
                        next_gu(b, e, e + 2)
                    elif not last:
                        next_gu(b, e, e + 2 - NX)
                sp.wait_ge(dve_dn, LC * NX * (b + 1) + 1)
                dst = out[b] if isinstance(b, int) else out[bass.ds(b, 1)].rearrange("a l h -> (a l) h")
                sp.dma_start(dst.rearrange("(c p) h -> p c h", p=P), x1[:]).then_inc(dma_out, 16)

            with sp.Fori(0, B - 1) as b:
                batch(b, False)
            batch(B - 1, True)
            sp.wait_ge(dma_out, 16 * (B + 1))

        @block.tensor
        def _(pe):
            mm = nc.tensor.matmul

            def replicate(nb, e, k):
                pe.wait_ge(dve_sel, ssm_rep(nb, e, k) + 1)
                pe.wait_ge(act_rep, ssm_rep(nb, e, k) + 1)
                mm(b_s[:], sel[:, k, :], s_st[:], start=True, stop=True).then_inc(pe_rep, 1)

            def ssm_pre(nb, first):
                pe.wait_ge(dve_ctx, nb + 1)
                pe.wait_ge(pool_lo_d, pre_split(nb))
                if not first:
                    pe.wait_ge(dve_x1, LC * nb)
                for m in range(HC):
                    n = 0
                    for c in range(DM // P):
                        o = PRE_IN + c * H + m * P
                        for w, v in three(d_h[:, o:o + P], d_l[:, o:o + P], hh[:, c, :], hl[:, c, :]):
                            i = mm(four[m][:], w, v, start=(n == 0), stop=(n == 5))
                            n += 1
                    i.then_inc(pe_in, 1)
                n = 0
                for c in range(HC):
                    pe.wait_ge(dve_ul, HC * nb + c + 1)
                    o = PRE_XP + c * P
                    for w, v in three(d_h[:, o:o + P], d_l[:, o:o + P], xe_h[:, c, :], xe_l[:, c, :]):
                        i = mm(b_q[:], w, v, start=(n == 0), stop=(n == 11))
                        n += 1
                i.then_inc(pe_xd, 1)
                pe.wait_ge(dve_s, nb + 1)
                for m in range(HC):
                    o = PRE_DT + m * P
                    mm(four[m][:], d_h[:, o:o + P], s_st[:], start=True, stop=False)
                    mm(four[m][:], d_l[0:DR, o:o + P], s_st[0:DR, :], start=False, stop=True).then_inc(pe_dt, 1)

            def ssm_post(b):
                pe.wait_ge(dve_y3, b + 1)
                for lc in range(LC):
                    for dc in range(HC):
                        i = nc.tensor.transpose(four[lc][:, dc * P:(dc + 1) * P], du[:, dc, lc * P:(lc + 1) * P], ident)
                    i.then_inc(pe_yt, 1)

            def router(b, last):
                pe.wait_ge(dve_xn, LC * (b + 1))
                if not last:
                    pe.wait_ge(act_relu, HC * (b + 2))
                for hc in range(HC):
                    for tc in range(LC):
                        i = nc.tensor.transpose(four[hc][:, tc * P:(tc + 1) * P], xu[:, tc, hc * P:(hc + 1) * P], ident)
                    i.then_inc(pe_xnT, 1)
                pe.wait_ge(dve_xl, HC * (b + 1))
                pe.wait_ge(act_xnT, HC * (b + 1))
                for tc in range(LC):
                    n = 0
                    for c in range(HC):
                        t = slice(tc * P, (tc + 1) * P)
                        for v, w in ((xe_h, gw_h), (xe_l, gw_h), (xe_h, gw_l)):
                            i = mm(b_q[:, tc * NE:(tc + 1) * NE], v[:, c, t], w[:, c, :], start=(n == 0), stop=(n == 11))
                            n += 1
                i.then_inc(pe_lg, 1)
                pe.wait_ge(dve_rt, ROUTE_STEPS * (b + 1))
                for tc in range(LC):
                    i = mm(b_g0[0:NE, tc * P:(tc + 1) * P], wd[:, tc, :], ident, start=True, stop=True)
                i.then_inc(pe_wdT, 1)
                pe.wait_ge(act_wdT, b + 1)
                for tc in range(LC):
                    i = mm(b_u0[:, tc * NE:(tc + 1) * NE], wdT[:, tc * P:(tc + 1) * P], pm[:], start=True, stop=True)
                i.then_inc(pe_fl, 1)
                pe.wait_ge(dve_ft, FLAT_STEPS * (b + 1))
                for tc in range(LC):
                    i = nc.tensor.transpose(b_g1[:, tc * P:(tc + 1) * P],
                                            soft2[:, tc, :, :].rearrange("p a k -> p (a k)"), ident)
                i.then_inc(pe_sT, 1)
                pe.wait_ge(dve_sT, b + 1)
                pe.wait_ge(act_sT, b + 1)

            def wrep(r):
                pe.wait_ge(act_rsel, r + 1)
                mm(b_q[:], r_sel[:], soft_s[:], start=True, stop=True).then_inc(pe_wr, 1)

            def delta_xe(r, dn_before):
                pe.wait_ge(dve_mu, r + 1)
                pe.wait_ge(dve_ws, r + 1)
                pe.wait_ge(act_ws, r + 1)
                for c in range(HC):
                    if c < 2:
                        pe.wait_ge(dve_dn, dn_before)
                    else:
                        pe.wait_ge(dve_xt, HC * r + c - 1)
                    mm(bd[c % 2][:], mu[:, c * P:(c + 1) * P], ws[:], start=True, stop=True).then_inc(pe_xe, 1)

            def body(b, e, last, routed, nxt, ssm):
                a, r = a_(b, e), (r_(b, e) if routed else None)
                xi = x_(b, e if routed else NF)
                if routed:
                    pe.wait_ge(pool_lo_r, r + 1)
                    n = 0
                    for c in range(HC):
                        pe.wait_ge(dve_xe, HC * xi + c + 1)
                        o = R_QA + c * P
                        for w, v in three(r_h[:, o:o + P], r_l[:, o:o + P], xe_h[:, c, :], xe_l[:, c, :]):
                            i = mm(b_q[:], w, v, start=(n == 0), stop=(n == 11))
                            n += 1
                    i.then_inc(pe_qa, 1)
                else:
                    pe.wait_ge(dve_xe, HC * xi + HC)
                if ssm:
                    replicate(b + 1, e, 0)
                for m in range(IC):
                    if m == 2:
                        pe.wait_ge(dve_h, IC * a + 1)
                    for j, out_b in ((0, bg[m]), (1, bu[m])):
                        if m == 0:
                            pe.wait_ge((pool_lo_g, pool_lo_u)[j], a + 1)
                        n = 0
                        for c in range(HC):
                            cols = slice(m * P, m * P + IW[m])
                            for w, v in three(gu_h[:, j, c, cols], gu_l[:, j, c, cols], xe_h[:, c, :], xe_l[:, c, :]):
                                i = mm(out_b[0:IW[m], :], w, v, start=(n == 0), stop=(n == 11 and not routed))
                                n += 1
                    if m < 2 and ssm:
                        replicate(b + 1, e, 1 + m)
                    if routed:
                        if m == 0:
                            pe.wait_ge(dve_awl, r + 1)
                        cols = slice(R_QB + m * P, R_QB + m * P + IW[m])
                        for k, (w, v) in enumerate(((r_h, aw_h), (r_h, aw_l), (r_l, aw_h))):
                            for j, out_b in ((0, bg[m]), (1, bu[m])):
                                rows = slice(j * HALF, (j + 1) * HALF)
                                i = mm(out_b[0:IW[m], :], w[rows, cols], v[rows, :], start=False, stop=(k == 2))
                    i.then_inc(pe_gu, 1)
                    if m == 1:
                        if ssm:
                            replicate(b + 1, e, 3)
                        if nxt:
                            wrep(r + 1)
                if nxt:
                    delta_xe(r + 1, LC * a + 1)
                if routed:
                    n = 0
                    for m in range(IC):
                        pe.wait_ge(dve_hl, IC * a + m + 1)
                        pe.wait_ge(pool_lo_d, d_split(b, e, last))
                        k = slice(0, IW[m])
                        o = D_QA + m * P
                        for w, v in three(d_h[k, o:o + P], d_l[k, o:o + P], hh[k, m, :], hl[k, m, :]):
                            i = mm(b_q[:], w, v, start=(n == 0), stop=(n == 8))
                            n += 1
                    i.then_inc(pe_dqa, 1)
                else:
                    pe.wait_ge(dve_hl, IC * a + IC)
                    pe.wait_ge(pool_lo_d, d_split(b, e, last))

                def down(tc):
                    t = slice(tc * P, (tc + 1) * P)
                    if tc >= 2:
                        pe.wait_ge(dve_dn, LC * a + tc)
                    elif nxt:
                        pe.wait_ge(dve_xt, HC * (r + 1) + HC - 1 + tc)
                    else:
                        pe.wait_ge(dve_dn, LC * a + 1)
                    n = 0
                    for m in range(IC):
                        k = slice(0, IW[m])
                        o = D_W + m * H
                        for v, w in ((hh, d_h), (hl, d_h), (hh, d_l)):
                            i = mm(bd[tc % 2][:], v[k, m, t], w[k, o:o + H], start=(n == 0),
                                   stop=(n == 8 and not routed))
                            n += 1
                    if not routed:
                        i.then_inc(pe_dn, 1)

                def adapter(tc):
                    t = slice(tc * P, (tc + 1) * P)
                    mm(bd[tc % 2][:], daw_s[:, t], d_h[:, D_QB:D_QB + H], start=False, stop=False)
                    mm(bd[tc % 2][:], daw_s[0:HALF, t], d_l[0:HALF, D_QB:D_QB + H],
                       start=False, stop=True).then_inc(pe_dn, 1)

                if routed:
                    down(0)
                    down(1)
                    pe.wait_ge(dve_daw, r + 2)
                    pe.wait_ge(act_daw, r + 1)
                    adapter(0)
                    adapter(1)
                    for tc in (2, 3):
                        down(tc)
                        adapter(tc)
                else:
                    for tc in range(LC):
                        down(tc)

            pe.wait_ge(set_dve, SETUP_DVE)
            ssm_pre(0, True)
            with pe.Fori(0, NF) as e:
                for k in range(4):
                    replicate(0, e, k)

            def batch(b, last):
                ssm_post(b)
                if not last:
                    ssm_pre(b + 1, False)
                router(b, last)
                wrep(r_(b, 0))
                delta_xe(r_(b, 0), LC * a_(b, 0) + 1)
                with pe.Fori(0, NF - 1) as e:
                    body(b, e, last, True, True, not last)
                body(b, NF - 1, last, True, False, not last)
                body(b, NF, last, False, False, False)
                body(b, NF + 1, last, False, False, False)

            with pe.Fori(0, B - 1) as b:
                batch(b, False)
            batch(B - 1, True)

        @block.scalar
        def _(act):
            def f(out_, in_, func, **k):
                return nc.scalar.activation(out_, in_, func, **k)

            def rounded(out_, in_):
                return f(out_, in_, ACT.Copy)

            def split_d(loaded, routed, pe_ready, r=None):
                act.wait_ge(dma_d, 16 * loaded)
                if r is not None:
                    act.wait_ge(pool_scale_d, r + 1)
                for s_, v in pe_ready:
                    act.wait_ge(s_, v)
                n = D_SPLIT if routed else IC * H
                rounded(d_h[:, 0:n], raw_d[:, 0:n]).then_inc(act_hi_d, 1)

            def mu_conv(k, first):
                act.wait_ge(dma_r, 16 * (k + 1))
                if not first:
                    act.wait_ge(dve_daw, k)
                rounded(rnd[:], raw_r[:, R_MU:R_MU + H]).then_inc(act_mu, 1)
                if not first:
                    act.wait_ge(pe_wr, k)
                rounded(r_sel[:], raw_r[:, R_SEL:R_SEL + P]).then_inc(act_rsel, 1)

            def split_r(k, a_done):
                act.wait_ge(pool_scale_r, k + 1)
                if a_done is not None:
                    act.wait_ge(pe_gu, a_done)
                rounded(r_h[:], raw_r[:, 0:R_SPLIT]).then_inc(act_hi_r, 1)

            def split_gu(k, a_done):
                act.wait_ge(dma_gu, 16 * (k + 1))
                if a_done is not None:
                    act.wait_ge(pe_gu, a_done)
                for j in range(2):
                    rounded(gu_h[:, j], raw_gu[:, j * HC * I:(j + 1) * HC * I].rearrange("p (c i) -> p c i", c=HC)
                            ).then_inc(act_hi_gu, 1)

            def rep_copy(nb, e, k):
                act.wait_ge(pe_rep, ssm_rep(nb, e, k) + 1)
                n = 16 * nb + 2 * e + k // 2
                if k % 2 == 0:
                    act.wait_ge(pool_dbu, 4 * n + 4)
                    dst = b_rep[:, k // 2, :]
                else:
                    act.wait_ge(dve_p, 4 * n + 1)
                    dst = c_rep[:]
                f(dst, b_s[:], ACT.Copy).then_inc(act_rep, 1)

            def exp_tile(nb, e, j):
                t = ssm_tile(nb, e, j)
                if j == 0:
                    act.wait_ge(dve_y, nb + 1)
                act.wait_ge(dve_scan, t + 1)
                dc, k = j % 4, j // 4
                f(dA[:, j % 2, :], delta[:, dc, :], ACT.Exp,
                  scale=col(a_neg, 2 * e + (dc * NS + k))).then_inc(act_da, 1)

            def wr_copy(r):
                act.wait_ge(pe_wr, r + 1)
                act.wait_ge(dve_mu, r + 1)
                f(wr_n[:], b_q[:], ACT.Copy).then_inc(act_ws, 1)
                rounded(rnd[HALF:P, :], b_q[HALF:P, :]).then_inc(act_ws, 1)
                rounded(ws[0:HALF, :], b_q[0:HALF, :]).then_inc(act_ws, 1)

            def xe_hi(b, e, r):
                xi = x_(b, e)
                for c in range(HC):
                    act.wait_ge(dve_xt, HC * r + c + 1)
                    rounded(xe_h[:, c, :], xt[:, c % 2, :]).then_inc(act_xe, 1)

            def ssm_pre(nb, first):
                split_d(pre_split(nb), True, [] if first else [(pe_yt, LC * nb)])
                act.wait_ge(dma_ctx, 16 * (nb + 1))
                if not first:
                    act.wait_ge(pe_yt, LC * nb)
                rounded(hh[:, 0:2, :], dA[:]).then_inc(act_ctx, 1)
                if not first:
                    act.wait_ge(dve_y3, nb)
                for m in range(HC):
                    act.wait_ge(pe_in, HC * nb + m + 1)
                    f(y[:, m, :], four[m][:], ACT.Copy).then_inc(act_xs, 1)
                for m in range(HC):
                    act.wait_ge(dve_cv, 16 * nb + 12 + m + 1)
                    f(du[:, m, :], delta[:, m, :], ACT.Tanh).then_inc(act_tc, 1)
                for m in range(HC):
                    act.wait_ge(dve_u, HC * nb + m + 1)
                    rounded(xe_h[:, m, :], xu[:, m, :]).then_inc(act_u, 1)
                act.wait_ge(pe_xd, nb + 1)
                rounded(rnd[HALF:P, :], b_q[HALF:P, :]).then_inc(act_rnd, 1)
                rounded(s_st[0:HALF, :], b_q[0:HALF, :]).then_inc(act_s, 1)
                for m in range(HC):
                    act.wait_ge(pe_dt, HC * nb + m + 1)
                    bias = cs[:, C_DB + m:C_DB + m + 1]
                    f(delta[:, m, :], four[m][:], ACT.Abs, bias=bias).then_inc(act_abs, 1)
                    f(xnT[:, m, :], four[m][:], ACT.Relu, bias=bias).then_inc(act_relu, 1)
                act.wait_ge(act_abs, HC * (nb + 1))
                f(delta[:], delta[:], ACT.Exp, scale=-1.0).then_inc(act_ev, 1)
                act.wait_ge(dve_w, 4 * nb + 1)
                f(y, du[:], ACT.Ln).then_inc(act_ln, 1)

            def root(u):
                act.wait_ge(dve_stat, STAT_STEPS * u + 11)
                f(st[:, 1, :], st[:, 0, :], ACT.Sqrt).then_inc(act_sqrt, 1)

            def ssm_post(b):
                root(2 * b)
                act.wait_ge(dve_zh, LC * (b + 1))
                f(delta[:], xnT[:], ACT.Tanh).then_inc(act_tz, 1)

            def router(b):
                root(2 * b + 1)
                for hc in range(HC):
                    act.wait_ge(pe_xnT, HC * b + hc + 1)
                    rounded(xe_h[:, hc, :], four[hc][:]).then_inc(act_xh, 1)
                    f(xnT[:, hc, :], four[hc][:], ACT.Copy).then_inc(act_xnT, 1)
                act.wait_ge(dve_rt, ROUTE_STEPS * b + 2)
                f(sc[:, :, 0:NE], sc[:, :, 0:NE], ACT.Exp).then_inc(act_ex, 1)
                act.wait_ge(pe_wdT, b + 1)
                f(wdT, b_g0[0:NE, :], ACT.Copy).then_inc(act_wdT, 1)
                act.wait_ge(dve_ft, FLAT_STEPS * b + 5)
                f(fz, fz, ACT.Exp).then_inc(act_fe, 1)
                act.wait_ge(pe_sT, b + 1)
                rounded(rnd[HALF:P, :], b_g1[HALF:P, :]).then_inc(act_sr, 1)
                rounded(soft_s[0:HALF, :], b_g1[0:HALF, :]).then_inc(act_sT, 1)

            def body(b, e, last, routed, nxt, ssm):
                a, r = a_(b, e), (r_(b, e) if routed else None)
                split_d(d_loaded(b, e), routed,
                        [(pe_dn, LC * a + 1)], r)
                more_r = routed and not (last and not nxt)
                if more_r:
                    mu_conv(r + 1, False)
                if routed:
                    act.wait_ge(act_ws, 3 * (r + 1))
                    f(wr_c[:], wr_n[:], ACT.Copy).then_inc(act_wrc, 1)
                if ssm:
                    rep_copy(b + 1, e, 0)
                if routed:
                    act.wait_ge(dve_aw, 2 * r + 1)
                    rounded(aw_h[:], aw[:]).then_inc(act_aw, 1)
                if ssm:
                    rep_copy(b + 1, e, 1)
                    exp_tile(b + 1, e, 0)
                    exp_tile(b + 1, e, 1)

                def tanh(m):
                    w = IW[m]
                    act.wait_ge(pe_gu, IC * a + m + 1)
                    if m == 2:
                        act.wait_ge(dve_hl, IC * a + 1)
                    f(tt[0:w, m % 2, :], bg[m][0:w, :], ACT.Tanh, scale=0.5).then_inc(act_tanh, 1)

                def h_hi(m):
                    w = IW[m]
                    act.wait_ge(dve_h, IC * a + m + 1)
                    rounded(hh[0:w, m, :], tt[0:w, m % 2, :]).then_inc(act_hh, 1)

                tanh(0)
                if ssm:
                    exp_tile(b + 1, e, 2)
                h_hi(0)
                if ssm:
                    exp_tile(b + 1, e, 3)
                    rep_copy(b + 1, e, 2)
                tanh(1)
                if ssm:
                    exp_tile(b + 1, e, 4)
                h_hi(1)
                if ssm:
                    rep_copy(b + 1, e, 3)
                    exp_tile(b + 1, e, 5)
                if nxt:
                    wr_copy(r + 1)
                tanh(2)
                h_hi(2)
                if nxt:
                    xe_hi(b, e + 1, r + 1)
                elif routed:
                    for c in range(HC):
                        rounded(xe_h[:, c, :], xnT[:, c, :]).then_inc(act_xe, 1)
                if more_r:
                    split_r(r + 1, IC * (a + 1))
                if routed:
                    act.wait_ge(dve_aw, 2 * r + 2)
                    rounded(daw_s[0:HALF, :], aw[0:HALF, :]).then_inc(act_daw, 1)
                    rounded(rnd[HALF:P, :], aw[HALF:P, :]).then_inc(act_daw, 1)
                if not (last and isinstance(e, int) and e == NX - 1):
                    split_gu(a + 1, IC * (a + 1))
                if ssm:
                    exp_tile(b + 1, e, 6)
                    exp_tile(b + 1, e, 7)

            act.wait_ge(dma_cst, 32)
            f(a_neg[:], cs[:, C_AL:C_AL + HC * NS], ACT.Exp).then_inc(set_act, 1)
            f(tgx[:], cs[:, C_GX:C_GX + 1], ACT.Tanh).then_inc(set_act, 1)
            f(tgf[:], cs[:, C_GF:C_GF + 1], ACT.Tanh).then_inc(set_act, 1)
            rounded(gw_h[:], cs[:, C_GW:C_GW + HC * NE].rearrange("p (c n) -> p c n", c=HC)).then_inc(set_act, 1)
            f(pad[:, 4:5], cs[:, 0:1], ACT.Copy).then_inc(act_rep, 1)
            act.wait_ge(set_dve, SETUP_DVE)
            ssm_pre(0, True)
            mu_conv(0, True)
            split_r(0, None)
            split_gu(0, None)
            with act.Fori(0, NF) as e:
                rep_copy(0, e, 0)
                rep_copy(0, e, 1)
                for j in range(3):
                    exp_tile(0, e, j)
                rep_copy(0, e, 2)
                exp_tile(0, e, 3)
                exp_tile(0, e, 4)
                rep_copy(0, e, 3)
                for j in range(5, 8):
                    exp_tile(0, e, j)

            def batch(b, last):
                ssm_post(b)
                if not last:
                    ssm_pre(b + 1, False)
                router(b)
                wr_copy(r_(b, 0))
                xe_hi(b, 0, r_(b, 0))
                with act.Fori(0, NF - 1) as e:
                    body(b, e, last, True, True, not last)
                body(b, NF - 1, last, True, False, not last)
                body(b, NF, last, False, False, False)
                body(b, NF + 1, last, False, False, False)

            with act.Fori(0, B - 1) as b:
                batch(b, False)
            batch(B - 1, True)

        @block.gpsimd
        def _(pool):
            v = nc.gpsimd

            def lo(out_, raw, hi):
                return v.tensor_tensor(out_, raw, hi.bitcast(F32), ALU.subtract)

            def split_d(split_count, routed):
                pool.wait_ge(act_hi_d, split_count)
                n = D_SPLIT if routed else IC * H
                lo(d_l[:, 0:n], raw_d[:, 0:n], d_h[:, 0:n]).then_inc(pool_lo_d, 1)

            def scale_d(b, e):
                pool.wait_ge(dma_d, 16 * d_loaded(b, e))
                v.tensor_tensor(raw_d[:, D_QB:D_QB + H], raw_d[:, D_QB:D_QB + H], raw_d[:, D_S:D_S + H],
                                ALU.mult).then_inc(pool_scale_d, 1)

            def prepare_r(k, first):
                raw = raw_r[:, R_MU:R_MU + H]
                pool.wait_ge(act_mu, k + 1)
                lo(raw, raw, rnd[:]).then_inc(pool_mu, 1)
                v.tensor_tensor(raw_r[:, R_QB:R_QB + I], raw_r[:, R_QB:R_QB + I], raw_r[:, R_S:R_S + I],
                                ALU.mult).then_inc(pool_scale_r, 1)
                pool.wait_ge(pool_mu, 2 * k + 1)
                v.tensor_tensor(raw, raw, cs[:, C_MB:C_MB + 1].broadcast_to([P, H]), ALU.mult).then_inc(pool_mu, 1)

            def split_r(k):
                pool.wait_ge(act_hi_r, k + 1)
                lo(r_l[:], raw_r[:, 0:R_SPLIT], r_h[:]).then_inc(pool_lo_r, 1)

            def split_gu(k):
                for j, s_ in enumerate((pool_lo_g, pool_lo_u)):
                    pool.wait_ge(act_hi_gu, 2 * k + j + 1)
                    lo(gu_l[:, j], raw_gu[:, j * HC * I:(j + 1) * HC * I].rearrange("p (c i) -> p c i", c=HC),
                       gu_h[:, j]).then_inc(s_, 1)

            def dbu(nb, e, j):
                t = ssm_tile(nb, e, j)
                if j == 0:
                    pool.wait_ge(dve_y, nb + 1)
                if j % 4 == 0:
                    pool.wait_ge(act_rep, ssm_rep(nb, e, j // 2) + 2)
                pool.wait_ge(pool_y, t + 1)
                v.tensor_tensor(wt[:, j % 2, :], du[:, j % 4, :], b_rep[:, j // 4, :], ALU.mult).then_inc(pool_dbu, 1)

            def add_y(nb, e, j):
                pool.wait_ge(dve_p, ssm_tile(nb, e, j) + 2)
                yd = y[:, j % 4, :]
                v.tensor_tensor(yd, yd, wt[:, j % 2, :], ALU.add).then_inc(pool_y, 1)

            def body(b, e, last, routed, nxt, ssm):
                a, r = a_(b, e), (r_(b, e) if routed else None)
                if routed:
                    scale_d(b, e)
                split_d(d_split(b, e, last), routed)
                more_r = routed and not (last and not nxt)
                if more_r:
                    prepare_r(r + 1, False)
                if ssm:
                    dbu(b + 1, e, 0)
                    dbu(b + 1, e, 1)
                    for j in range(6):
                        add_y(b + 1, e, j)
                        dbu(b + 1, e, j + 2)
                if more_r:
                    split_r(r + 1)
                if not (last and isinstance(e, int) and e == NX - 1):
                    split_gu(a + 1)
                if ssm:
                    add_y(b + 1, e, 6)
                    add_y(b + 1, e, 7)

            v.memset(pad[:, 5:6], 0.0).then_inc(pool_dbu, 8)
            v.memset(pad[:, 6:7], 0.0).then_inc(pool_y, 2)
            pool.wait_ge(dma_cst, 32)
            split_d(1, True)
            prepare_r(0, True)
            split_r(0)
            split_gu(0)
            with pool.Fori(0, NF) as e:
                dbu(0, e, 0)
                dbu(0, e, 1)
                for j in range(6):
                    add_y(0, e, j)
                    dbu(0, e, j + 2)
                add_y(0, e, 6)
                add_y(0, e, 7)

            def batch(b, last):
                if not last:
                    split_d(pre_split(b + 1), True)
                with pool.Fori(0, NF - 1) as e:
                    body(b, e, last, True, True, not last)
                body(b, NF - 1, last, True, False, not last)
                body(b, NF, last, False, False, False)
                body(b, NF + 1, last, False, False, False)

            with pool.Fori(0, B - 1) as b:
                batch(b, False)
            batch(B - 1, True)

        @block.vector
        def _(dve):
            v = nc.vector
            tt_ = v.tensor_tensor

            def stt(out_, a, s_, b_, op0, op1):
                return v.scalar_tensor_tensor(out=out_, in0=a, scalar=s_, in1=b_, op0=op0, op1=op1)

            def lo(out_, whole, hi):
                return tt_(out_, whole, hi.bitcast(F32), ALU.subtract)

            def chain(s_, base):
                done = [0]

                def step(ins, wait=True):
                    done[0] += 1
                    ins.then_inc(s_, 1)
                    if wait:
                        dve.wait_ge(s_, base + done[0])
                return step

            def carrier(k):
                return v.memset(pad[:, 12 + k:13 + k], 0.0)

            def selectors(nb, e):
                for k in range(4):
                    v.tensor_scalar(sel[:, k, :], ones[:], col(cs, 2 * e + (C_E + (k % 2) * NS + k // 2)), None,
                                    ALU.mult).then_inc(dve_sel, 1)

            def tile(nb, e, j):
                t = ssm_tile(nb, e, j)
                w = wt[:, j % 2, :]
                dve.wait_ge(act_da, t + 1)
                dve.wait_ge(pool_dbu, t + 9)
                v.tensor_tensor_scan(w, dA[:, j % 2, :], w, 0.0, ALU.mult, ALU.add).then_inc(dve_scan, 1)
                if j % 4 == 0:
                    dve.wait_ge(act_rep, ssm_rep(nb, e, j // 2 + 1) + 2)
                dve.wait_ge(dve_scan, t + 3)
                tt_(w, w, c_rep[:], ALU.mult).then_inc(dve_p, 1)

            def stats(u, src, half):
                step = chain(dve_stat, STAT_STEPS * u)
                step(carrier(0), False)
                for c in range(LC):
                    step(v.bn_stats(bst[:, c, :], src[:, c, :]), c == LC - 1)
                step(carrier(1), False)
                for c in range(LC):
                    step(v.bn_aggr(mv[:, c, :], bst[:, c, :]), c == LC - 1)
                step(v.tensor_scalar(st[:, 0, :], mv[:, :, 1], EPS, None, ALU.add))
                dve.wait_ge(act_sqrt, u + 1)
                step(v.reciprocal(st[:, 2, :], st[:, 1, :]))
                step(tt_(st[:, 3, :], st[:, 0, :], st[:, 2, :], ALU.mult))
                step(tt_(st[:, 4, :], st[:, 1, :], st[:, 3, :], ALU.add))
                step(v.reciprocal(st[:, 5, :], st[:, 4, :]))
                step(v.tensor_scalar(st[:, 6, :], st[:, 5, :], 1.0 if half else 2.0, None, ALU.mult))
                step(stt(st[:, 7, :], mv[:, :, 0], -1.0, st[:, 6, :], ALU.mult, ALU.mult))

            def normed(dst, src, c):
                return v.tensor_scalar(dst[:, c, :], src[:, c, :], st[:, 6, c:c + 1], st[:, 7, c:c + 1],
                                       ALU.mult, ALU.add)

            def ssm_pre(nb, first):
                dve.wait_ge(act_ctx, nb + 1)
                lo(hl[:, 0:2, :], dA[:], hh[:, 0:2, :]).then_inc(dve_ctx, 1)
                for j in range(TAPS):
                    k = TAPS - 1 - j
                    for m in range(HC):
                        w = cwh[:, m * TAPS + k:m * TAPS + k + 1]
                        src = yx[:, m, k:k + L]
                        if j == 0:
                            dve.wait_ge(act_xs, HC * nb + m + 1)
                            v.tensor_scalar(delta[:, m, :], src, w, cbh[:, m:m + 1], ALU.mult, ALU.add
                                            ).then_inc(dve_cv, 1)
                        else:
                            dve.wait_ge(dve_cv, 16 * nb + 4 * (j - 1) + m + 1)
                            stt(delta[:, m, :], src, w, delta[:, m, :], ALU.mult, ALU.add).then_inc(dve_cv, 1)
                for m in range(HC):
                    dve.wait_ge(act_tc, HC * nb + m + 1)
                    stt(xu[:, m, :], du[:, m, :], 1.0, delta[:, m, :], ALU.add, ALU.mult).then_inc(dve_u, 1)
                for m in range(HC):
                    dve.wait_ge(act_u, HC * nb + m + 1)
                    lo(xe_l[:, m, :], xu[:, m, :], xe_h[:, m, :]).then_inc(dve_ul, 1)
                dve.wait_ge(act_rnd, nb + 1)
                dve.wait_ge(act_s, nb + 1)
                lo(s_st[HALF:P, :], b_q[HALF:P, :], rnd[HALF:P, :]).then_inc(dve_s, 1)
                dve.wait_ge(act_ev, nb + 1)
                v.tensor_scalar(du[:], delta[:], 1.0, None, ALU.add).then_inc(dve_w, 1)
                dve.wait_ge(act_ln, nb + 1)
                stt(du[:], du[:], 1.0, delta[:], ALU.subtract, ALU.subtract).then_inc(dve_w, 1)
                dve.wait_ge(dve_w, 4 * nb + 2)
                tt_(delta[:], y, du[:], ALU.subtract).then_inc(dve_w, 1)
                dve.wait_ge(dve_w, 4 * nb + 3)
                dve.wait_ge(act_relu, HC * (nb + 1))
                tt_(delta[:], delta[:], xnT[:], ALU.add).then_inc(dve_w, 1)
                for m in range(HC):
                    v.tensor_scalar(y[:, m, :], xu[:, m, :], cs[:, C_D + m:C_D + m + 1], None, ALU.mult
                                    ).then_inc(dve_dl, 1)
                dve.wait_ge(dve_w, 4 * nb + 4)
                dve.wait_ge(dve_dl, HC * (nb + 1))
                tt_(du[:], delta[:], xu[:], ALU.mult).then_inc(dve_y, 1)

            def ssm_post(b):
                dve.wait_ge(dma_x, 16 * (b + 1))
                stats(2 * b, xu, True)
                for c in range(LC):
                    normed(xnT, xu, c).then_inc(dve_zh, 1)
                dve.wait_ge(act_tz, b + 1)
                stt(xnT[:], delta[:], 1.0, xnT[:], ALU.add, ALU.mult).then_inc(dve_z, 1)
                dve.wait_ge(dve_z, b + 1)
                dve.wait_ge(pool_y, PRIME + 64 * (b + 1))
                tt_(du[:], y, xnT[:], ALU.mult).then_inc(dve_y3, 1)
                dve.wait_ge(dma_out, 16 * (b + 1))
                for lc in range(LC):
                    dve.wait_ge(pe_yt, LC * b + lc + 1)
                    stt(x1[:, lc, :], four[lc][:], tgx[:], xu[:, lc, :], ALU.mult, ALU.add).then_inc(dve_x1, 1)

            def router(b):
                dve.wait_ge(dve_x1, LC * (b + 1))
                stats(2 * b + 1, x1, False)
                for c in range(LC):
                    normed(xu, x1, c).then_inc(dve_xn, 1)
                for hc in range(HC):
                    dve.wait_ge(act_xnT, HC * b + hc + 1)
                    lo(xe_l[:, hc, :], four[hc][:], xe_h[:, hc, :]).then_inc(dve_xl, 1)
                step = chain(dve_rt, ROUTE_STEPS * b)
                lg = b_q[:, 0:LC * NE].rearrange("p (c n) -> p c n", c=LC)
                s_ = sc[:, :, 0:NE]
                dve.wait_ge(pe_lg, b + 1)
                step(v.tensor_reduce(mx[:], lg, AX_X, ALU.max))
                step(tt_(s_, lg, mx[:].unsqueeze(2).broadcast_to([P, LC, NE]), ALU.subtract))
                dve.wait_ge(act_ex, b + 1)
                step(v.tensor_reduce(mx[:], s_, AX_X, ALU.add))
                step(v.reciprocal(mx[:], mx[:]))
                step(tt_(s_, s_, mx[:].unsqueeze(2).broadcast_to([P, LC, NE]), ALU.mult))
                step(carrier(2), False)
                for c in range(LC):
                    step(v.max(m8[:, c, :], s_[:, c, :]), c == LC - 1)
                step(v.memset(m8[:, :, TOPK:8], -1.0))
                step(carrier(3), False)
                for c in range(LC):
                    step(v.match_replace(rep[:, c, :], m8[:, c, :], sc[:, c, :], 0.0), c == LC - 1)
                step(tt_(wd, s_, rep[:, :, 0:NE], ALU.subtract))
                step = chain(dve_ft, FLAT_STEPS * b)
                dve.wait_ge(pe_fl, b + 1)
                fv = fz.rearrange("p g k -> p (g k)")
                bc = [P, LC * NF, NK]
                step(v.tensor_copy(flat.rearrange("p g k -> p (g k)"), b_u0[:, 0:LC * NE]))
                step(v.tensor_scalar(fz, flat, 0.0, -1e9, ALU.is_equal, ALU.mult))
                step(tt_(fz, fz, flat, ALU.add))
                step(v.tensor_reduce(g1[:], fz, AX_X, ALU.max))
                step(tt_(fz, fz, g1[:].unsqueeze(2).broadcast_to(bc), ALU.subtract))
                dve.wait_ge(act_fe, b + 1)
                step(v.tensor_reduce(g1[:], fz, AX_X, ALU.add))
                step(v.reciprocal(g1[:], g1[:]))
                step(v.tensor_reduce(g2[:], flat, AX_X, ALU.add))
                step(v.tensor_scalar(scal[:].rearrange("p c f -> p (c f)"), g2[:], tgf[:], None, ALU.mult))
                step(tt_(fz, fz, g1[:].unsqueeze(2).broadcast_to(bc), ALU.mult))
                step(v.tensor_copy(soft2, fv.rearrange("p (c n) -> p c n", c=LC).unsqueeze(2)
                                   .broadcast_to([P, LC, 2, NE])))
                dve.wait_ge(act_sr, b + 1)
                dve.wait_ge(act_sT, b + 1)
                lo(soft_s[HALF:P, :], b_g1[HALF:P, :], rnd[HALF:P, :]).then_inc(dve_sT, 1)

            def ws_lo(r):
                dve.wait_ge(act_ws, 3 * r + 3)
                lo(ws[HALF:P, :], b_q[HALF:P, :], rnd[HALF:P, :]).then_inc(dve_ws, 1)

            def mask_up(k, first):
                dve.wait_ge(pool_mu, 2 * k + 2)
                if not first:
                    dve.wait_ge(pe_xe, HC * k)
                stt(mu[:], rnd[:].bitcast(F32), cs[:, C_MA:C_MA + 1], raw_r[:, R_MU:R_MU + H], ALU.mult, ALU.add
                    ).then_inc(dve_mu, 1)

            def xe(b, e, r):
                for c in range(HC):
                    dve.wait_ge(pe_xe, HC * r + c + 1)
                    if c >= 2:
                        dve.wait_ge(dve_xe, HC * x_(b, e) + c - 1)
                    tt_(xt[:, c % 2, :], bd[c % 2][:], xnT[:, c, :], ALU.add).then_inc(dve_xt, 1)
                    if c:
                        xe_lo(b, e, c - 1)
                xe_lo(b, e, HC - 1)

            def xe_lo(b, e, c):
                dve.wait_ge(act_xe, HC * x_(b, e) + c + 1)
                lo(xe_l[:, c, :], xt[:, c % 2, :], xe_h[:, c, :]).then_inc(dve_xe, 1)

            def body(b, e, last, routed, nxt, ssm):
                a, r = a_(b, e), (r_(b, e) if routed else None)
                if ssm:
                    selectors(b + 1, e)
                if routed:
                    dve.wait_ge(pe_qa, r + 1)
                    dve.wait_ge(act_wrc, r + 1)
                    tt_(aw[:], b_q[:], wr_c[:], ALU.mult).then_inc(dve_aw, 1)
                    dve.wait_ge(act_aw, r + 1)
                    lo(aw_l[:], aw[:], aw_h[:]).then_inc(dve_awl, 1)
                if routed and not (last and not nxt):
                    mask_up(r + 1, False)

                def hidden(m):
                    w = IW[m]
                    t = tt[0:w, m % 2, :]
                    dve.wait_ge(act_tanh, IC * a + m + 1)
                    stt(t, t, 1.0, bg[m][0:w, :], ALU.add, ALU.mult).then_inc(dve_g2, 1)
                    dve.wait_ge(dve_g2, IC * a + m + 1)
                    stt(t, t, 0.5, bu[m][0:w, :], ALU.mult, ALU.mult).then_inc(dve_h, 1)
                    dve.wait_ge(act_hh, IC * a + m + 1)
                    lo(hl[0:w, m, :], t, hh[0:w, m, :]).then_inc(dve_hl, 1)

                def tiles(*js):
                    if ssm:
                        for j in js:
                            tile(b + 1, e, j)

                def add_down(tc):
                    dve.wait_ge(pe_dn, LC * a + tc + 2)
                    s_ = col(scal[:].rearrange("p c f -> p (c f)"), tc * NF + e) if routed else tgf[:]
                    stt(x1[:, tc, :], bd[tc % 2][:], s_, x1[:, tc, :], ALU.mult, ALU.add).then_inc(dve_dn, 1)

                tiles(0, 1)
                hidden(0)
                tiles(2, 3)
                hidden(1)
                tiles(4)
                if nxt:
                    ws_lo(r + 1)
                tiles(5)
                hidden(2)
                if nxt:
                    xe(b, e + 1, r + 1)
                elif routed:
                    for c in range(HC):
                        dve.wait_ge(act_xe, HC * x_(b, NF) + c + 1)
                        lo(xe_l[:, c, :], xnT[:, c, :], xe_h[:, c, :]).then_inc(dve_xe, 1)
                if routed:
                    dve.wait_ge(pe_dqa, r + 1)
                    tt_(aw[:], b_q[:], wr_c[:], ALU.mult).then_inc(dve_aw, 1)
                    dve.wait_ge(act_daw, 2 * r + 2)
                    lo(daw_s[HALF:P, :], aw[HALF:P, :], rnd[HALF:P, :]).then_inc(dve_daw, 1)
                tiles(6)
                add_down(0)
                add_down(1)
                tiles(7)
                add_down(2)
                add_down(3)

            v.memset(yx[:], 0.0).then_inc(set_dve, 1)
            v.memset(ones[:], 1.0).then_inc(set_dve, 1)
            v.memset(sc[:], -1.0).then_inc(set_dve, 1)
            v.memset(pad[:, 7:8], 0.0).then_inc(dve_scan, PRIME)
            v.memset(pad[:, 8:9], 0.0).then_inc(dve_p, 1)
            v.memset(pad[:, 9:10], 0.0).then_inc(dve_dn, 1)
            v.memset(pad[:, 0:1], 0.0).then_inc(pe_dn, 1)
            v.memset(pad[:, 1:2], 0.0).then_inc(dve_daw, 1)
            v.memset(pad[:, 10:11], 0.0).then_inc(dma_out, 16)
            v.memset(pad[:, 11:12], 0.0).then_inc(set_dve, 1)
            dve.wait_ge(dma_cst, 32)
            v.tensor_scalar(cwh[:], cs[:, C_CW:C_CW + HC * TAPS], 0.5, None, ALU.mult).then_inc(set_dve, 1)
            v.tensor_scalar(cbh[:], cs[:, C_CB:C_CB + HC], 0.5, None, ALU.mult).then_inc(set_dve, 1)
            v.tensor_copy(inv_f[:], inv_i[:]).then_inc(set_dve, 1)
            dve.wait_ge(set_dve, 7)
            v.tensor_scalar(pm[:], inv_f[:], cs[0:NE, C_IO:C_IO + 1], None, ALU.is_equal).then_inc(set_dve, 1)
            dve.wait_ge(set_act, 4)
            lo(gw_l[:], cs[:, C_GW:C_GW + HC * NE].rearrange("p (c n) -> p c n", c=HC), gw_h[:]).then_inc(set_dve, 1)
            v.tensor_scalar(a_neg[:], a_neg[:], -1.0, None, ALU.mult).then_inc(set_dve, 1)
            ssm_pre(0, True)
            mask_up(0, True)
            with dve.Fori(0, NF) as e:
                selectors(0, e)
                for j in range(8):
                    tile(0, e, j)

            def batch(b, last):
                ssm_post(b)
                if not last:
                    ssm_pre(b + 1, False)
                router(b)
                ws_lo(r_(b, 0))
                xe(b, 0, r_(b, 0))
                with dve.Fori(0, NF - 1) as e:
                    body(b, e, last, True, True, not last)
                body(b, NF - 1, last, True, False, not last)
                body(b, NF, last, False, False, False)
                body(b, NF + 1, last, False, False, False)

            with dve.Fori(0, B - 1) as b:
                batch(b, False)
            batch(B - 1, True)


def kernel(**inputs):
    import numpy as np
    import concourse.bacc as bacc
    from concourse.bass_utils import run_bass_kernel_spmd

    def get(n):
        return np.asarray(inputs[n])

    def chunks(w, pad=0):
        k, n = w.shape
        if pad:
            w = np.concatenate([w, np.zeros((pad, n), w.dtype)])
        return w.reshape(-1, P, n).transpose(1, 0, 2).reshape(P, -1)

    x = np.ascontiguousarray(get("x"))
    f32 = x.dtype
    ctxT = np.stack([chunks(c.T) for c in get("ctx_1024")])
    w = {n: get("L0_ffn_" + n) for n in ("mask_up_W", "gate_W", "gate_qa", "gate_qb", "gate_scale", "up_W", "up_qa",
                                         "up_qb", "up_scale", "down_W", "down_qa", "down_qb", "down_scale",
                                         "sh_gate_W", "sh_up_W", "sh_down_W", "gate_weight", "inv_mapping")}
    m = {n: get("L0_xattn_" + n) for n in ("in_proj_w", "conv_w", "conv_b", "x_proj_w", "dt_proj_w", "dt_proj_b",
                                           "A_log", "D")}
    gu, dd, rr = [], [], []
    pad = IC * P - I
    for f in range(NF):
        gu.append(np.concatenate([chunks(w["gate_W"][f].T), chunks(w["up_W"][f].T)], 1))
        qa = w["down_qa"][f].reshape(KR, I).T
        qb = w["down_qb"][f].transpose(0, 2, 1).reshape(KR, H)
        dd.append(np.concatenate([chunks(w["down_W"][f].T, pad), chunks(np.concatenate([qa, qa], 1), pad),
                                  np.concatenate([qb, qb]), np.broadcast_to(w["down_scale"][f], (P, H))], 1))
        qa = np.concatenate([w["gate_qa"][f].reshape(KR, H), w["up_qa"][f].reshape(KR, H)])
        qb = np.concatenate([w[n][f].transpose(0, 2, 1).reshape(KR, I) for n in ("gate_qb", "up_qb")])
        qs = np.concatenate([np.broadcast_to(w[n][f], (HALF, I)) for n in ("gate_scale", "up_scale")])
        mup = np.repeat(w["mask_up_W"][f].T, NR, 0)
        p_, c_ = np.arange(P)[:, None] % HALF, np.arange(P)[None, :] % HALF
        selr = (p_ == f * NK + c_ // NR).astype(f32)
        rr.append(np.concatenate([chunks(qa.T), qb, qs, np.concatenate([mup, mup]), selr], 1))
    for s in range(2):
        rows = slice(s * I, (s + 1) * I)
        gu.append(np.concatenate([chunks(w["sh_gate_W"][rows].T), chunks(w["sh_up_W"][rows].T)], 1))
        d = chunks(w["sh_down_W"][:, rows].T, pad)
        dd.append(np.concatenate([d, np.zeros((P, D_ALL - IC * H), f32)], 1))
    xp = np.zeros((H, P), f32)
    xp[:, 0:DR + 2 * NS] = xp[:, HALF:HALF + DR + 2 * NS] = m["x_proj_w"].T
    dt = np.zeros((P, H), f32)
    dt[0:DR] = dt[HALF:HALF + DR] = m["dt_proj_w"].T
    pre = np.concatenate([chunks(m["in_proj_w"].T), chunks(xp), np.zeros((P, D_QB - IC * H), f32), dt], 1)
    i = np.arange(P)[:, None]
    j = np.arange(2 * NS)[None, :]
    cst = np.concatenate([
        np.eye(P), i % NR == 0, (i < HALF) & (i % NR == 1), i % HALF == DR + j,
        chunks(m["A_log"]), chunks(m["conv_w"]), chunks(m["conv_b"][:, None]), chunks(m["dt_proj_b"][:, None]),
        chunks(m["D"][:, None]), chunks(w["gate_weight"].T), np.broadcast_to(get("g_xattn"), (P, 1)),
        np.broadcast_to(get("g_ffn"), (P, 1)), i], 1).astype(f32)
    arrays = {"x": x, "ctxT": ctxT, "gu": np.stack(gu), "dd": np.stack(dd), "pre": pre, "rr": np.stack(rr),
              "cst": cst, "inv": w["inv_mapping"].reshape(-1)}
    nc = bacc.Bacc("TRN2", target_bir_lowering=False, num_devices=1)
    args, feed = [], {}
    for n, a in arrays.items():
        a = np.ascontiguousarray(a)
        feed[f"in_{n}"] = a
        args.append(nc.dram_tensor(f"in_{n}", a.shape, mybir.dt.from_np(a.dtype), kind="ExternalInput").ap())
    args.append(nc.dram_tensor("out_0", x.shape, F32, kind="ExternalOutput").ap())
    gated_ssm_moe(nc, *args)
    r = run_bass_kernel_spmd(nc, [feed], core_ids=[0])
    return r.results[0]["out_0"]
```

```python
from contextlib import ExitStack

import concourse.bass as bass
from concourse import mybir

F32 = mybir.dt.float32
F32R = mybir.dt.float32r
I32 = mybir.dt.int32
ALU = mybir.AluOpType
ACT = mybir.ActivationFunctionType
AX_X = mybir.AxisListType.X

P = 128
B, L, H = 4, 512, 512
HC = H // P
LC = L // P
DM = 256
NS, DR, TAPS = 16, 16, 4
NF, NK, NR = 8, 8, 8
NE = NF * NK
KR = NK * NR
TOPK = 6
I = 352
IC = 3
IW = [min(P, I - P * m) for m in range(IC)]
NX = NF + 2
EPS = 1e-5
HALF = P // 2

GU = 2 * HC * I
D_W, D_QA, D_QB, D_S = 0, IC * H, IC * H + IC * P, IC * H + IC * P + H
D_SPLIT, D_ALL = D_S, D_S + H
PRE_IN, PRE_XP, PRE_DT, PRE_ALL = 0, 2 * H, 3 * H, 4 * H
R_QA, R_QB, R_S = 0, HC * P, HC * P + I
R_MU, R_SEL = R_S + I, R_S + I + H
R_SPLIT, R_ALL = R_S, R_SEL + P
C_ID, C_MA, C_MB, C_E, C_AL, C_CW, C_CB, C_DB, C_D, C_GW, C_GX, C_GF, C_IO, C_ALL = (
    0, 128, 129, 130, 162, 226, 242, 246, 250, 254, 510, 511, 512, 513)


def gated_ssm_moe(nc, x, ctxT, gu, dd, pre, rr, cst, inv, out):
    with ExitStack() as ctx:
        def sb(name, shape, dt=F32):
            return ctx.enter_context(nc.sbuf_tensor(name, shape, dt))

        def sem(name):
            return ctx.enter_context(nc.semaphore(name))

        raw_gu = sb("raw_gu", [P, GU])
        raw_d = sb("raw_d", [P, D_ALL])
        raw_r = sb("raw_r", [P, R_ALL])
        gu_h, gu_l = sb("gu_h", [P, 2, HC, I], F32R), sb("gu_l", [P, 2, HC, I], F32R)
        d_h, d_l = sb("d_h", [P, D_SPLIT], F32R), sb("d_l", [P, D_SPLIT], F32R)
        r_h, r_l = sb("r_h", [P, R_SPLIT], F32R), sb("r_l", [P, R_SPLIT], F32R)
        mu = sb("mu", [P, H], F32R)
        r_sel = sb("r_sel", [P, P], F32R)
        cs = sb("cs", [P, C_ALL])
        inv_i, inv_f = sb("inv_i", [NE, NE], I32), sb("inv_f", [NE, NE])
        pm = sb("pm", [NE, NE])
        ones = sb("ones", [P, P])
        a_neg = sb("a_neg", [P, HC * NS])
        cwh, cbh = sb("cwh", [P, HC * TAPS]), sb("cbh", [P, HC])
        gw = cs[:, C_GW:C_GW + HC * NE].rearrange("p (c n) -> p c n", c=HC)
        tgx, tgf = sb("tgx", [P, 1]), sb("tgf", [P, 1])
        x1 = sb("x1", [P, LC, H])
        xu = sb("xu", [P, LC, H])
        xnT = sb("xnT", [P, HC, L])
        xe_h, xe_l = sb("xe_h", [P, HC, L], F32R), sb("xe_l", [P, HC, L], F32R)
        xt = sb("xt", [P, 2, L])
        wr_n, wr_c = sb("wr_next", [P, L]), sb("wr_cur", [P, L])
        rnd = sb("rnd", [P, L], F32R)
        ws = sb("ws", [P, L], F32R)
        soft_s = sb("soft_s", [P, L], F32R)
        aw = sb("aw", [P, L])
        aw_h, aw_l = sb("aw_h", [P, L], F32R), sb("aw_l", [P, L], F32R)
        daw_s = sb("daw_s", [P, L], F32R)
        tt = sb("tt", [P, 2, L])
        hh, hl = sb("hh", [P, IC, L], F32R), sb("hl", [P, IC, L], F32R)
        delta, du = sb("delta", [P, HC, L]), sb("du", [P, HC, L])
        yx = sb("yx", [P, HC, L + TAPS - 1])
        y = yx[:, :, TAPS - 1:]
        s_st = sb("s_st", [P, L], F32R)
        b_rep, c_rep = sb("b_rep", [P, 2, L]), sb("c_rep", [P, 2, L])
        sel = sb("sel", [P, 4, P], F32R)
        dA = sb("dA", [P, 2, L])
        wt = sb("wt", [P, 2, L])
        bst, mv = sb("bst", [P, LC, 6]), sb("mv", [P, LC, 2])
        st = sb("st", [P, 8, LC])
        mx = sb("mx", [P, LC])
        pad = sb("pad", [P, 16])
        sc = sb("sc", [P, LC, NE + 2])
        rep = xt[:, 0, 0:LC * (NE + 2)].rearrange("p (c n) -> p c n", c=LC)
        m8 = sb("m8", [P, LC, 8])
        wd = xt[:, 1, 0:LC * NE].rearrange("p (c n) -> p c n", c=LC)
        flat = tt[:, 0, 0:LC * NE].rearrange("p (g k) -> p g k", k=NK)
        fz = tt[:, 1, 0:LC * NE].rearrange("p (g k) -> p g k", k=NK)
        g1, g2 = sb("g1", [P, LC * NF]), sb("g2", [P, LC * NF])
        soft2 = wr_c[:].rearrange("p (c a n) -> p c a n", c=LC, a=2)
        wdT = aw[0:NE, :]
        scal = sb("scal", [P, LC, NF])

        def bank(name):
            return ctx.enter_context(nc.psum_tensor(name, [P, 512], F32))

        b_q, b_g0, b_u0, b_g1, b_u1, b_d0, b_d1, b_s = [bank("b_" + n) for n in
                                                         ("q", "g0", "u0", "g1", "u1", "d0", "d1", "s")]
        bg, bu, bd = [b_g0, b_g1, b_g0], [b_u0, b_u1, b_u0], [b_d0, b_d1, b_g0, b_u0]
        bx = [b_d0, b_d1, b_g1, b_u1]
        four = [b_g0, b_u0, b_g1, b_u1]

        ident = cs[:, C_ID:C_ID + P]

        dma_cst, dma_gu, dma_d, dma_r, dma_x, dma_ctx = (
            sem(n) for n in ("dma_cst", "dma_gu", "dma_d", "dma_r", "dma_x", "dma_ctx"))
        dma_out = sem("dma_out")
        set_dve, set_act = (
            sem(n) for n in ("set_dve", "set_act"))
        pool_scale_d, act_hi_d, dve_lo_d, pool_scale_r, act_hi_r, dve_lo_r = (
            sem(n) for n in ("pool_scale_d", "act_hi_d", "dve_lo_d", "pool_scale_r", "act_hi_r", "dve_lo_r"))
        act_hi_gu, pool_lo_g, pool_lo_u, act_mu, act_rsel = (
            sem(n) for n in ("act_hi_gu", "pool_lo_g", "pool_lo_u", "act_mu", "act_rsel"))
        dve_mu = sem("dve_mu")
        pe_qa, pe_gu, pe_wr, pe_xe, pe_dqa, pe_dn = (
            sem(n) for n in ("pe_qa", "pe_gu", "pe_wr", "pe_xe", "pe_dqa", "pe_dn"))
        pe_rep, act_ws, dve_ws, act_wrc, dve_xt, act_xe = (
            sem(n) for n in ("pe_rep", "act_ws", "dve_ws", "act_wrc", "dve_xt", "act_xe"))
        dve_xe, dve_aw, act_aw, dve_awl, act_daw, dve_daw = (
            sem(n) for n in ("dve_xe", "dve_aw", "act_aw", "dve_awl", "act_daw", "dve_daw"))
        act_tanh, dve_g2, dve_h, act_hh, dve_hl, dve_dn = (
            sem(n) for n in ("act_tanh", "dve_g2", "dve_h", "act_hh", "dve_hl", "dve_dn"))
        act_y = sem("act_y")
        dve_sel, act_rep, act_da, pool_dbu, dve_scan, dve_p = (
            sem(n) for n in ("dve_sel", "act_rep", "act_da", "pool_dbu", "dve_scan", "dve_p"))
        y_added = sem("y_added")
        act_hi_in, dve_lo_in, act_hi_x, pool_lo_x, act_d_u = (
            sem(n) for n in ("act_hi_in", "dve_lo_in", "act_hi_x", "pool_lo_x", "act_d_u"))
        act_ctx, pool_ctx, pe_in, act_xs, dve_cv, act_tc = (
            sem(n) for n in ("act_ctx", "pool_ctx", "pe_in", "act_xs", "dve_cv", "act_tc"))
        act_cv = sem("act_cv")
        dve_u, act_u, dve_ul, pe_xd, act_rnd, act_s = (
            sem(n) for n in ("dve_u", "act_u", "dve_ul", "pe_xd", "act_rnd", "act_s"))
        dve_s, pe_dt, act_abs, act_relu, act_ev, dve_w = (
            sem(n) for n in ("dve_s", "pe_dt", "act_abs", "act_relu", "act_ev", "dve_w"))
        act_ln, dve_y = (
            sem(n) for n in ("act_ln", "dve_y"))
        dve_stat, act_sqrt, dve_zh, act_tz, dve_z, dve_y3 = (
            sem(n) for n in ("dve_stat", "act_sqrt", "dve_zh", "act_tz", "dve_z", "dve_y3"))
        pe_yt, dve_x1, act_x1 = (
            sem(n) for n in ("pe_yt", "dve_x1", "act_x1"))
        dve_xn, pe_xnT, act_xnT, pe_lg = (
            sem(n) for n in ("dve_xn", "pe_xnT", "act_xnT", "pe_lg"))
        dve_rt, act_ex, pe_wdT, act_wdT, pe_fl, dve_ft = (
            sem(n) for n in ("dve_rt", "act_ex", "pe_wdT", "act_wdT", "pe_fl", "dve_ft"))
        act_fe, pe_sT, act_sr, act_sT, dve_sT = (
            sem(n) for n in ("act_fe", "pe_sT", "act_sr", "act_sT", "dve_sT"))

        def a_(b, e):
            return NX * b + e

        def r_(b, e):
            return NF * b + e

        def x_(b, e):
            return (NF + 1) * b + e

        def d_loaded(b, e):
            return 11 * b + 2 + e + (0 if isinstance(b, int) and b == B - 1 else 1)

        def pre_loaded(nb):
            return 1 if isinstance(nb, int) and nb == 0 else 11 * (nb - 1) + 2

        PRIME, PRIME_Y = 2, 4

        def ssm_tile(nb, e, j):
            return 64 * nb + 8 * e + j

        def ssm_rep(nb, e, k):
            return 32 * nb + 4 * e + k

        def col(t, i, n=1):
            return t[:, bass.ds(i, n)] if not isinstance(i, int) else t[:, i:i + n]

        ROUTE_STEPS, FLAT_STEPS, STAT_STEPS = 17, 11, 17
        SETUP_DVE = 9
        ctx_h, ctx_l = [aw_h, daw_s], [aw_l, ws]
        u_h = [hh[:, 0, :], hh[:, 1, :], hh[:, 2, :], aw_h[:]]
        u_l = [hl[:, 0, :], hl[:, 1, :], hl[:, 2, :], aw_l[:]]
        w_e = [wt, tt]
        bt = [b_q, b_s]
        b_dt = [b_g1, b_u1, b_g0, b_u0]

        ring = [wt[:, 0, :], wt[:, 1, :]]
        ring_0 = ring + [xt[:, 0, :], xt[:, 1, :]]

        def three(w_h, w_l, v_h, v_l):
            return ((w_h, v_h), (w_h, v_l), (w_l, v_h))

        block = ctx.enter_context(nc.Block())

        @block.sync
        def _(sp):
            def load_gu(e):
                sp.dma_start(raw_gu[:], gu[e] if isinstance(e, int) else gu[bass.ds(e, 1)]
                             .rearrange("a p n -> (a p) n")).then_inc(dma_gu, 16)

            def load_d(e):
                sp.dma_start(raw_d[:], dd[e] if isinstance(e, int) else dd[bass.ds(e, 1)]
                             .rearrange("a p n -> (a p) n")).then_inc(dma_d, 16)

            def load_r(e):
                sp.dma_start(raw_r[:], rr[e] if isinstance(e, int) else rr[bass.ds(e, 1)]
                             .rearrange("a p n -> (a p) n")).then_inc(dma_r, 16)

            def load_pre():
                sp.dma_start(raw_d[:, 0:PRE_ALL], pre).then_inc(dma_d, 16)

            def of_batch(t, b):
                return t[b] if isinstance(b, int) else t[bass.ds(b, 1)].rearrange("a p n -> (a p) n")

            def load_x(b):
                src = x[b] if isinstance(b, int) else x[bass.ds(b, 1)].rearrange("a l h -> (a l) h")
                sp.dma_start(xu[:], src.rearrange("(c p) h -> p c h", p=P)).then_inc(dma_x, 16)

            def load_ctx(b):
                sp.wait_ge(dve_scan, PRIME + 64 * b)
                sp.dma_start(dA[:], of_batch(ctxT, b)).then_inc(dma_ctx, 16)

            def next_d(b, e, after):
                sp.wait_ge(dve_lo_d, a_(b, e) + 1)
                if isinstance(e, int) and e == NX - 1:
                    if after == "pre":
                        load_pre()
                    elif after == "experts":
                        load_d(0)
                else:
                    load_d(e + 1)

            def first_d_and_x(nb):
                sp.wait_ge(pool_lo_x, nb + 1)
                sp.wait_ge(dve_lo_in, nb + 1)
                load_d(0)
                sp.wait_ge(act_d_u, HC * (nb + 1))
                sp.wait_ge(dve_y, nb + 1)
                load_x(nb)

            def next_r(b, e, to):
                sp.wait_ge(dve_lo_r, r_(b, e) + 2)
                sp.wait_ge(dve_mu, r_(b, e) + 2)
                sp.wait_ge(act_rsel, r_(b, e) + 2)
                load_r(to)

            def next_gu(b, e, to):
                sp.wait_ge(pool_lo_u, a_(b, e) + 2)
                load_gu(to)

            sp.dma_start(cs[:], cst).then_inc(dma_cst, 16)
            sp.dma_start(inv_i[:], inv.partition_broadcast(NE)).then_inc(dma_cst, 16)
            sp.dma_start(dA[:], ctxT[0]).then_inc(dma_ctx, 16)
            load_pre()
            load_r(0)
            load_gu(0)
            sp.wait_ge(pool_lo_x, 1)
            sp.wait_ge(dve_lo_in, 1)
            load_pre()
            sp.wait_ge(dve_y, 1)
            sp.wait_ge(act_d_u, HC)
            load_x(0)
            sp.wait_ge(dve_lo_r, 1)
            sp.wait_ge(dve_mu, 1)
            sp.wait_ge(act_rsel, 1)
            load_r(1)
            sp.wait_ge(pool_lo_u, 1)
            load_gu(1)

            load_ctx(1)
            first_d_and_x(1)

            def batch(b, after):
                last = after is None
                with sp.Fori(0, NF - 2) as e:
                    next_d(b, e, after)
                    next_r(b, e, e + 2)
                    next_gu(b, e, e + 2)
                for e in range(NF - 2, NX):
                    next_d(b, e, after)
                    if e < NF and not last:
                        next_r(b, e, e + 2 - NF)
                    if e == NF - 1 and after == "pre":
                        load_ctx(b + 2)
                    if e + 2 < NX:
                        next_gu(b, e, e + 2)
                    elif not last:
                        next_gu(b, e, e + 2 - NX)
                sp.wait_ge(dve_dn, LC * NX * (b + 1) + 1)
                dst = out[b] if isinstance(b, int) else out[bass.ds(b, 1)].rearrange("a l h -> (a l) h")
                sp.dma_start(dst.rearrange("(c p) h -> p c h", p=P), x1[:]).then_inc(dma_out, 16)
                if after == "pre":
                    first_d_and_x(b + 2)

            with sp.Fori(0, B - 2) as b:
                batch(b, "pre")
            batch(B - 2, "experts")
            batch(B - 1, None)
            sp.wait_ge(dma_out, 16 * (B + 1))

        @block.tensor
        def _(pe):
            mm = nc.tensor.matmul

            def replicate(nb, e, k):
                pe.wait_ge(dve_sel, ssm_rep(nb, e, k) + 1)
                pe.wait_ge(act_rep, ssm_rep(nb, e, k) + 1)
                mm(b_s[:], sel[:, k, :], s_st[:], start=True, stop=True).then_inc(pe_rep, 1)

            def in_proj(nb):
                pe.wait_ge(pool_ctx, 2 * (nb + 1))
                pe.wait_ge(dve_lo_in, nb + 1)
                if isinstance(nb, int):
                    if nb == 1:
                        pe.wait_ge(act_y, HC)
                else:
                    pe.wait_ge(dve_dn, LC * NX * (nb - 1) + 1)
                for m in range(HC):
                    n = 0
                    for c in range(DM // P):
                        o = PRE_IN + c * H + m * P
                        for w, v in three(d_h[:, o:o + P], d_l[:, o:o + P], ctx_h[c][:], ctx_l[c][:]):
                            i = mm(four[m][:], w, v, start=(n == 0), stop=(n == 5))
                            n += 1
                    i.then_inc(pe_in, 1)

            def x_proj(nb):
                pe.wait_ge(pool_lo_x, nb + 1)
                n = 0
                for c in range(HC):
                    pe.wait_ge(dve_ul, HC * nb + c + 1)
                    o = PRE_XP + c * P
                    for w, v in three(d_h[:, o:o + P], d_l[:, o:o + P], u_h[c], u_l[c]):
                        i = mm(b_s[:], w, v, start=(n == 0), stop=(n == 11))
                        n += 1
                i.then_inc(pe_xd, 1)
                pe.wait_ge(dve_s, nb + 1)
                for m in range(HC):
                    o = PRE_DT + m * P
                    mm(b_dt[m][:], d_h[:, o:o + P], s_st[:], start=True, stop=False)
                    mm(b_dt[m][:], d_l[0:DR, o:o + P], s_st[0:DR, :], start=False, stop=True).then_inc(pe_dt, 1)

            def y_transposed(b, lcs):
                pe.wait_ge(dve_y3, b + 1)
                for lc in lcs:
                    if lc >= 2:
                        pe.wait_ge(dve_x1, LC * b + lc - 1)
                    for dc in range(HC):
                        i = nc.tensor.transpose(bt[lc % 2][:, dc * P:(dc + 1) * P], du[:, dc, lc * P:(lc + 1) * P],
                                                ident)
                    i.then_inc(pe_yt, 1)

            def xn_transposed(b, hcs):
                pe.wait_ge(dve_xn, LC * (b + 1))
                for hc in hcs:
                    if hc >= 2:
                        pe.wait_ge(act_xnT, HC * b + hc - 1)
                    for tc in range(LC):
                        i = nc.tensor.transpose(bt[hc % 2][:, tc * P:(tc + 1) * P],
                                                delta[:, tc, hc * P:(hc + 1) * P], ident)
                    i.then_inc(pe_xnT, 1)

            def logits(b):
                pe.wait_ge(act_xnT, HC * (b + 1))
                for tc in range(LC):
                    for c in range(HC):
                        i = mm(b_q[:, tc * NE:(tc + 1) * NE], xnT[:, c, tc * P:(tc + 1) * P], gw[:, c, :],
                               start=(c == 0), stop=(c == HC - 1))
                i.then_inc(pe_lg, 1)

            def weights_transposed(b):
                pe.wait_ge(dve_rt, ROUTE_STEPS * (b + 1))
                for tc in range(LC):
                    i = mm(b_s[0:NE, tc * P:(tc + 1) * P], wd[:, tc, :], ident, start=True, stop=True)
                i.then_inc(pe_wdT, 1)

            def places(b):
                pe.wait_ge(act_wdT, b + 1)
                for tc in range(LC):
                    i = mm(b_q[:, tc * NE:(tc + 1) * NE], wdT[:, tc * P:(tc + 1) * P], pm[:], start=True, stop=True)
                i.then_inc(pe_fl, 1)

            def soft_transposed(b):
                pe.wait_ge(dve_ft, FLAT_STEPS * (b + 1))
                for tc in range(LC):
                    i = nc.tensor.transpose(b_s[:, tc * P:(tc + 1) * P],
                                            soft2[:, tc, :, :].rearrange("p a k -> p (a k)"), ident)
                i.then_inc(pe_sT, 1)
                pe.wait_ge(dve_sT, b + 1)
                pe.wait_ge(act_sT, b + 1)

            def wrep(r):
                pe.wait_ge(act_rsel, r + 1)
                mm(b_q[:], r_sel[:], soft_s[:], start=True, stop=True).then_inc(pe_wr, 1)

            def delta_xe(r, dn_before, h_before):
                pe.wait_ge(dve_mu, r + 1)
                pe.wait_ge(dve_ws, r + 1)
                pe.wait_ge(act_ws, r + 1)
                pe.wait_ge(dve_dn, dn_before)
                for c in range(HC):
                    if c == 2 and h_before is not None:
                        pe.wait_ge(*h_before)
                    mm(bx[c][:], mu[:, c * P:(c + 1) * P], ws[:], start=True, stop=True).then_inc(pe_xe, 1)

            def body(b, e, last, routed, nxt, ssm, start=False):
                a, r = a_(b, e), (r_(b, e) if routed else None)
                xi = x_(b, e if routed else NF)
                if routed:
                    pe.wait_ge(dve_lo_r, r + 1)
                    n = 0
                    for c in range(HC):
                        pe.wait_ge(dve_xe, HC * xi + c + 1)
                        o = R_QA + c * P
                        for w, v in three(r_h[:, o:o + P], r_l[:, o:o + P], xe_h[:, c, :], xe_l[:, c, :]):
                            i = mm(b_q[:], w, v, start=(n == 0), stop=(n == 11))
                            n += 1
                    i.then_inc(pe_qa, 1)
                else:
                    pe.wait_ge(dve_xe, HC * xi + HC)
                for m in range(IC):
                    if m == 0:
                        pe.wait_ge(dve_dn, LC * a + 1)
                    if m == 2:
                        pe.wait_ge(dve_h, IC * a + 1)
                    for j, out_b in ((0, bg[m]), (1, bu[m])):
                        if m == 0:
                            pe.wait_ge((pool_lo_g, pool_lo_u)[j], a + 1)
                        n = 0
                        for c in range(HC):
                            cols = slice(m * P, m * P + IW[m])
                            for w, v in three(gu_h[:, j, c, cols], gu_l[:, j, c, cols], xe_h[:, c, :], xe_l[:, c, :]):
                                i = mm(out_b[0:IW[m], :], w, v, start=(n == 0), stop=(n == 11 and not routed))
                                n += 1
                    if m < 2 and ssm:
                        replicate(b + 1, e, 2 + m)
                    if m == IC - 1 and nxt:
                        delta_xe(r + 1, LC * a + 1, (dve_h, IC * a + 2))
                    if routed:
                        if m == 0:
                            pe.wait_ge(dve_awl, r + 1)
                        cols = slice(R_QB + m * P, R_QB + m * P + IW[m])
                        for k, (w, v) in enumerate(((r_h, aw_h), (r_h, aw_l), (r_l, aw_h))):
                            for j, out_b in ((0, bg[m]), (1, bu[m])):
                                rows = slice(j * HALF, (j + 1) * HALF)
                                i = mm(out_b[0:IW[m], :], w[rows, cols], v[rows, :], start=False, stop=(k == 2))
                    i.then_inc(pe_gu, 1)
                    if m == 1:
                        if nxt:
                            wrep(r + 1)
                    if start and e == NF and m > 0:
                        y_transposed(b + 1, (2 * m - 2, 2 * m - 1))
                    if start and e == NX - 1:
                        if m < IC - 1:
                            xn_transposed(b + 1, (2 * m, 2 * m + 1))
                        else:
                            logits(b + 1)
                def adapter_a(m):
                    pe.wait_ge(dve_hl, IC * a + m + 1)
                    k = slice(0, IW[m])
                    o = D_QA + m * P
                    n = 3 * m
                    for w, v in three(d_h[k, o:o + P], d_l[k, o:o + P], hh[k, m, :], hl[k, m, :]):
                        i = mm(b_q[:], w, v, start=(n == 0), stop=(n == 8))
                        n += 1
                    if m == IC - 1:
                        i.then_inc(pe_dqa, 1)

                def down(tc, ms=range(IC)):
                    t = slice(tc * P, (tc + 1) * P)
                    for m in ms:
                        n = 3 * m
                        k = slice(0, IW[m])
                        o = D_W + m * H
                        for v, w in ((hh, d_h), (hl, d_h), (hh, d_l)):
                            i = mm(bd[tc][:], v[k, m, t], w[k, o:o + H], start=(n == 0),
                                   stop=(n == 8 and not routed))
                            n += 1
                        if m == IC - 1 and not routed:
                            i.then_inc(pe_dn, 1)

                def adapter_b(tc):
                    t = slice(tc * P, (tc + 1) * P)
                    mm(bd[tc][:], daw_s[:, t], d_h[:, D_QB:D_QB + H], start=False, stop=False)
                    mm(bd[tc][:], daw_s[0:HALF, t], d_l[0:HALF, D_QB:D_QB + H],
                       start=False, stop=True).then_inc(pe_dn, 1)

                pe.wait_ge(dve_lo_d, a_(b, e) + 1)
                if routed:
                    adapter_a(0)
                    adapter_a(1)
                    if nxt:
                        pe.wait_ge(dve_xt, HC * (r + 1) + 1)
                    down(0, range(IC - 1))
                    if nxt:
                        pe.wait_ge(dve_xt, HC * (r + 1) + 2)
                    down(1, range(IC - 1))
                    adapter_a(IC - 1)
                    down(0, [IC - 1])
                    down(1, [IC - 1])
                    down(2)
                    if nxt and ssm:
                        replicate(b + 1, e + 1, 0)
                    pe.wait_ge(dve_daw, r + 2)
                    pe.wait_ge(act_daw, 2 * r + 2)
                    for tc in range(3):
                        adapter_b(tc)
                    down(3)
                    adapter_b(3)
                    if nxt and ssm:
                        replicate(b + 1, e + 1, 1)
                else:
                    pe.wait_ge(dve_hl, IC * a + IC - 1)
                    down(0, range(IC - 1))
                    down(1, range(IC - 1))
                    pe.wait_ge(dve_hl, IC * a + IC)
                    down(0, [IC - 1])
                    down(1, [IC - 1])
                    down(2)
                    if start and e == NX - 1:
                        weights_transposed(b + 1)
                    down(3)

            pe.wait_ge(set_dve, SETUP_DVE)
            in_proj(0)
            x_proj(0)
            pe.wait_ge(dve_y, 1)
            pe.wait_ge(act_d_u, HC)
            for dc in range(HC):
                mm(four[dc][:], ident, y[:, dc, :], start=True, stop=False, skip_group_check=True)

            replicate(0, 0, 0)
            replicate(0, 0, 1)

            def sum_states(e, stop):
                for j in range(8):
                    if j == 0:
                        replicate(0, e, 2)
                        replicate(0, e, 3)
                    elif j == 4 and not stop:
                        replicate(0, e + 1, 0)
                        replicate(0, e + 1, 1)
                    pe.wait_ge(dve_p, ssm_tile(0, e, j) + 9)
                    mm(four[j % 4][:], ident, ring_0[j % 4], start=False, stop=(stop and j >= 4),
                       skip_group_check=True).then_inc(y_added, 1)

            with pe.Fori(0, NF - 1) as e:
                sum_states(e, False)
            sum_states(NF - 1, True)

            def bridge(b, pre):
                places(b)
                if pre:
                    in_proj(b + 1)
                soft_transposed(b)
                if pre:
                    x_proj(b + 1)
                    replicate(b + 1, 0, 0)
                wrep(r_(b, 0))
                if pre:
                    replicate(b + 1, 0, 1)
                delta_xe(r_(b, 0), LC * a_(b, 0) + 1, (act_relu, HC * (b + 1) + 2) if pre else None)
                if pre:
                    pe.wait_ge(act_relu, HC * (b + 2))

            def batch(b, last, ssm):
                with pe.Fori(0, NF - 1) as e:
                    body(b, e, last, True, True, ssm)
                body(b, NF - 1, last, True, False, ssm)
                body(b, NF, last, False, False, False, not last)
                body(b, NF + 1, last, False, False, False, not last)

            y_transposed(0, range(LC))
            xn_transposed(0, range(HC))
            logits(0)
            weights_transposed(0)
            bridge(0, True)
            with pe.Fori(0, B - 2) as b:
                batch(b, False, True)
                bridge(b + 1, True)
            batch(B - 2, False, True)
            bridge(B - 1, False)
            batch(B - 1, True, False)

        @block.scalar
        def _(act):
            def f(out_, in_, func, **k):
                return nc.scalar.activation(out_, in_, func, **k)

            def rounded(out_, in_):
                return f(out_, in_, ACT.Copy)

            def split_d(loaded, routed, pe_ready, r=None):
                act.wait_ge(dma_d, 16 * loaded)
                if r is not None:
                    act.wait_ge(pool_scale_d, r + 1)
                for s_, v in pe_ready:
                    act.wait_ge(s_, v)
                n = D_SPLIT if routed else IC * H
                rounded(d_h[:, 0:n], raw_d[:, 0:n]).then_inc(act_hi_d, 1)

            def mu_conv(k, first):
                act.wait_ge(dma_r, 16 * (k + 1))
                if not first:
                    act.wait_ge(dve_daw, k)
                raw = raw_r[:, R_MU:R_MU + H]
                rounded(rnd[:], raw).then_inc(act_mu, 1)
                act.wait_ge(act_mu, 2 * k + 1)
                f(raw, raw, ACT.Copy, scale=cs[:, C_MB:C_MB + 1]).then_inc(act_mu, 1)
                if not first:
                    act.wait_ge(pe_wr, k)
                rounded(r_sel[:], raw_r[:, R_SEL:R_SEL + P]).then_inc(act_rsel, 1)

            def split_r(k, a_done):
                act.wait_ge(pool_scale_r, k + 1)
                if a_done is not None:
                    act.wait_ge(pe_gu, a_done)
                rounded(r_h[:], raw_r[:, 0:R_SPLIT]).then_inc(act_hi_r, 1)

            def split_gu(k, a_done, js=range(2)):
                act.wait_ge(dma_gu, 16 * (k + 1))
                if a_done is not None:
                    act.wait_ge(pe_gu, a_done)
                for j in js:
                    rounded(gu_h[:, j], raw_gu[:, j * HC * I:(j + 1) * HC * I].rearrange("p (c i) -> p c i", c=HC)
                            ).then_inc(act_hi_gu, 1)

            def rep_copy(nb, e, k):
                act.wait_ge(pe_rep, ssm_rep(nb, e, k) + 1)
                n = 16 * nb + 2 * e + k // 2
                if k % 2 == 0:
                    act.wait_ge(pool_dbu, 4 * n + 4)
                    dst = b_rep[:, k // 2, :]
                else:
                    act.wait_ge(dve_p, 4 * n + 4)
                    dst = c_rep[:, k // 2, :]
                f(dst, b_s[:], ACT.Copy).then_inc(act_rep, 1)

            def exp_tile(nb, e, j):
                t = ssm_tile(nb, e, j)
                if j == 0:
                    act.wait_ge(dve_y, nb + 1)
                act.wait_ge(dve_scan, t + 1)
                dc, k = j % 4, j // 4
                f(dA[:, j % 2, :], delta[:, dc, :], ACT.Exp,
                  scale=col(a_neg, 2 * e + (dc * NS + k))).then_inc(act_da, 1)

            def wr_copy(r):
                act.wait_ge(pe_wr, r + 1)
                act.wait_ge(dve_mu, r + 1)
                f(wr_n[:], b_q[:], ACT.Copy).then_inc(act_ws, 1)
                rounded(rnd[HALF:P, :], b_q[HALF:P, :]).then_inc(act_ws, 1)
                rounded(ws[0:HALF, :], b_q[0:HALF, :]).then_inc(act_ws, 1)

            def xe_hi(b, e, r, cs_=range(HC)):
                xi = x_(b, e)
                for c in cs_:
                    act.wait_ge(dve_xt, HC * r + c + 1)
                    rounded(xe_h[:, c, :], xt[:, c % 2, :]).then_inc(act_xe, 1)

            def round_ctx(nb):
                act.wait_ge(dma_ctx, 16 * (nb + 1))
                for c in range(DM // P):
                    rounded(ctx_h[c][:], dA[:, c, :]).then_inc(act_ctx, 1)

            def split_pre(nb):
                act.wait_ge(dma_d, 16 * pre_loaded(nb))
                if isinstance(nb, int):
                    if nb == 1:
                        act.wait_ge(pe_dt, HC)
                else:
                    act.wait_ge(pe_dn, LC * NX * (nb - 1) + 1)
                rounded(d_h[:, 0:PRE_XP], raw_d[:, 0:PRE_XP]).then_inc(act_hi_in, 1)
                rounded(d_h[:, PRE_XP:PRE_ALL], raw_d[:, PRE_XP:PRE_ALL]).then_inc(act_hi_x, 1)

            def in_proj(nb):
                if not (isinstance(nb, int) and nb == 0):
                    act.wait_ge(dve_y3, nb)
                for m in range(HC):
                    act.wait_ge(pe_in, HC * nb + m + 1)
                    f(y[:, m, :], four[m][:], ACT.Copy).then_inc(act_xs, 1)
                    f(delta[:, m, :], four[m][:], ACT.Identity, bias=cbh[:, m:m + 1],
                      scale=cwh[:, m * TAPS + TAPS - 1:m * TAPS + TAPS]).then_inc(act_cv, 1)

            def conv_tanh(nb):
                for m in range(HC):
                    act.wait_ge(dve_cv, 12 * nb + 6 * (m // 2) + 4 + m % 2 + 1)
                    f(du[:, m, :], delta[:, m, :], ACT.Tanh).then_inc(act_tc, 1)
                for m in range(HC):
                    act.wait_ge(dve_u, HC * nb + m + 1)
                    rounded(u_h[m], xu[:, m, :]).then_inc(act_u, 1)

            def x_proj(nb):
                act.wait_ge(pe_xd, nb + 1)
                rounded(rnd[HALF:P, :], b_s[HALF:P, :]).then_inc(act_rnd, 1)
                rounded(s_st[0:HALF, :], b_s[0:HALF, :]).then_inc(act_s, 1)
                for m in range(HC):
                    act.wait_ge(pe_dt, HC * nb + m + 1)
                    bias = cs[:, C_DB + m:C_DB + m + 1]
                    f(du[:, m, :], b_dt[m][:], ACT.Abs, bias=bias).then_inc(act_abs, 1)
                    f(delta[:, m, :], b_dt[m][:], ACT.Relu, bias=bias).then_inc(act_relu, 1)
                act.wait_ge(act_abs, HC * (nb + 1))
                f(du[:], du[:], ACT.Exp, scale=-1.0).then_inc(act_ev, 1)

            def softplus(nb):
                for q in range(2):
                    act.wait_ge(dve_w, 8 * nb + q + 1)
                    f(y[:, 2 * q:2 * q + 2, :], w_e[q][:], ACT.Ln).then_inc(act_ln, 1)
                for m in range(HC):
                    act.wait_ge(dve_w, 8 * nb + 4 + m // 2 + 1)
                    f(y[:, m, :], xu[:, m, :], ACT.Copy, scale=cs[:, C_D + m:C_D + m + 1]).then_inc(act_d_u, 1)

            def root(u):
                act.wait_ge(dve_stat, STAT_STEPS * u + 11)
                f(st[:, 1, :], st[:, 0, :], ACT.Sqrt).then_inc(act_sqrt, 1)

            def tanh_z(b):
                act.wait_ge(act_da, 64 * (b + 1))
                act.wait_ge(dve_zh, LC * (b + 1))
                f(delta[:], xnT[:], ACT.Tanh).then_inc(act_tz, 1)

            def xnT_copy(b, hcs):
                for hc in hcs:
                    act.wait_ge(pe_xnT, HC * b + hc + 1)
                    f(xnT[:, hc, :], bt[hc % 2][:], ACT.Copy).then_inc(act_xnT, 1)

            def exp_scores(b):
                act.wait_ge(dve_rt, ROUTE_STEPS * b + 2)
                f(sc[:, :, 0:NE], sc[:, :, 0:NE], ACT.Exp).then_inc(act_ex, 1)

            def bridge(b, pre):
                act.wait_ge(pe_wdT, b + 1)
                f(wdT, b_s[0:NE, :], ACT.Copy).then_inc(act_wdT, 1)
                if pre:
                    split_pre(b + 1)
                act.wait_ge(dve_ft, FLAT_STEPS * b + 5)
                f(fz, fz, ACT.Exp).then_inc(act_fe, 1)
                if pre:
                    in_proj(b + 1)
                act.wait_ge(pe_sT, b + 1)
                rounded(rnd[HALF:P, :], b_s[HALF:P, :]).then_inc(act_sr, 1)
                rounded(soft_s[0:HALF, :], b_s[0:HALF, :]).then_inc(act_sT, 1)
                act.wait_ge(dma_out, 16 * (b + 1))
                act.wait_ge(dve_x1, LC * (b + 1))
                f(x1[:], xu[:], ACT.Copy).then_inc(act_x1, 1)
                if pre:
                    conv_tanh(b + 1)
                    x_proj(b + 1)
                    rep_copy(b + 1, 0, 0)
                wr_copy(r_(b, 0))
                if pre:
                    rep_copy(b + 1, 0, 1)
                xe_hi(b, 0, r_(b, 0))
                if pre:
                    softplus(b + 1)

            def body(b, e, last, routed, nxt, ssm, start=False, pre=False):
                a, r = a_(b, e), (r_(b, e) if routed else None)
                more_r = routed and not (last and not nxt)
                if routed:
                    act.wait_ge(act_ws, 3 * (r + 1))
                    f(wr_c[:], wr_n[:], ACT.Copy).then_inc(act_wrc, 1)
                if ssm:
                    exp_tile(b + 1, e, 0)
                if routed:
                    act.wait_ge(dve_aw, 2 * r + 1)
                    rounded(aw_h[:], aw[:]).then_inc(act_aw, 1)
                if start and routed:
                    root(2 * (b + 1))
                if ssm:
                    exp_tile(b + 1, e, 1)
                split_d(d_loaded(b, e), routed, [(pe_dn, LC * a + 1)], r)
                if ssm:
                    exp_tile(b + 1, e, 2)
                    rep_copy(b + 1, e, 2)
                if more_r:
                    mu_conv(r + 1, False)

                def tanh(m):
                    w = IW[m]
                    act.wait_ge(pe_gu, IC * a + m + 1)
                    if m == 2:
                        act.wait_ge(dve_hl, IC * a + 1)
                    f(tt[0:w, m % 2, :], bg[m][0:w, :], ACT.Tanh, scale=0.5).then_inc(act_tanh, 1)

                def h_hi(m):
                    w = IW[m]
                    act.wait_ge(dve_h, IC * a + m + 1)
                    rounded(hh[0:w, m, :], tt[0:w, m % 2, :]).then_inc(act_hh, 1)

                tanh(0)
                h_hi(0)
                if start and e == NX - 1 and pre:
                    round_ctx(b + 2)
                if ssm:
                    exp_tile(b + 1, e, 3)
                    rep_copy(b + 1, e, 3)
                if start and e == NX - 1:
                    xnT_copy(b + 1, (0, 1))
                tanh(1)
                if nxt:
                    wr_copy(r + 1)
                if ssm:
                    exp_tile(b + 1, e, 4)
                h_hi(1)
                if ssm:
                    exp_tile(b + 1, e, 5)
                if start and e == NX - 1:
                    xnT_copy(b + 1, (2, 3))
                tanh(2)
                h_hi(2)
                if start and e == NX - 1:
                    exp_scores(b + 1)
                def next_x(c):
                    if nxt:
                        xe_hi(b, e + 1, r + 1, (c,))
                    elif routed:
                        rounded(xe_h[:, c, :], xnT[:, c, :]).then_inc(act_xe, 1)

                more_gu = not (last and isinstance(e, int) and e == NX - 1)
                if routed:
                    next_x(0)
                if more_gu:
                    split_gu(a + 1, IC * (a + 1), (0,))
                if routed:
                    next_x(1)
                    next_x(2)
                if not nxt and more_gu:
                    split_gu(a + 1, IC * (a + 1), (1,))
                if ssm:
                    exp_tile(b + 1, e, 6)
                if routed:
                    act.wait_ge(dve_aw, 2 * r + 2)
                    rounded(rnd[HALF:P, :], aw[HALF:P, :]).then_inc(act_daw, 1)
                    rounded(daw_s[0:HALF, :], aw[0:HALF, :]).then_inc(act_daw, 1)
                    next_x(3)
                if ssm:
                    exp_tile(b + 1, e, 7)
                if nxt:
                    split_gu(a + 1, IC * (a + 1), (1,))
                if ssm and nxt:
                    rep_copy(b + 1, e + 1, 0)
                if more_r:
                    split_r(r + 1, IC * (a + 1))
                if start and e == NF:
                    root(2 * (b + 1) + 1)
                if start and routed:
                    tanh_z(b + 1)
                if ssm and nxt:
                    rep_copy(b + 1, e + 1, 1)

            act.wait_ge(dma_cst, 32)
            f(a_neg[:], cs[:, C_AL:C_AL + HC * NS], ACT.Exp).then_inc(set_act, 1)
            f(tgx[:], cs[:, C_GX:C_GX + 1], ACT.Tanh).then_inc(set_act, 1)
            f(tgf[:], cs[:, C_GF:C_GF + 1], ACT.Tanh).then_inc(set_act, 1)
            f(pad[:, 4:5], cs[:, 0:1], ACT.Copy).then_inc(act_rep, 1)
            act.wait_ge(set_dve, SETUP_DVE)
            round_ctx(0)
            split_pre(0)
            in_proj(0)
            conv_tanh(0)
            x_proj(0)
            softplus(0)
            mu_conv(0, True)
            split_r(0, None)
            split_gu(0, None)
            rep_copy(0, 0, 0)
            rep_copy(0, 0, 1)

            def tiles_0(e, more):
                for j in range(8):
                    exp_tile(0, e, j)
                    if j in (1, 2):
                        rep_copy(0, e, j + 1)
                    elif j in (5, 6) and more:
                        rep_copy(0, e + 1, j - 5)

            with act.Fori(0, NF - 1) as e:
                tiles_0(e, True)
            tiles_0(NF - 1, False)
            act.wait_ge(y_added, PRIME_Y + 64)
            for dc in range(HC):
                f(y[:, dc, :], four[dc][:], ACT.Copy).then_inc(act_y, 1)

            def batch(b, last, ssm, pre):
                with act.Fori(0, NF - 1) as e:
                    body(b, e, last, True, True, ssm)
                body(b, NF - 1, last, True, False, ssm, not last)
                body(b, NF, last, False, False, False, not last)
                body(b, NF + 1, last, False, False, False, not last, pre)

            root(0)
            tanh_z(0)
            root(1)
            round_ctx(1)
            xnT_copy(0, range(HC))
            exp_scores(0)
            bridge(0, True)
            with act.Fori(0, B - 2) as b:
                batch(b, False, True, True)
                bridge(b + 1, True)
            batch(B - 2, False, True, False)
            bridge(B - 1, False)
            batch(B - 1, True, False, False)

        @block.gpsimd
        def _(pool):
            v = nc.gpsimd

            def lo(out_, raw, hi):
                return v.tensor_tensor(out_, raw, hi.bitcast(F32), ALU.subtract)

            def scale_d(b, e):
                pool.wait_ge(dma_d, 16 * d_loaded(b, e))
                v.tensor_tensor(raw_d[:, D_QB:D_QB + H], raw_d[:, D_QB:D_QB + H], raw_d[:, D_S:D_S + H],
                                ALU.mult).then_inc(pool_scale_d, 1)

            def scale_r(k):
                pool.wait_ge(dma_r, 16 * (k + 1))
                v.tensor_tensor(raw_r[:, R_QB:R_QB + I], raw_r[:, R_QB:R_QB + I], raw_r[:, R_S:R_S + I],
                                ALU.mult).then_inc(pool_scale_r, 1)

            def split_gu(k, js=range(2)):
                for j in js:
                    pool.wait_ge(act_hi_gu, 2 * k + j + 1)
                    lo(gu_l[:, j], raw_gu[:, j * HC * I:(j + 1) * HC * I].rearrange("p (c i) -> p c i", c=HC),
                       gu_h[:, j]).then_inc((pool_lo_g, pool_lo_u)[j], 1)

            def dbu(nb, e, j, ring):
                t = ssm_tile(nb, e, j)
                if j == 0:
                    pool.wait_ge(dve_y, nb + 1)
                if j % 4 == 0:
                    pool.wait_ge(act_rep, ssm_rep(nb, e, j // 2) + 2)
                pool.wait_ge(y_added, PRIME_Y + t + 1 - len(ring))
                v.tensor_tensor(ring[j % len(ring)], du[:, j % 4, :], b_rep[:, j // 4, :], ALU.mult).then_inc(pool_dbu, 1)

            def split_x_dt(nb):
                pool.wait_ge(act_hi_x, nb + 1)
                o = slice(PRE_XP, PRE_ALL)
                lo(d_l[:, o], raw_d[:, o], d_h[:, o]).then_inc(pool_lo_x, 1)

            def split_ctx(nb):
                for c in range(DM // P):
                    pool.wait_ge(act_ctx, 2 * nb + c + 1)
                    lo(ctx_l[c][:], dA[:, c, :], ctx_h[c][:]).then_inc(pool_ctx, 1)

            def add_y(nb, e, j):
                if j == 0:
                    pool.wait_ge(act_d_u, HC * (nb + 1))
                pool.wait_ge(dve_p, ssm_tile(nb, e, j) + 9)
                yd = y[:, j % 4, :]
                v.tensor_tensor(yd, yd, ring[j % 2], ALU.add).then_inc(y_added, 1)

            def body(b, e, last, routed, nxt, ssm, start=False):
                a, r = a_(b, e), (r_(b, e) if routed else None)
                more_r = routed and not (last and not nxt)
                if ssm:
                    for j in range(6):
                        add_y(b + 1, e, j)
                        dbu(b + 1, e, j + 2, ring)
                        if j == 2:
                            scale_r(r + 1)
                elif more_r:
                    scale_r(r + 1)
                if nxt:
                    scale_d(b, e + 1)
                if not (last and isinstance(e, int) and e == NX - 1):
                    split_gu(a + 1, (0,))
                    if ssm and nxt:
                        add_y(b + 1, e, 6)
                    split_gu(a + 1, (1,))
                if ssm:
                    if not nxt:
                        add_y(b + 1, e, 6)
                    add_y(b + 1, e, 7)
                    if nxt:
                        dbu(b + 1, e + 1, 0, ring)
                        dbu(b + 1, e + 1, 1, ring)

            v.memset(pad[:, 5:6], 0.0).then_inc(pool_dbu, 8)
            v.memset(pad[:, 6:7], 0.0).then_inc(y_added, PRIME_Y)
            split_ctx(0)
            split_x_dt(0)
            scale_r(0)
            split_gu(0)
            with pool.Fori(0, NF) as e:
                for j in range(8):
                    dbu(0, e, j, ring_0)

            def first_tiles(nb):
                dbu(nb, 0, 0, ring)
                dbu(nb, 0, 1, ring)

            def batch(b, last, ssm, pre):
                with pool.Fori(0, NF - 1) as e:
                    body(b, e, last, True, True, ssm)
                body(b, NF - 1, last, True, False, ssm)
                body(b, NF, last, False, False, False)
                if pre:
                    split_ctx(b + 2)
                body(b, NF + 1, last, False, False, False)
                if pre:
                    split_x_dt(b + 2)
                if not last:
                    scale_d(b + 1, 0)
                if pre:
                    first_tiles(b + 2)

            split_ctx(1)
            split_x_dt(1)
            scale_d(0, 0)
            first_tiles(1)
            with pool.Fori(0, B - 2) as b:
                batch(b, False, True, True)
            batch(B - 2, False, True, False)
            batch(B - 1, True, False, False)

        @block.vector
        def _(dve):
            v = nc.vector
            tt_ = v.tensor_tensor

            def stt(out_, a, s_, b_, op0, op1):
                return v.scalar_tensor_tensor(out=out_, in0=a, scalar=s_, in1=b_, op0=op0, op1=op1)

            def lo(out_, whole, hi):
                return tt_(out_, whole, hi.bitcast(F32), ALU.subtract)

            def chain(s_, base):
                done = [0]

                def step(ins, wait=True):
                    done[0] += 1
                    ins.then_inc(s_, 1)
                    if wait:
                        dve.wait_ge(s_, base + done[0])
                return step

            def carrier(k):
                return v.memset(pad[:, 12 + k:13 + k], 0.0)

            def selectors(nb, e, ks):
                for k in ks:
                    v.tensor_scalar(sel[:, k, :], ones[:], col(cs, 2 * e + (C_E + (k % 2) * NS + k // 2)), None,
                                    ALU.mult).then_inc(dve_sel, 1)

            def tile(nb, e, j, ring):
                t = ssm_tile(nb, e, j)
                w = ring[j % len(ring)]
                dve.wait_ge(act_da, t + 1)
                dve.wait_ge(pool_dbu, t + 9)
                v.tensor_tensor_scan(w, dA[:, j % 2, :], w, 0.0, ALU.mult, ALU.add).then_inc(dve_scan, 1)
                if j % 4 == 0:
                    dve.wait_ge(act_rep, ssm_rep(nb, e, j // 2 + 1) + 2)
                dve.wait_ge(dve_scan, t + 3)
                tt_(w, w, c_rep[:, j // 4, :], ALU.mult).then_inc(dve_p, 1)

            def stats(u, src, half):
                row_sums(u, src)
                scales(u, half)

            def row_sums(u, src):
                step = chain(dve_stat, STAT_STEPS * u)
                step(carrier(0), False)
                for c in range(LC):
                    step(v.bn_stats(bst[:, c, :], src[:, c, :]), c == LC - 1)

            def scales(u, half):
                step = chain(dve_stat, STAT_STEPS * u + 1 + LC)
                step(carrier(1), False)
                for c in range(LC):
                    step(v.bn_aggr(mv[:, c, :], bst[:, c, :]), c == LC - 1)
                step(v.tensor_scalar(st[:, 0, :], mv[:, :, 1], EPS, None, ALU.add))
                dve.wait_ge(act_sqrt, u + 1)
                step(v.reciprocal(st[:, 2, :], st[:, 1, :]))
                step(tt_(st[:, 3, :], st[:, 0, :], st[:, 2, :], ALU.mult))
                step(tt_(st[:, 4, :], st[:, 1, :], st[:, 3, :], ALU.add))
                step(v.reciprocal(st[:, 5, :], st[:, 4, :]))
                step(v.tensor_scalar(st[:, 6, :], st[:, 5, :], 1.0 if half else 2.0, None, ALU.mult))
                step(stt(st[:, 7, :], mv[:, :, 0], -1.0, st[:, 6, :], ALU.mult, ALU.mult))

            def normed(dst, src, c):
                return v.tensor_scalar(dst[:, c, :], src[:, c, :], st[:, 6, c:c + 1], st[:, 7, c:c + 1],
                                       ALU.mult, ALU.add)

            def split_in(nb):
                dve.wait_ge(act_hi_in, nb + 1)
                lo(d_l[:, 0:PRE_XP], raw_d[:, 0:PRE_XP], d_h[:, 0:PRE_XP]).then_inc(dve_lo_in, 1)

            def conv(nb):
                for pair in range(HC // 2):
                    for j in range(TAPS - 1):
                        k = TAPS - 2 - j
                        for m in (2 * pair, 2 * pair + 1):
                            w = cwh[:, m * TAPS + k:m * TAPS + k + 1]
                            src = yx[:, m, k:k + L]
                            if j == 0:
                                dve.wait_ge(act_cv, HC * nb + m + 1)
                                dve.wait_ge(act_xs, HC * nb + m + 1)
                            else:
                                dve.wait_ge(dve_cv, 12 * nb + 6 * pair + 2 * (j - 1) + m % 2 + 1)
                            stt(delta[:, m, :], src, w, delta[:, m, :], ALU.mult, ALU.add).then_inc(dve_cv, 1)

            def u_parts(nb):
                if not (isinstance(nb, int) and nb == 0):
                    dve.wait_ge(act_x1, nb)
                for m in range(HC):
                    dve.wait_ge(act_tc, HC * nb + m + 1)
                    stt(xu[:, m, :], du[:, m, :], 1.0, delta[:, m, :], ALU.add, ALU.mult).then_inc(dve_u, 1)
                for m in range(HC):
                    dve.wait_ge(act_u, HC * nb + m + 1)
                    tt_(u_l[m], xu[:, m, :], u_h[m].bitcast(F32), ALU.subtract).then_inc(dve_ul, 1)

            def lo_state(nb):
                dve.wait_ge(act_rnd, nb + 1)
                dve.wait_ge(act_s, nb + 1)
                lo(s_st[HALF:P, :], b_s[HALF:P, :], rnd[HALF:P, :]).then_inc(dve_s, 1)

            def one_plus(nb):
                dve.wait_ge(act_ev, nb + 1)
                for q in range(2):
                    v.tensor_scalar(w_e[q][:], du[:, 2 * q:2 * q + 2, :], 1.0, None, ALU.add).then_inc(dve_w, 1)

            def softplus(nb):
                half = [slice(0, 2), slice(2, 4)]
                for q in range(2):
                    dve.wait_ge(act_ln, 2 * nb + q + 1)
                    stt(w_e[q][:], w_e[q][:], 1.0, du[:, half[q], :], ALU.subtract, ALU.subtract).then_inc(dve_w, 1)
                for q in range(2):
                    dve.wait_ge(dve_w, 8 * nb + 2 + q + 1)
                    tt_(w_e[q][:], y[:, half[q], :], w_e[q][:], ALU.subtract).then_inc(dve_w, 1)
                dve.wait_ge(act_relu, HC * (nb + 1))
                for q in range(2):
                    dve.wait_ge(dve_w, 8 * nb + 4 + q + 1)
                    tt_(delta[:, half[q], :], delta[:, half[q], :], w_e[q][:], ALU.add).then_inc(dve_w, 1)
                dve.wait_ge(dve_w, 8 * nb + 8)
                tt_(du[:], delta[:], xu[:], ALU.mult).then_inc(dve_y, 1)

            def norm_z(b):
                for c in range(LC):
                    normed(xnT, xu, c).then_inc(dve_zh, 1)

            def gate_z(b):
                dve.wait_ge(act_tz, b + 1)
                stt(xnT[:], delta[:], 1.0, xnT[:], ALU.add, ALU.mult).then_inc(dve_z, 1)

            def y_gated(b):
                dve.wait_ge(dve_z, b + 1)
                dve.wait_ge(act_y, HC)
                dve.wait_ge(y_added, PRIME_Y + 64 * (b + 1))
                tt_(du[:], y, xnT[:], ALU.mult).then_inc(dve_y3, 1)

            def add_ssm(b, lc):
                dve.wait_ge(pe_yt, LC * b + lc + 1)
                stt(xu[:, lc, :], bt[lc % 2][:], tgx[:], xu[:, lc, :], ALU.mult, ALU.add).then_inc(dve_x1, 1)

            def norm_x1(b):
                for c in range(LC):
                    normed(delta, xu, c).then_inc(dve_xn, 1)

            def route(b):
                step = chain(dve_rt, ROUTE_STEPS * b)
                lg = b_q[:, 0:LC * NE].rearrange("p (c n) -> p c n", c=LC)
                s_ = sc[:, :, 0:NE]
                dve.wait_ge(pe_lg, b + 1)
                step(v.tensor_reduce(mx[:], lg, AX_X, ALU.max))
                step(tt_(s_, lg, mx[:].unsqueeze(2).broadcast_to([P, LC, NE]), ALU.subtract))
                dve.wait_ge(act_ex, b + 1)
                step(v.tensor_reduce(mx[:], s_, AX_X, ALU.add))
                step(v.reciprocal(mx[:], mx[:]))
                step(tt_(s_, s_, mx[:].unsqueeze(2).broadcast_to([P, LC, NE]), ALU.mult))
                step(carrier(2), False)
                for c in range(LC):
                    step(v.max(m8[:, c, :], s_[:, c, :]), c == LC - 1)
                step(v.memset(m8[:, :, TOPK:8], -1.0))
                step(carrier(3), False)
                for c in range(LC):
                    step(v.match_replace(rep[:, c, :], m8[:, c, :], sc[:, c, :], 0.0), c == LC - 1)
                step(tt_(wd, s_, rep[:, :, 0:NE], ALU.subtract))

            def flat_weights(b):
                step = chain(dve_ft, FLAT_STEPS * b)
                dve.wait_ge(pe_fl, b + 1)
                fv = fz.rearrange("p g k -> p (g k)")
                bc = [P, LC * NF, NK]
                step(v.tensor_copy(flat.rearrange("p g k -> p (g k)"), b_q[:, 0:LC * NE]))
                step(v.tensor_scalar(fz, flat, 0.0, -1e9, ALU.is_equal, ALU.mult))
                step(tt_(fz, fz, flat, ALU.add))
                step(v.tensor_reduce(g1[:], fz, AX_X, ALU.max))
                step(tt_(fz, fz, g1[:].unsqueeze(2).broadcast_to(bc), ALU.subtract))
                dve.wait_ge(act_fe, b + 1)
                step(v.tensor_reduce(g1[:], fz, AX_X, ALU.add))
                step(v.reciprocal(g1[:], g1[:]))
                step(v.tensor_reduce(g2[:], flat, AX_X, ALU.add))
                step(v.tensor_scalar(scal[:].rearrange("p c f -> p (c f)"), g2[:], tgf[:], None, ALU.mult))
                step(tt_(fz, fz, g1[:].unsqueeze(2).broadcast_to(bc), ALU.mult))
                step(v.tensor_copy(soft2, fv.rearrange("p (c n) -> p c n", c=LC).unsqueeze(2)
                                   .broadcast_to([P, LC, 2, NE])))

            def lo_soft(b):
                dve.wait_ge(act_sr, b + 1)
                dve.wait_ge(act_sT, b + 1)
                lo(soft_s[HALF:P, :], b_s[HALF:P, :], rnd[HALF:P, :]).then_inc(dve_sT, 1)

            def bridge(b, pre):
                if pre:
                    split_in(b + 1)
                flat_weights(b)
                if pre:
                    conv(b + 1)
                lo_soft(b)
                if pre:
                    u_parts(b + 1)
                    lo_state(b + 1)
                    selectors(b + 1, 0, (0, 1))
                    one_plus(b + 1)
                ws_lo(r_(b, 0))
                xe_sum(b, 0, r_(b, 0), 0)
                xe(b, 0, r_(b, 0))
                if pre:
                    softplus(b + 1)
                dve.wait_ge(act_x1, b + 1)

            def split_r(k):
                dve.wait_ge(act_hi_r, k + 1)
                lo(r_l[:], raw_r[:, 0:R_SPLIT], r_h[:]).then_inc(dve_lo_r, 1)

            def ws_lo(r):
                dve.wait_ge(act_ws, 3 * r + 3)
                lo(ws[HALF:P, :], b_q[HALF:P, :], rnd[HALF:P, :]).then_inc(dve_ws, 1)

            def split_d(split_count, routed):
                dve.wait_ge(act_hi_d, split_count)
                n = D_SPLIT if routed else IC * H
                lo(d_l[:, 0:n], raw_d[:, 0:n], d_h[:, 0:n]).then_inc(dve_lo_d, 1)

            def mask_up(k, first):
                dve.wait_ge(act_mu, 2 * k + 2)
                if not first:
                    dve.wait_ge(pe_xe, HC * k)
                stt(mu[:], rnd[:].bitcast(F32), cs[:, C_MA:C_MA + 1], raw_r[:, R_MU:R_MU + H], ALU.mult, ALU.add
                    ).then_inc(dve_mu, 1)

            def xe(b, e, r):
                for c in range(1, HC):
                    xe_sum(b, e, r, c)
                    xe_lo(b, e, c - 1)
                xe_lo(b, e, HC - 1)

            def xe_shared(b, c):
                dve.wait_ge(act_xe, HC * x_(b, NF) + c + 1)
                lo(xe_l[:, c, :], xnT[:, c, :], xe_h[:, c, :]).then_inc(dve_xe, 1)

            def xe_sum(b, e, r, c):
                dve.wait_ge(pe_xe, HC * r + c + 1)
                if c >= 2:
                    dve.wait_ge(dve_xe, HC * x_(b, e) + c - 1)
                tt_(xt[:, c % 2, :], bx[c][:], xnT[:, c, :], ALU.add).then_inc(dve_xt, 1)

            def xe_lo(b, e, c):
                dve.wait_ge(act_xe, HC * x_(b, e) + c + 1)
                lo(xe_l[:, c, :], xt[:, c % 2, :], xe_h[:, c, :]).then_inc(dve_xe, 1)

            def body(b, e, last, routed, nxt, ssm, start=False):
                a, r = a_(b, e), (r_(b, e) if routed else None)
                if routed:
                    dve.wait_ge(pe_qa, r + 1)
                    dve.wait_ge(act_wrc, r + 1)
                    tt_(aw[:], b_q[:], wr_c[:], ALU.mult).then_inc(dve_aw, 1)
                    dve.wait_ge(act_aw, r + 1)
                    lo(aw_l[:], aw[:], aw_h[:]).then_inc(dve_awl, 1)
                more_r = routed and not (last and not nxt)
                if routed and start:
                    dve.wait_ge(dma_x, 16 * (b + 2))
                    stats(2 * (b + 1), xu, True)

                def hidden(m):
                    w = IW[m]
                    t = tt[0:w, m % 2, :]
                    dve.wait_ge(act_tanh, IC * a + m + 1)
                    stt(t, t, 1.0, bg[m][0:w, :], ALU.add, ALU.mult).then_inc(dve_g2, 1)
                    dve.wait_ge(dve_g2, IC * a + m + 1)
                    stt(t, t, 0.5, bu[m][0:w, :], ALU.mult, ALU.mult).then_inc(dve_h, 1)
                    if m > 0 and start and e == NF:
                        add_ssm(b + 1, 2 * m - 2)
                    dve.wait_ge(act_hh, IC * a + m + 1)
                    lo(hl[0:w, m, :], t, hh[0:w, m, :]).then_inc(dve_hl, 1)
                    if m > 0 and start and e == NF:
                        add_ssm(b + 1, 2 * m - 1)

                def tiles(*js):
                    if ssm:
                        for j in js:
                            tile(b + 1, e, j, ring)

                def add_down(tc):
                    dve.wait_ge(pe_dn, LC * a + tc + 2)
                    s_ = col(scal[:].rearrange("p c f -> p (c f)"), tc * NF + e) if routed else tgf[:]
                    stt(x1[:, tc, :], bd[tc][:], s_, x1[:, tc, :], ALU.mult, ALU.add).then_inc(dve_dn, 1)

                if start and e == NF:
                    gate_z(b + 1)
                tiles(0)
                if ssm:
                    selectors(b + 1, e, (2, 3))
                    if nxt:
                        selectors(b + 1, e + 1, (0, 1))
                tiles(1)
                hidden(0)
                if start and e == NF:
                    y_gated(b + 1)
                split_d(a_(b, e) + 1, routed)
                if more_r:
                    mask_up(r + 1, False)
                tiles(2, 3)
                hidden(1)
                if nxt:
                    ws_lo(r + 1)
                tiles(4, 5)
                if nxt:
                    xe_sum(b, e + 1, r + 1, 0)
                    xe_sum(b, e + 1, r + 1, 1)
                hidden(2)
                if nxt:
                    xe_lo(b, e + 1, 0)
                    xe_sum(b, e + 1, r + 1, 2)
                    xe_lo(b, e + 1, 1)
                elif routed:
                    xe_shared(b, 0)
                    xe_shared(b, 1)
                if routed:
                    dve.wait_ge(pe_dqa, r + 1)
                    tt_(aw[:], b_q[:], wr_c[:], ALU.mult).then_inc(dve_aw, 1)
                if nxt:
                    xe_sum(b, e + 1, r + 1, 3)
                elif routed:
                    xe_shared(b, 2)
                if routed:
                    dve.wait_ge(act_daw, 2 * r + 1)
                    lo(daw_s[HALF:P, :], aw[HALF:P, :], rnd[HALF:P, :]).then_inc(dve_daw, 1)
                if nxt:
                    xe_lo(b, e + 1, 2)
                    xe_lo(b, e + 1, 3)
                elif routed:
                    xe_shared(b, 3)
                if start and e == NX - 1:
                    route(b + 1)
                tiles(6, 7)
                if more_r and nxt:
                    split_r(r + 1)
                if start and e == NF:
                    dve.wait_ge(dve_x1, LC * (b + 2))
                    row_sums(2 * (b + 1) + 1, xu)
                add_down(0)
                add_down(1)
                add_down(2)
                add_down(3)
                if start and routed:
                    norm_z(b + 1)
                elif start and e == NF:
                    scales(2 * (b + 1) + 1, False)
                if more_r and not nxt:
                    split_r(r + 1)
                if start and e == NF:
                    norm_x1(b + 1)

            v.memset(yx[:], 0.0).then_inc(set_dve, 1)
            v.memset(ones[:], 1.0).then_inc(set_dve, 1)
            v.memset(sc[:], -1.0).then_inc(set_dve, 1)
            v.memset(pad[:, 7:8], 0.0).then_inc(dve_scan, PRIME)
            v.memset(pad[:, 8:9], 0.0).then_inc(dve_p, 8)
            v.memset(pad[:, 9:10], 0.0).then_inc(dve_dn, 1)
            v.memset(pad[:, 0:1], 0.0).then_inc(pe_dn, 1)
            v.memset(pad[:, 1:2], 0.0).then_inc(dve_daw, 1)
            v.memset(pad[:, 10:11], 0.0).then_inc(dma_out, 16)
            v.memset(pad[:, 11:12], 0.0).then_inc(set_dve, 1)
            dve.wait_ge(dma_cst, 32)
            v.tensor_scalar(cwh[:], cs[:, C_CW:C_CW + HC * TAPS], 0.5, None, ALU.mult).then_inc(set_dve, 1)
            v.tensor_scalar(cbh[:], cs[:, C_CB:C_CB + HC], 0.5, None, ALU.mult).then_inc(set_dve, 1)
            v.tensor_copy(inv_f[:], inv_i[:]).then_inc(set_dve, 1)
            dve.wait_ge(set_dve, 7)
            v.tensor_scalar(pm[:], inv_f[:], cs[0:NE, C_IO:C_IO + 1], None, ALU.is_equal).then_inc(set_dve, 1)
            dve.wait_ge(set_act, 3)
            v.tensor_scalar(a_neg[:], a_neg[:], -1.0, None, ALU.mult).then_inc(set_dve, 1)
            split_in(0)
            conv(0)
            u_parts(0)
            lo_state(0)
            one_plus(0)
            softplus(0)
            mask_up(0, True)
            split_r(0)
            selectors(0, 0, (0, 1))

            def tiles_0(e, more):
                for j in range(8):
                    tile(0, e, j, ring_0)
                    if j == 0:
                        selectors(0, e, (2, 3))
                        if more:
                            selectors(0, e + 1, (0, 1))

            with dve.Fori(0, NF - 1) as e:
                tiles_0(e, True)
            tiles_0(NF - 1, False)

            def batch(b, last, ssm):
                with dve.Fori(0, NF - 1) as e:
                    body(b, e, last, True, True, ssm)
                body(b, NF - 1, last, True, False, ssm, not last)
                body(b, NF, last, False, False, False, not last)
                body(b, NF + 1, last, False, False, False, not last)

            dve.wait_ge(dma_x, 16)
            stats(0, xu, True)
            norm_z(0)
            gate_z(0)
            y_gated(0)
            for lc in range(LC):
                add_ssm(0, lc)
            dve.wait_ge(dve_x1, LC)
            stats(1, xu, False)
            norm_x1(0)
            route(0)
            bridge(0, True)
            with dve.Fori(0, B - 2) as b:
                batch(b, False, True)
                bridge(b + 1, True)
            batch(B - 2, False, True)
            bridge(B - 1, False)
            batch(B - 1, True, False)


def kernel(**inputs):
    import numpy as np
    import concourse.bacc as bacc
    from concourse.bass_utils import run_bass_kernel_spmd

    def get(n):
        return np.asarray(inputs[n])

    def chunks(w, pad=0):
        k, n = w.shape
        if pad:
            w = np.concatenate([w, np.zeros((pad, n), w.dtype)])
        return w.reshape(-1, P, n).transpose(1, 0, 2).reshape(P, -1)

    x = np.ascontiguousarray(get("x"))
    f32 = x.dtype
    ctxT = np.stack([chunks(c.T) for c in get("ctx_1024")])
    w = {n: get("L0_ffn_" + n) for n in ("mask_up_W", "gate_W", "gate_qa", "gate_qb", "gate_scale", "up_W", "up_qa",
                                         "up_qb", "up_scale", "down_W", "down_qa", "down_qb", "down_scale",
                                         "sh_gate_W", "sh_up_W", "sh_down_W", "gate_weight", "inv_mapping")}
    m = {n: get("L0_xattn_" + n) for n in ("in_proj_w", "conv_w", "conv_b", "x_proj_w", "dt_proj_w", "dt_proj_b",
                                           "A_log", "D")}
    gu, dd, rr = [], [], []
    pad = IC * P - I
    for f in range(NF):
        gu.append(np.concatenate([chunks(w["gate_W"][f].T), chunks(w["up_W"][f].T)], 1))
        qa = w["down_qa"][f].reshape(KR, I).T
        qb = w["down_qb"][f].transpose(0, 2, 1).reshape(KR, H)
        dd.append(np.concatenate([chunks(w["down_W"][f].T, pad), chunks(np.concatenate([qa, qa], 1), pad),
                                  np.concatenate([qb, qb]), np.broadcast_to(w["down_scale"][f], (P, H))], 1))
        qa = np.concatenate([w["gate_qa"][f].reshape(KR, H), w["up_qa"][f].reshape(KR, H)])
        qb = np.concatenate([w[n][f].transpose(0, 2, 1).reshape(KR, I) for n in ("gate_qb", "up_qb")])
        qs = np.concatenate([np.broadcast_to(w[n][f], (HALF, I)) for n in ("gate_scale", "up_scale")])
        mup = np.repeat(w["mask_up_W"][f].T, NR, 0)
        p_, c_ = np.arange(P)[:, None] % HALF, np.arange(P)[None, :] % HALF
        selr = (p_ == f * NK + c_ // NR).astype(f32)
        rr.append(np.concatenate([chunks(qa.T), qb, qs, np.concatenate([mup, mup]), selr], 1))
    for s in range(2):
        rows = slice(s * I, (s + 1) * I)
        gu.append(np.concatenate([chunks(w["sh_gate_W"][rows].T), chunks(w["sh_up_W"][rows].T)], 1))
        d = chunks(w["sh_down_W"][:, rows].T, pad)
        dd.append(np.concatenate([d, np.zeros((P, D_ALL - IC * H), f32)], 1))
    xp = np.zeros((H, P), f32)
    xp[:, 0:DR + 2 * NS] = xp[:, HALF:HALF + DR + 2 * NS] = m["x_proj_w"].T
    dt = np.zeros((P, H), f32)
    dt[0:DR] = dt[HALF:HALF + DR] = m["dt_proj_w"].T
    pre = np.concatenate([chunks(m["in_proj_w"].T), chunks(xp), dt], 1)
    i = np.arange(P)[:, None]
    j = np.arange(2 * NS)[None, :]
    cst = np.concatenate([
        np.eye(P), 1 * (i % NR == 0) - 1 * ((i < HALF) & (i % NR == 1)), (i < HALF) & (i % NR == 1), i % HALF == DR + j,
        chunks(m["A_log"]), chunks(m["conv_w"]), chunks(m["conv_b"][:, None]), chunks(m["dt_proj_b"][:, None]),
        chunks(m["D"][:, None]), chunks(w["gate_weight"].T), np.broadcast_to(get("g_xattn"), (P, 1)),
        np.broadcast_to(get("g_ffn"), (P, 1)), i], 1).astype(f32)
    arrays = {"x": x, "ctxT": ctxT, "gu": np.stack(gu), "dd": np.stack(dd), "pre": pre, "rr": np.stack(rr),
              "cst": cst, "inv": w["inv_mapping"].reshape(-1)}
    nc = bacc.Bacc("TRN2", target_bir_lowering=False, num_devices=1)
    args, feed = [], {}
    for n, a in arrays.items():
        a = np.ascontiguousarray(a)
        feed[f"in_{n}"] = a
        args.append(nc.dram_tensor(f"in_{n}", a.shape, mybir.dt.from_np(a.dtype), kind="ExternalInput").ap())
    args.append(nc.dram_tensor("out_0", x.shape, F32, kind="ExternalOutput").ap())
    gated_ssm_moe(nc, *args)
    r = run_bass_kernel_spmd(nc, [feed], core_ids=[0])
    return r.results[0]["out_0"]
```

```python
from contextlib import ExitStack

import concourse.bass as bass
from concourse import mybir

F32 = mybir.dt.float32
F32R = mybir.dt.float32r
I32 = mybir.dt.int32
ALU = mybir.AluOpType
ACT = mybir.ActivationFunctionType
AX_X = mybir.AxisListType.X

P = 128
B, L, H = 4, 512, 512
HC = H // P
LC = L // P
DM = 256
NS, DR, TAPS = 16, 16, 4
NF, NK, NR = 8, 8, 8
NE = NF * NK
KR = NK * NR
TOPK = 6
I = 352
IC = 3
IW = [min(P, I - P * m) for m in range(IC)]
NX = NF + 2
EPS = 1e-5
HALF = P // 2

GU = 2 * HC * I
D_W, D_QA, D_QB, D_S = 0, IC * H, IC * H + IC * P, IC * H + IC * P + H
D_SPLIT, D_ALL = D_S, D_S + H
PRE_IN, PRE_XP, PRE_DT, PRE_ALL = 0, 2 * H, 3 * H, 4 * H
R_QA, R_QB, R_S = 0, HC * P, HC * P + I
R_MU, R_SEL = R_S + I, R_S + I + H
R_SPLIT, R_ALL = R_S, R_SEL + P
C_ID, C_MA, C_MB, C_E, C_AL, C_CW, C_CB, C_DB, C_D, C_GW, C_GX, C_GF, C_IO, C_ALL = (
    0, 128, 129, 130, 162, 226, 242, 246, 250, 254, 510, 511, 512, 513)


def gated_ssm_moe(nc, x, ctxT, gu, dd, pre, rr, cst, inv, out):
    with ExitStack() as ctx:
        def sb(name, shape, dt=F32):
            return ctx.enter_context(nc.sbuf_tensor(name, shape, dt))

        def sem(name):
            return ctx.enter_context(nc.semaphore(name))

        raw_gu = sb("raw_gu", [P, GU])
        raw_d = sb("raw_d", [P, D_ALL])
        raw_r = sb("raw_r", [P, R_ALL])
        gu_h, gu_l = sb("gu_h", [P, 2, HC, I], F32R), sb("gu_l", [P, 2, HC, I], F32R)
        d_h, d_l = sb("d_h", [P, D_SPLIT], F32R), sb("d_l", [P, D_SPLIT], F32R)
        r_h, r_l = sb("r_h", [P, R_SPLIT], F32R), sb("r_l", [P, R_SPLIT], F32R)
        mu = sb("mu", [P, H], F32R)
        r_sel = sb("r_sel", [P, P], F32R)
        cs = sb("cs", [P, C_ALL])
        inv_i, inv_f = sb("inv_i", [NE, NE], I32), sb("inv_f", [NE, NE])
        pm = sb("pm", [NE, NE])
        ones = sb("ones", [P, P])
        a_neg = sb("a_neg", [P, HC * NS])
        cwh, cbh = sb("cwh", [P, HC * TAPS]), sb("cbh", [P, HC])
        gw = cs[:, C_GW:C_GW + HC * NE].rearrange("p (c n) -> p c n", c=HC)
        tgx, tgf = sb("tgx", [P, 1]), sb("tgf", [P, 1])
        x1 = sb("x1", [P, LC, H])
        xu = sb("xu", [P, LC, H])
        xnT = sb("xnT", [P, HC, L])
        xe_h, xe_l = sb("xe_h", [P, HC, L], F32R), sb("xe_l", [P, HC, L], F32R)
        xt = sb("xt", [P, 2, L])
        wr_n, wr_c = sb("wr_next", [P, L]), sb("wr_cur", [P, L])
        rnd = sb("rnd", [P, L], F32R)
        ws = sb("ws", [P, L], F32R)
        soft_s = sb("soft_s", [P, L], F32R)
        aw = sb("aw", [P, L])
        aw_h, aw_l = sb("aw_h", [P, L], F32R), sb("aw_l", [P, L], F32R)
        daw_s = sb("daw_s", [P, L], F32R)
        tt = sb("tt", [P, 2, L])
        hh, hl = sb("hh", [P, IC, L], F32R), sb("hl", [P, IC, L], F32R)
        delta, du = sb("delta", [P, HC, L]), sb("du", [P, HC, L])
        yx = sb("yx", [P, HC, L + TAPS - 1])
        y = yx[:, :, TAPS - 1:]
        s_st = sb("s_st", [P, L], F32R)
        b_rep, c_rep = sb("b_rep", [P, 2, L]), sb("c_rep", [P, 2, L])
        sel = sb("sel", [P, 4, P], F32R)
        dA = sb("dA", [P, 2, L])
        wt = sb("wt", [P, 2, L])
        bst, mv = sb("bst", [P, LC, 6]), sb("mv", [P, LC, 2])
        st = sb("st", [P, 8, LC])
        mx = sb("mx", [P, LC])
        pad = sb("pad", [P, 16])
        sc = sb("sc", [P, LC, NE + 2])
        rep = xt[:, 0, 0:LC * (NE + 2)].rearrange("p (c n) -> p c n", c=LC)
        m8 = sb("m8", [P, LC, 8])
        wd = xt[:, 1, 0:LC * NE].rearrange("p (c n) -> p c n", c=LC)
        flat = tt[:, 0, 0:LC * NE].rearrange("p (g k) -> p g k", k=NK)
        fz = tt[:, 1, 0:LC * NE].rearrange("p (g k) -> p g k", k=NK)
        g1, g2 = sb("g1", [P, LC * NF]), sb("g2", [P, LC * NF])
        soft2 = wr_c[:].rearrange("p (c a n) -> p c a n", c=LC, a=2)
        wdT = aw[0:NE, :]
        scal = sb("scal", [P, LC, NF])

        def bank(name):
            return ctx.enter_context(nc.psum_tensor(name, [P, 512], F32))

        b_q, b_g0, b_u0, b_g1, b_u1, b_d0, b_d1, b_s = [bank("b_" + n) for n in
                                                         ("q", "g0", "u0", "g1", "u1", "d0", "d1", "s")]
        bg, bu, bd = [b_g0, b_g1, b_g0], [b_u0, b_u1, b_u0], [b_d0, b_d1, b_g0, b_u0]
        bx = [b_d0, b_d1, b_g1, b_u1]
        four = [b_g0, b_u0, b_g1, b_u1]

        ident = cs[:, C_ID:C_ID + P]

        dma_cst, dma_gu, dma_d, dma_r, dma_x, dma_ctx = (
            sem(n) for n in ("dma_cst", "dma_gu", "dma_d", "dma_r", "dma_x", "dma_ctx"))
        dma_x0, dma_out = (sem(n) for n in ("dma_x0", "dma_out"))
        set_dve, set_act = (
            sem(n) for n in ("set_dve", "set_act"))
        pool_scale_d, act_hi_d, lo_of_d, pool_scale_r, act_hi_r, dve_lo_r = (
            sem(n) for n in ("pool_scale_d", "act_hi_d", "lo_of_d", "pool_scale_r", "act_hi_r", "dve_lo_r"))
        act_hi_gu, pool_lo_g, pool_lo_u, act_mu, act_rsel = (
            sem(n) for n in ("act_hi_gu", "pool_lo_g", "pool_lo_u", "act_mu", "act_rsel"))
        dve_mu = sem("dve_mu")
        pe_qa, pe_gu, pe_wr, pe_xe, pe_dqa, pe_dn = (
            sem(n) for n in ("pe_qa", "pe_gu", "pe_wr", "pe_xe", "pe_dqa", "pe_dn"))
        pe_rep, act_ws, dve_ws, act_wrc, dve_xt, act_xe = (
            sem(n) for n in ("pe_rep", "act_ws", "dve_ws", "act_wrc", "dve_xt", "act_xe"))
        dve_xe, dve_aw, act_aw, dve_awl, act_daw, dve_daw = (
            sem(n) for n in ("dve_xe", "dve_aw", "act_aw", "dve_awl", "act_daw", "dve_daw"))
        act_tanh, dve_g2, dve_h, act_hh, dve_hl, dve_dn = (
            sem(n) for n in ("act_tanh", "dve_g2", "dve_h", "act_hh", "dve_hl", "dve_dn"))
        dve_sel, act_rep, act_da, pool_dbu, dve_scan, dve_p = (
            sem(n) for n in ("dve_sel", "act_rep", "act_da", "pool_dbu", "dve_scan", "dve_p"))
        y_added = sem("y_added")
        act_hi_in, dve_lo_in, act_hi_x, pool_lo_x, act_d_u = (
            sem(n) for n in ("act_hi_in", "dve_lo_in", "act_hi_x", "pool_lo_x", "act_d_u"))
        act_ctx, pool_ctx, pe_in, act_xs, dve_cv, act_tc = (
            sem(n) for n in ("act_ctx", "pool_ctx", "pe_in", "act_xs", "dve_cv", "act_tc"))
        act_cv = sem("act_cv")
        dve_u, act_u, pool_ul, pe_xd, act_rnd, act_s = (
            sem(n) for n in ("dve_u", "act_u", "pool_ul", "pe_xd", "act_rnd", "act_s"))
        dve_s, pe_dt, act_abs, act_relu, act_ev, dve_w = (
            sem(n) for n in ("dve_s", "pe_dt", "act_abs", "act_relu", "act_ev", "dve_w"))
        act_ln, dve_y = (
            sem(n) for n in ("act_ln", "dve_y"))
        dve_stat, act_sqrt, dve_zh, act_tz, dve_z, dve_y3 = (
            sem(n) for n in ("dve_stat", "act_sqrt", "dve_zh", "act_tz", "dve_z", "dve_y3"))
        pe_yt, dve_x1, act_x1 = (
            sem(n) for n in ("pe_yt", "dve_x1", "act_x1"))
        dve_xn, pe_xnT, act_xnT, pe_lg = (
            sem(n) for n in ("dve_xn", "pe_xnT", "act_xnT", "pe_lg"))
        dve_rt, act_ex, pe_wdT, act_wdT, pe_fl, dve_ft = (
            sem(n) for n in ("dve_rt", "act_ex", "pe_wdT", "act_wdT", "pe_fl", "dve_ft"))
        act_fe, pe_sT, act_sr, act_sT, dve_sT = (
            sem(n) for n in ("act_fe", "pe_sT", "act_sr", "act_sT", "dve_sT"))

        def a_(b, e):
            return NX * b + e

        def r_(b, e):
            return NF * b + e

        def x_(b, e):
            return (NF + 1) * b + e

        def d_loaded(b, e):
            return 11 * b + 2 + e + (0 if isinstance(b, int) and b == B - 1 else 1)

        def pre_loaded(nb):
            return 1 if isinstance(nb, int) and nb == 0 else 11 * (nb - 1) + 2

        PRIME, PRIME_Y = 2, 4

        def ssm_tile(nb, e, j):
            return 64 * nb + 8 * e + j

        def ssm_rep(nb, e, k):
            return 32 * nb + 4 * e + k

        def col(t, i, n=1):
            return t[:, bass.ds(i, n)] if not isinstance(i, int) else t[:, i:i + n]

        ROUTE_STEPS, FLAT_STEPS, STAT_STEPS = 17, 11, 17
        SETUP_DVE = 9
        ctx_h, ctx_l = [aw_h, daw_s], [aw_l, ws]
        u_h = [hh[:, 0, :], hh[:, 1, :], hh[:, 2, :], daw_s[:]]
        u_l = [hl[:, 0, :], hl[:, 1, :], hl[:, 2, :], s_st[:]]
        w_e = [wt, dA]
        z_0 = x1[:]
        bt = [b_q, b_s]
        b_dt = [b_g1, b_u1, b_d0, b_d1]


        ring = [wt[:, 0, :], wt[:, 1, :]]
        ring_0 = ring + [xt[:, 0, :], xt[:, 1, :]]

        def three(w_h, w_l, v_h, v_l):
            return ((w_h, v_h), (w_h, v_l), (w_l, v_h))

        block = ctx.enter_context(nc.Block())

        @block.sync
        def _(sp):
            def load_gu(e):
                sp.dma_start(raw_gu[:], gu[e] if isinstance(e, int) else gu[bass.ds(e, 1)]
                             .rearrange("a p n -> (a p) n")).then_inc(dma_gu, 16)

            def load_d(e):
                sp.dma_start(raw_d[:], dd[e] if isinstance(e, int) else dd[bass.ds(e, 1)]
                             .rearrange("a p n -> (a p) n")).then_inc(dma_d, 16)

            def load_r(e):
                sp.dma_start(raw_r[:], rr[e] if isinstance(e, int) else rr[bass.ds(e, 1)]
                             .rearrange("a p n -> (a p) n")).then_inc(dma_r, 16)

            def load_pre():
                sp.dma_start(raw_d[:, 0:PRE_ALL], pre).then_inc(dma_d, 16)

            def of_batch(t, b):
                return t[b] if isinstance(b, int) else t[bass.ds(b, 1)].rearrange("a p n -> (a p) n")

            def load_x(b):
                src = x[b] if isinstance(b, int) else x[bass.ds(b, 1)].rearrange("a l h -> (a l) h")
                sp.dma_start(xu[:], src.rearrange("(c p) h -> p c h", p=P)).then_inc(dma_x, 16)

            def load_ctx(b):
                sp.wait_ge(dve_scan, PRIME + 64 * b)
                sp.dma_start(dA[:], of_batch(ctxT, b)).then_inc(dma_ctx, 16)

            def next_d(b, e, after):
                sp.wait_ge(lo_of_d, a_(b, e) + 1)
                if isinstance(e, int) and e == NX - 1:
                    if after == "pre":
                        load_pre()
                    elif after == "experts":
                        load_d(0)
                else:
                    load_d(e + 1)

            def first_d_and_x(nb):
                sp.wait_ge(pool_lo_x, nb + 1)
                sp.wait_ge(dve_lo_in, nb + 1)
                load_d(0)
                sp.wait_ge(act_d_u, HC * (nb + 1))
                sp.wait_ge(dve_y, nb + 1)
                load_x(nb)

            def next_r(b, e, to):
                sp.wait_ge(dve_lo_r, r_(b, e) + 2)
                sp.wait_ge(dve_mu, r_(b, e) + 2)
                sp.wait_ge(act_rsel, r_(b, e) + 2)
                load_r(to)

            def next_gu(b, e, to):
                sp.wait_ge(pool_lo_u, a_(b, e) + 2)
                load_gu(to)

            sp.dma_start(cs[:], cst).then_inc(dma_cst, 16)
            sp.dma_start(inv_i[:], inv.partition_broadcast(NE)).then_inc(dma_cst, 16)
            sp.dma_start(dA[:], ctxT[0]).then_inc(dma_ctx, 16)
            load_pre()
            sp.dma_start(x1[:], x[0].rearrange("(c p) h -> p c h", p=P)).then_inc(dma_x0, 16)
            load_gu(0)
            load_r(0)
            sp.wait_ge(pool_lo_x, 1)
            sp.wait_ge(dve_lo_in, 1)
            load_pre()
            sp.wait_ge(dve_y, 1)
            sp.wait_ge(act_d_u, HC)
            load_x(0)
            load_ctx(1)
            sp.wait_ge(dve_lo_r, 1)
            sp.wait_ge(dve_mu, 1)
            sp.wait_ge(act_rsel, 1)
            load_r(1)
            sp.wait_ge(pool_lo_u, 1)
            load_gu(1)

            first_d_and_x(1)

            def batch(b, after):
                last = after is None
                with sp.Fori(0, NF - 2) as e:
                    next_d(b, e, after)
                    next_r(b, e, e + 2)
                    next_gu(b, e, e + 2)
                for e in range(NF - 2, NX):
                    next_d(b, e, after)
                    if e < NF and not last:
                        next_r(b, e, e + 2 - NF)
                    if e == NF - 1 and after == "pre":
                        load_ctx(b + 2)
                    if e + 2 < NX:
                        next_gu(b, e, e + 2)
                    elif not last:
                        next_gu(b, e, e + 2 - NX)
                sp.wait_ge(dve_dn, LC * NX * (b + 1) + 1)
                dst = out[b] if isinstance(b, int) else out[bass.ds(b, 1)].rearrange("a l h -> (a l) h")
                sp.dma_start(dst.rearrange("(c p) h -> p c h", p=P), x1[:]).then_inc(dma_out, 16)
                if after == "pre":
                    first_d_and_x(b + 2)

            with sp.Fori(0, B - 2) as b:
                batch(b, "pre")
            batch(B - 2, "experts")
            batch(B - 1, None)
            sp.wait_ge(dma_out, 16 * (B + 1))

        @block.tensor
        def _(pe):
            mm = nc.tensor.matmul

            def replicate(nb, e, k):
                pe.wait_ge(dve_sel, ssm_rep(nb, e, k) + 1)
                pe.wait_ge(act_rep, ssm_rep(nb, e, k) + 1)
                mm(b_s[:], sel[:, k, :], s_st[:], start=True, stop=True).then_inc(pe_rep, 1)

            def in_proj(nb):
                pe.wait_ge(pool_ctx, 2 * (nb + 1))
                pe.wait_ge(dve_lo_in, nb + 1)
                if isinstance(nb, int):
                    if nb == 1:
                        pe.wait_ge(dve_y3, 1)
                else:
                    pe.wait_ge(dve_dn, LC * NX * (nb - 1) + 1)
                for m in range(HC):
                    n = 0
                    for c in range(DM // P):
                        o = PRE_IN + c * H + m * P
                        for w, v in three(d_h[:, o:o + P], d_l[:, o:o + P], ctx_h[c][:], ctx_l[c][:]):
                            i = mm(four[m][:], w, v, start=(n == 0), stop=(n == 5))
                            n += 1
                    i.then_inc(pe_in, 1)

            def x_proj(nb):
                pe.wait_ge(pool_lo_x, nb + 1)
                n = 0
                for c in range(HC):
                    pe.wait_ge(pool_ul, HC * nb + c + 1)
                    o = PRE_XP + c * P
                    for w, v in three(d_h[:, o:o + P], d_l[:, o:o + P], u_h[c], u_l[c]):
                        i = mm(b_s[:], w, v, start=(n == 0), stop=(n == 11))
                        n += 1
                i.then_inc(pe_xd, 1)

            def dt_proj(nb):
                pe.wait_ge(dve_s, nb + 1)
                for m in range(HC):
                    o = PRE_DT + m * P
                    mm(b_dt[m][:], d_h[:, o:o + P], s_st[:], start=True, stop=False)
                    mm(b_dt[m][:], d_l[0:DR, o:o + P], s_st[0:DR, :], start=False, stop=True).then_inc(pe_dt, 1)

            def y_transposed(b, lcs):
                pe.wait_ge(dve_y3, b + 1)
                for lc in lcs:
                    if lc >= 2:
                        pe.wait_ge(dve_x1, LC * b + lc - 1)
                    for dc in range(HC):
                        i = nc.tensor.transpose(bt[lc % 2][:, dc * P:(dc + 1) * P], du[:, dc, lc * P:(lc + 1) * P],
                                                ident)
                    i.then_inc(pe_yt, 1)

            def xn_transposed(b, hcs):
                pe.wait_ge(dve_xn, LC * (b + 1))
                for hc in hcs:
                    if hc >= 2:
                        pe.wait_ge(act_xnT, HC * b + hc - 1)
                    for tc in range(LC):
                        i = nc.tensor.transpose(bt[hc % 2][:, tc * P:(tc + 1) * P],
                                                delta[:, tc, hc * P:(hc + 1) * P], ident)
                    i.then_inc(pe_xnT, 1)

            def logits(b):
                pe.wait_ge(act_xnT, HC * (b + 1))
                for tc in range(LC):
                    for c in range(HC):
                        i = mm(b_q[:, tc * NE:(tc + 1) * NE], xnT[:, c, tc * P:(tc + 1) * P], gw[:, c, :],
                               start=(c == 0), stop=(c == HC - 1))
                i.then_inc(pe_lg, 1)

            def weights_transposed(b):
                pe.wait_ge(dve_rt, ROUTE_STEPS * (b + 1))
                for tc in range(LC):
                    i = mm(b_s[0:NE, tc * P:(tc + 1) * P], wd[:, tc, :], ident, start=True, stop=True)
                i.then_inc(pe_wdT, 1)

            def places(b):
                pe.wait_ge(act_wdT, b + 1)
                for tc in range(LC):
                    i = mm(b_q[:, tc * NE:(tc + 1) * NE], wdT[:, tc * P:(tc + 1) * P], pm[:], start=True, stop=True)
                i.then_inc(pe_fl, 1)

            def soft_transposed(b):
                pe.wait_ge(dve_ft, FLAT_STEPS * (b + 1))
                for tc in range(LC):
                    i = nc.tensor.transpose(b_s[:, tc * P:(tc + 1) * P],
                                            soft2[:, tc, :, :].rearrange("p a k -> p (a k)"), ident)
                i.then_inc(pe_sT, 1)
                pe.wait_ge(dve_sT, b + 1)
                pe.wait_ge(act_sT, b + 1)

            def wrep(r):
                pe.wait_ge(act_rsel, r + 1)
                mm(b_q[:], r_sel[:], soft_s[:], start=True, stop=True).then_inc(pe_wr, 1)

            def delta_xe(r, dn_before, h_before):
                pe.wait_ge(dve_mu, r + 1)
                pe.wait_ge(dve_ws, r + 1)
                pe.wait_ge(act_ws, r + 1)
                pe.wait_ge(dve_dn, dn_before)
                for c in range(HC):
                    if c == 2 and h_before is not None:
                        pe.wait_ge(*h_before)
                    mm(bx[c][:], mu[:, c * P:(c + 1) * P], ws[:], start=True, stop=True).then_inc(pe_xe, 1)

            def body(b, e, last, routed, nxt, ssm, start=False, proj=False, late=False):
                a, r = a_(b, e), (r_(b, e) if routed else None)
                xi = x_(b, e if routed else NF)
                if late:
                    replicate(b + 1, e, 0)
                if routed:
                    pe.wait_ge(dve_lo_r, r + 1)
                    n = 0
                    for c in range(HC):
                        pe.wait_ge(dve_xe, HC * xi + c + 1)
                        o = R_QA + c * P
                        for w, v in three(r_h[:, o:o + P], r_l[:, o:o + P], xe_h[:, c, :], xe_l[:, c, :]):
                            i = mm(b_q[:], w, v, start=(n == 0), stop=(n == 11))
                            n += 1
                    i.then_inc(pe_qa, 1)
                else:
                    pe.wait_ge(dve_xe, HC * xi + HC)
                for m in range(IC):
                    if m == 0:
                        pe.wait_ge(dve_dn, LC * a + 1)
                    if m == 1 and proj:
                        pe.wait_ge(act_relu, HC * (b + 1) + 2)
                    if m == 2:
                        pe.wait_ge(dve_h, IC * a + 1)
                    for j, out_b in ((0, bg[m]), (1, bu[m])):
                        if m == 0:
                            pe.wait_ge((pool_lo_g, pool_lo_u)[j], a + 1)
                        n = 0
                        for c in range(HC):
                            cols = slice(m * P, m * P + IW[m])
                            for w, v in three(gu_h[:, j, c, cols], gu_l[:, j, c, cols], xe_h[:, c, :], xe_l[:, c, :]):
                                i = mm(out_b[0:IW[m], :], w, v, start=(n == 0), stop=(n == 11 and not routed))
                                n += 1
                        if m == 0 and proj:
                            (x_proj, dt_proj)[j](b + 1)
                        if m == 0 and late and j == 0:
                            replicate(b + 1, e, 1)
                    if proj:
                        replicate(b + 1, e, m)
                    elif m < 2 and ssm:
                        replicate(b + 1, e, 2 + m)
                    if routed:
                        if m == 0:
                            pe.wait_ge(dve_awl, r + 1)
                        cols = slice(R_QB + m * P, R_QB + m * P + IW[m])
                        for k, (w, v) in enumerate(((r_h, aw_h), (r_h, aw_l), (r_l, aw_h))):
                            for j, out_b in ((0, bg[m]), (1, bu[m])):
                                rows = slice(j * HALF, (j + 1) * HALF)
                                i = mm(out_b[0:IW[m], :], w[rows, cols], v[rows, :], start=False, stop=(k == 2))
                    i.then_inc(pe_gu, 1)
                    if m == 1 and nxt:
                        wrep(r + 1)
                    if m == IC - 1 and proj:
                        pe.wait_ge(act_relu, HC * (b + 2))
                    if m == IC - 1 and nxt:
                        delta_xe(r + 1, LC * a + 1, (dve_h, IC * a + 2))
                    if start and e == NF and m > 0:
                        y_transposed(b + 1, (2 * m - 2, 2 * m - 1))
                    if start and e == NX - 1:
                        if m < IC - 1:
                            xn_transposed(b + 1, (2 * m, 2 * m + 1))
                        else:
                            logits(b + 1)
                def adapter_a(m):
                    pe.wait_ge(dve_hl, IC * a + m + 1)
                    k = slice(0, IW[m])
                    o = D_QA + m * P
                    n = 3 * m
                    for w, v in three(d_h[k, o:o + P], d_l[k, o:o + P], hh[k, m, :], hl[k, m, :]):
                        i = mm(b_q[:], w, v, start=(n == 0), stop=(n == 8))
                        n += 1
                    if m == IC - 1:
                        i.then_inc(pe_dqa, 1)

                def down(tc, ms=range(IC)):
                    t = slice(tc * P, (tc + 1) * P)
                    for m in ms:
                        n = 3 * m
                        k = slice(0, IW[m])
                        o = D_W + m * H
                        for v, w in ((hh, d_h), (hl, d_h), (hh, d_l)):
                            i = mm(bd[tc][:], v[k, m, t], w[k, o:o + H], start=(n == 0),
                                   stop=(n == 8 and not routed))
                            n += 1
                        if m == IC - 1 and not routed:
                            i.then_inc(pe_dn, 1)

                def adapter_b(tc):
                    t = slice(tc * P, (tc + 1) * P)
                    mm(bd[tc][:], daw_s[:, t], d_h[:, D_QB:D_QB + H], start=False, stop=False)
                    mm(bd[tc][:], daw_s[0:HALF, t], d_l[0:HALF, D_QB:D_QB + H],
                       start=False, stop=True).then_inc(pe_dn, 1)

                pe.wait_ge(lo_of_d, a_(b, e) + 1)
                if routed:
                    adapter_a(0)
                    adapter_a(1)
                    if nxt:
                        pe.wait_ge(dve_xt, HC * (r + 1) + 1)
                    down(0, range(IC - 1))
                    if nxt:
                        pe.wait_ge(dve_xt, HC * (r + 1) + 2)
                    down(1, range(IC - 1))
                    adapter_a(IC - 1)
                    down(0, [IC - 1])
                    down(1, [IC - 1])
                    down(2)
                    if proj:
                        replicate(b + 1, e, 3)
                    elif nxt and ssm:
                        replicate(b + 1, e + 1, 0)
                    pe.wait_ge(dve_daw, r + 2)
                    pe.wait_ge(act_daw, 2 * r + 2)
                    for tc in range(3):
                        adapter_b(tc)
                    down(3)
                    adapter_b(3)
                    if nxt and ssm and not proj:
                        replicate(b + 1, e + 1, 1)
                else:
                    pe.wait_ge(dve_hl, IC * a + IC - 1)
                    down(0, range(IC - 1))
                    down(1, range(IC - 1))
                    pe.wait_ge(dve_hl, IC * a + IC)
                    down(0, [IC - 1])
                    down(1, [IC - 1])
                    down(2)
                    if start and e == NX - 1:
                        weights_transposed(b + 1)
                    down(3)

            pe.wait_ge(set_dve, SETUP_DVE)
            in_proj(0)
            x_proj(0)
            dt_proj(0)
            replicate(0, 0, 0)
            replicate(0, 0, 1)
            pe.wait_ge(dve_y, 1)
            pe.wait_ge(act_d_u, HC)
            for dc in range(HC):
                mm(four[dc][:], ident, y[:, dc, :], start=True, stop=False, skip_group_check=True)

            def sum_states(e, stop):
                for j in range(8):
                    if j == 0:
                        replicate(0, e, 2)
                        replicate(0, e, 3)
                    elif j == 4 and not stop:
                        replicate(0, e + 1, 0)
                        replicate(0, e + 1, 1)
                    pe.wait_ge(dve_p, ssm_tile(0, e, j) + 9)
                    mm(four[j % 4][:], ident, ring_0[j % 4], start=False, stop=(stop and j >= 4),
                       skip_group_check=True).then_inc(y_added, 1)

            with pe.Fori(0, NF - 1) as e:
                sum_states(e, False)
            sum_states(NF - 1, True)

            def bridge(b, pre):
                places(b)
                if pre:
                    in_proj(b + 1)
                soft_transposed(b)
                wrep(r_(b, 0))
                delta_xe(r_(b, 0), LC * a_(b, 0) + 1, (act_cv, HC * (b + 2)) if pre else None)

            def batch(b, last, ssm, proj):
                body(b, 0, last, True, True, ssm, proj=proj)
                body(b, 1, last, True, True, ssm, late=proj)
                with pe.Fori(2, NF - 1) as e:
                    body(b, e, last, True, True, ssm)
                body(b, NF - 1, last, True, False, ssm)
                body(b, NF, last, False, False, False, not last)
                body(b, NF + 1, last, False, False, False, not last)

            y_transposed(0, range(LC))
            xn_transposed(0, range(HC))
            logits(0)
            weights_transposed(0)
            bridge(0, True)
            with pe.Fori(0, B - 2) as b:
                batch(b, False, True, True)
                bridge(b + 1, True)
            batch(B - 2, False, True, True)
            bridge(B - 1, False)
            batch(B - 1, True, False, False)

        @block.scalar
        def _(act):
            def f(out_, in_, func, **k):
                return nc.scalar.activation(out_, in_, func, **k)

            def rounded(out_, in_):
                return f(out_, in_, ACT.Copy)

            def split_d(loaded, routed, pe_ready, r=None):
                act.wait_ge(dma_d, 16 * loaded)
                if r is not None:
                    act.wait_ge(pool_scale_d, r + 1)
                for s_, v in pe_ready:
                    act.wait_ge(s_, v)
                n = D_SPLIT if routed else IC * H
                rounded(d_h[:, 0:n], raw_d[:, 0:n]).then_inc(act_hi_d, 1)

            def mu_conv(k, first):
                act.wait_ge(dma_r, 16 * (k + 1))
                if not first:
                    act.wait_ge(dve_daw, k)
                raw = raw_r[:, R_MU:R_MU + H]
                rounded(rnd[:], raw).then_inc(act_mu, 1)
                act.wait_ge(act_mu, 2 * k + 1)
                f(raw, raw, ACT.Copy, scale=cs[:, C_MB:C_MB + 1]).then_inc(act_mu, 1)
                if not first:
                    act.wait_ge(pe_wr, k)
                rounded(r_sel[:], raw_r[:, R_SEL:R_SEL + P]).then_inc(act_rsel, 1)

            def split_r(k, a_done):
                act.wait_ge(pool_scale_r, k + 1)
                if a_done is not None:
                    act.wait_ge(pe_gu, a_done)
                rounded(r_h[:], raw_r[:, 0:R_SPLIT]).then_inc(act_hi_r, 1)

            def split_gu(k, a_done, js=range(2)):
                act.wait_ge(dma_gu, 16 * (k + 1))
                if a_done is not None:
                    act.wait_ge(pe_gu, a_done)
                for j in js:
                    rounded(gu_h[:, j], raw_gu[:, j * HC * I:(j + 1) * HC * I].rearrange("p (c i) -> p c i", c=HC)
                            ).then_inc(act_hi_gu, 1)

            def rep_copy(nb, e, k):
                act.wait_ge(pe_rep, ssm_rep(nb, e, k) + 1)
                n = 16 * nb + 2 * e + k // 2
                if k % 2 == 0:
                    act.wait_ge(pool_dbu, 4 * n + 4)
                    dst = b_rep[:, k // 2, :]
                else:
                    act.wait_ge(dve_p, 4 * n + 4)
                    dst = c_rep[:, k // 2, :]
                f(dst, b_s[:], ACT.Copy).then_inc(act_rep, 1)

            def exp_tile(nb, e, j):
                t = ssm_tile(nb, e, j)
                if j == 0:
                    act.wait_ge(dve_y, nb + 1)
                act.wait_ge(dve_scan, t + 1)
                dc, k = j % 4, j // 4
                f(dA[:, j % 2, :], delta[:, dc, :], ACT.Exp,
                  scale=col(a_neg, 2 * e + (dc * NS + k))).then_inc(act_da, 1)

            def wr_copy(r):
                act.wait_ge(pe_wr, r + 1)
                act.wait_ge(dve_mu, r + 1)
                f(wr_n[:], b_q[:], ACT.Copy).then_inc(act_ws, 1)
                rounded(rnd[HALF:P, :], b_q[HALF:P, :]).then_inc(act_ws, 1)
                rounded(ws[0:HALF, :], b_q[0:HALF, :]).then_inc(act_ws, 1)

            def xe_hi(b, e, r, cs_=range(HC)):
                xi = x_(b, e)
                for c in cs_:
                    act.wait_ge(dve_xt, HC * r + c + 1)
                    rounded(xe_h[:, c, :], xt[:, c % 2, :]).then_inc(act_xe, 1)

            def round_ctx(nb):
                act.wait_ge(dma_ctx, 16 * (nb + 1))
                for c in range(DM // P):
                    rounded(ctx_h[c][:], dA[:, c, :]).then_inc(act_ctx, 1)

            def split_pre(nb):
                act.wait_ge(dma_d, 16 * pre_loaded(nb))
                if isinstance(nb, int):
                    if nb == 1:
                        act.wait_ge(pe_dt, HC)
                else:
                    act.wait_ge(pe_dn, LC * NX * (nb - 1) + 1)
                rounded(d_h[:, 0:PRE_XP], raw_d[:, 0:PRE_XP]).then_inc(act_hi_in, 1)
                rounded(d_h[:, PRE_XP:PRE_ALL], raw_d[:, PRE_XP:PRE_ALL]).then_inc(act_hi_x, 1)

            def in_proj(nb):
                if not (isinstance(nb, int) and nb == 0):
                    act.wait_ge(dve_y3, nb)
                for m in range(HC):
                    act.wait_ge(pe_in, HC * nb + m + 1)
                    f(y[:, m, :], four[m][:], ACT.Copy).then_inc(act_xs, 1)
                    f(delta[:, m, :], four[m][:], ACT.Identity, bias=cbh[:, m:m + 1],
                      scale=cwh[:, m * TAPS + TAPS - 1:m * TAPS + TAPS]).then_inc(act_cv, 1)

            def conv_tanh(nb, ms=range(HC)):
                for m in ms:
                    act.wait_ge(dve_cv, 12 * nb + 6 * (m // 2) + 4 + m % 2 + 1)
                    f(du[:, m, :], delta[:, m, :], ACT.Tanh).then_inc(act_tc, 1)

            def u_hi(nb, ms=range(HC)):
                for m in ms:
                    act.wait_ge(dve_u, HC * nb + m + 1)
                    rounded(u_h[m], xu[:, m, :]).then_inc(act_u, 1)

            def x_proj(nb):
                act.wait_ge(pe_xd, nb + 1)
                rounded(rnd[HALF:P, :], b_s[HALF:P, :]).then_inc(act_rnd, 1)
                rounded(s_st[0:HALF, :], b_s[0:HALF, :]).then_inc(act_s, 1)
                for m in range(HC):
                    act.wait_ge(pe_dt, HC * nb + m + 1)
                    bias = cs[:, C_DB + m:C_DB + m + 1]
                    f(du[:, m, :], b_dt[m][:], ACT.Abs, bias=bias).then_inc(act_abs, 1)
                    f(delta[:, m, :], b_dt[m][:], ACT.Relu, bias=bias).then_inc(act_relu, 1)

            def exp_abs(nb):
                act.wait_ge(act_abs, HC * (nb + 1))
                f(du[:], du[:], ACT.Exp, scale=-1.0).then_inc(act_ev, 1)

            def log_w(nb):
                for q in range(2):
                    act.wait_ge(dve_w, 8 * nb + q + 1)
                    f(y[:, 2 * q:2 * q + 2, :], w_e[q][:], ACT.Ln).then_inc(act_ln, 1)

            def d_u(nb):
                for m in range(HC):
                    act.wait_ge(dve_w, 8 * nb + 4 + m // 2 + 1)
                    f(y[:, m, :], xu[:, m, :], ACT.Copy, scale=cs[:, C_D + m:C_D + m + 1]).then_inc(act_d_u, 1)

            def root(u):
                act.wait_ge(dve_stat, STAT_STEPS * u + 11)
                f(st[:, 1, :], st[:, 0, :], ACT.Sqrt).then_inc(act_sqrt, 1)

            def tanh_z(b):
                if isinstance(b, int) and b == 0:
                    act.wait_ge(dve_zh, LC)
                    f(z_0, xnT[:], ACT.Tanh).then_inc(act_tz, 1)
                    return
                act.wait_ge(act_da, 64 * (b + 1))
                act.wait_ge(dve_zh, LC * (b + 1))
                f(delta[:], xnT[:], ACT.Tanh).then_inc(act_tz, 1)

            def xnT_copy(b, hcs):
                for hc in hcs:
                    act.wait_ge(pe_xnT, HC * b + hc + 1)
                    f(xnT[:, hc, :], bt[hc % 2][:], ACT.Copy).then_inc(act_xnT, 1)

            def exp_scores(b):
                act.wait_ge(dve_rt, ROUTE_STEPS * b + 2)
                f(sc[:, :, 0:NE], sc[:, :, 0:NE], ACT.Exp).then_inc(act_ex, 1)

            def bridge(b, pre):
                act.wait_ge(pe_wdT, b + 1)
                f(wdT, b_s[0:NE, :], ACT.Copy).then_inc(act_wdT, 1)
                if pre:
                    split_pre(b + 1)
                act.wait_ge(dve_ft, FLAT_STEPS * b + 5)
                f(fz, fz, ACT.Exp).then_inc(act_fe, 1)
                if pre:
                    in_proj(b + 1)
                act.wait_ge(pe_sT, b + 1)
                rounded(rnd[HALF:P, :], b_s[HALF:P, :]).then_inc(act_sr, 1)
                rounded(soft_s[0:HALF, :], b_s[0:HALF, :]).then_inc(act_sT, 1)
                if pre:
                    conv_tanh(b + 1, (0, 1))
                wr_copy(r_(b, 0))
                act.wait_ge(dma_out, 16 * (b + 1))
                act.wait_ge(dve_x1, LC * (b + 1))
                f(x1[:], xu[:], ACT.Copy).then_inc(act_x1, 1)
                if pre:
                    conv_tanh(b + 1, (2, 3))
                    u_hi(b + 1, (0, 1))
                xe_hi(b, 0, r_(b, 0))
                if pre:
                    u_hi(b + 1, (2, 3))

            def body(b, e, last, routed, nxt, ssm, start=False, pre=False, proj=False, late=False):
                a, r = a_(b, e), (r_(b, e) if routed else None)
                more_r = routed and not (last and not nxt)
                if routed:
                    act.wait_ge(act_ws, 3 * (r + 1))
                    f(wr_c[:], wr_n[:], ACT.Copy).then_inc(act_wrc, 1)
                inner = ssm and not proj
                if late:
                    rep_copy(b + 1, e, 0)
                if inner:
                    exp_tile(b + 1, e, 0)
                if routed:
                    act.wait_ge(dve_aw, 2 * r + 1)
                    rounded(aw_h[:], aw[:]).then_inc(act_aw, 1)
                if start and routed:
                    root(2 * (b + 1))
                if late:
                    rep_copy(b + 1, e, 1)
                if inner:
                    exp_tile(b + 1, e, 1)
                if not proj:
                    split_d(d_loaded(b, e), routed, [(pe_dn, LC * a + 1)], r)
                if inner:
                    exp_tile(b + 1, e, 2)
                    rep_copy(b + 1, e, 2)
                if more_r and not proj:
                    mu_conv(r + 1, False)

                def tanh(m):
                    w = IW[m]
                    act.wait_ge(pe_gu, IC * a + m + 1)
                    if m == 2:
                        act.wait_ge(dve_hl, IC * a + 1)
                    f(tt[0:w, m % 2, :], bg[m][0:w, :], ACT.Tanh, scale=0.5).then_inc(act_tanh, 1)

                def h_hi(m):
                    w = IW[m]
                    act.wait_ge(dve_h, IC * a + m + 1)
                    rounded(hh[0:w, m, :], tt[0:w, m % 2, :]).then_inc(act_hh, 1)

                if proj:
                    x_proj(b + 1)
                tanh(0)
                if proj:
                    exp_abs(b + 1)
                    rep_copy(b + 1, e, 0)
                h_hi(0)
                if proj:
                    mu_conv(r + 1, False)
                    log_w(b + 1)
                    split_d(d_loaded(b, e), routed, [(pe_dn, LC * a + 1)], r)
                    rep_copy(b + 1, e, 1)
                if start and e == NX - 1 and pre:
                    round_ctx(b + 2)
                if inner:
                    exp_tile(b + 1, e, 3)
                    rep_copy(b + 1, e, 3)
                if start and e == NX - 1:
                    xnT_copy(b + 1, (0, 1))
                tanh(1)
                if nxt:
                    wr_copy(r + 1)
                if inner:
                    exp_tile(b + 1, e, 4)
                if proj:
                    d_u(b + 1)
                h_hi(1)
                if proj:
                    exp_tile(b + 1, e, 0)
                    exp_tile(b + 1, e, 1)
                if inner:
                    exp_tile(b + 1, e, 5)
                if start and e == NX - 1:
                    xnT_copy(b + 1, (2, 3))
                tanh(2)
                if proj:
                    rep_copy(b + 1, e, 2)
                h_hi(2)
                if start and e == NX - 1:
                    exp_scores(b + 1)
                def next_x(c):
                    if nxt:
                        xe_hi(b, e + 1, r + 1, (c,))
                    elif routed:
                        rounded(xe_h[:, c, :], xnT[:, c, :]).then_inc(act_xe, 1)

                more_gu = not (last and isinstance(e, int) and e == NX - 1)
                if routed:
                    next_x(0)
                if more_gu:
                    split_gu(a + 1, IC * (a + 1), (0,))
                if routed:
                    next_x(1)
                    next_x(2)
                if not nxt and more_gu:
                    split_gu(a + 1, IC * (a + 1), (1,))
                if proj:
                    exp_tile(b + 1, e, 2)
                    exp_tile(b + 1, e, 3)
                if inner:
                    exp_tile(b + 1, e, 6)
                if routed:
                    act.wait_ge(dve_aw, 2 * r + 2)
                    rounded(rnd[HALF:P, :], aw[HALF:P, :]).then_inc(act_daw, 1)
                    rounded(daw_s[0:HALF, :], aw[0:HALF, :]).then_inc(act_daw, 1)
                    next_x(3)
                if inner:
                    exp_tile(b + 1, e, 7)
                if nxt:
                    split_gu(a + 1, IC * (a + 1), (1,))
                if inner and nxt:
                    rep_copy(b + 1, e + 1, 0)
                if more_r:
                    split_r(r + 1, IC * (a + 1))
                if start and e == NF:
                    root(2 * (b + 1) + 1)
                if start and routed:
                    tanh_z(b + 1)
                if inner and nxt:
                    rep_copy(b + 1, e + 1, 1)
                if proj:
                    rep_copy(b + 1, e, 3)
                    for j in range(4, 8):
                        exp_tile(b + 1, e, j)

            act.wait_ge(dma_cst, 32)
            f(a_neg[:], cs[:, C_AL:C_AL + HC * NS], ACT.Exp).then_inc(set_act, 1)
            f(tgx[:], cs[:, C_GX:C_GX + 1], ACT.Tanh).then_inc(set_act, 1)
            f(tgf[:], cs[:, C_GF:C_GF + 1], ACT.Tanh).then_inc(set_act, 1)
            f(pad[:, 4:5], cs[:, 0:1], ACT.Copy).then_inc(act_rep, 1)
            act.wait_ge(set_dve, SETUP_DVE)
            round_ctx(0)
            split_pre(0)
            in_proj(0)
            conv_tanh(0)
            u_hi(0)
            root(0)
            x_proj(0)
            exp_abs(0)
            rep_copy(0, 0, 0)
            tanh_z(0)
            rep_copy(0, 0, 1)
            log_w(0)
            mu_conv(0, True)
            split_r(0, None)
            d_u(0)
            split_gu(0, None)

            def tiles_0(e, more):
                for j in range(8):
                    exp_tile(0, e, j)
                    if j in (1, 2):
                        rep_copy(0, e, j + 1)
                    elif j in (5, 6) and more:
                        rep_copy(0, e + 1, j - 5)

            with act.Fori(0, NF - 1) as e:
                tiles_0(e, True)
            tiles_0(NF - 1, False)

            def batch(b, last, ssm, pre, proj):
                body(b, 0, last, True, True, ssm, proj=proj)
                body(b, 1, last, True, True, ssm, late=proj)
                with act.Fori(2, NF - 1) as e:
                    body(b, e, last, True, True, ssm)
                body(b, NF - 1, last, True, False, ssm, not last)
                body(b, NF, last, False, False, False, not last)
                body(b, NF + 1, last, False, False, False, not last, pre)

            root(1)
            xnT_copy(0, range(HC))
            round_ctx(1)
            exp_scores(0)
            bridge(0, True)
            with act.Fori(0, B - 2) as b:
                batch(b, False, True, True, True)
                bridge(b + 1, True)
            batch(B - 2, False, True, False, True)
            bridge(B - 1, False)
            batch(B - 1, True, False, False, False)

        @block.gpsimd
        def _(pool):
            v = nc.gpsimd

            def lo(out_, raw, hi):
                return v.tensor_tensor(out_, raw, hi.bitcast(F32), ALU.subtract)

            def scale_d(b, e):
                pool.wait_ge(dma_d, 16 * d_loaded(b, e))
                v.tensor_tensor(raw_d[:, D_QB:D_QB + H], raw_d[:, D_QB:D_QB + H], raw_d[:, D_S:D_S + H],
                                ALU.mult).then_inc(pool_scale_d, 1)

            def scale_r(k):
                pool.wait_ge(dma_r, 16 * (k + 1))
                v.tensor_tensor(raw_r[:, R_QB:R_QB + I], raw_r[:, R_QB:R_QB + I], raw_r[:, R_S:R_S + I],
                                ALU.mult).then_inc(pool_scale_r, 1)

            def split_gu(k, js=range(2)):
                for j in js:
                    pool.wait_ge(act_hi_gu, 2 * k + j + 1)
                    lo(gu_l[:, j], raw_gu[:, j * HC * I:(j + 1) * HC * I].rearrange("p (c i) -> p c i", c=HC),
                       gu_h[:, j]).then_inc((pool_lo_g, pool_lo_u)[j], 1)

            def dbu(nb, e, j, ring):
                t = ssm_tile(nb, e, j)
                if j == 0:
                    pool.wait_ge(dve_y, nb + 1)
                if j % 4 == 0:
                    pool.wait_ge(act_rep, ssm_rep(nb, e, j // 2) + 2)
                pool.wait_ge(y_added, PRIME_Y + t + 1 - len(ring))
                v.tensor_tensor(ring[j % len(ring)], du[:, j % 4, :], b_rep[:, j // 4, :], ALU.mult).then_inc(pool_dbu, 1)

            def split_x_dt(nb):
                pool.wait_ge(act_hi_x, nb + 1)
                o = slice(PRE_XP, PRE_ALL)
                lo(d_l[:, o], raw_d[:, o], d_h[:, o]).then_inc(pool_lo_x, 1)

            def u_lo(nb):
                for m in range(HC):
                    pool.wait_ge(act_u, HC * nb + m + 1)
                    v.tensor_tensor(u_l[m], xu[:, m, :], u_h[m].bitcast(F32), ALU.subtract).then_inc(pool_ul, 1)

            def split_ctx(nb):
                for c in range(DM // P):
                    pool.wait_ge(act_ctx, 2 * nb + c + 1)
                    lo(ctx_l[c][:], dA[:, c, :], ctx_h[c][:]).then_inc(pool_ctx, 1)

            def add_y(nb, e, j):
                if j == 0:
                    pool.wait_ge(act_d_u, HC * (nb + 1))
                pool.wait_ge(dve_p, ssm_tile(nb, e, j) + 9)
                yd = y[:, j % 4, :]
                v.tensor_tensor(yd, yd, ring[j % 2], ALU.add).then_inc(y_added, 1)

            def first_tiles(nb):
                dbu(nb, 0, 0, ring)
                dbu(nb, 0, 1, ring)

            def body(b, e, last, routed, nxt, ssm, proj=False):
                a, r = a_(b, e), (r_(b, e) if routed else None)
                more_r = routed and not (last and not nxt)
                if proj:
                    scale_r(r + 1)
                    pool.wait_ge(act_hi_d, a + 1)
                    lo(d_l[:], raw_d[:, 0:D_SPLIT], d_h[:]).then_inc(lo_of_d, 1)
                    first_tiles(b + 1)
                if ssm:
                    for j in range(6):
                        if proj and j in (2, 4):
                            split_gu(a + 1, (j // 2 - 1,))
                        add_y(b + 1, e, j)
                        dbu(b + 1, e, j + 2, ring)
                        if j == 2 and not proj:
                            scale_r(r + 1)
                elif more_r:
                    scale_r(r + 1)
                if nxt:
                    scale_d(b, e + 1)
                if proj:
                    add_y(b + 1, e, 6)
                elif not (last and isinstance(e, int) and e == NX - 1):
                    split_gu(a + 1, (0,))
                    if ssm and nxt:
                        add_y(b + 1, e, 6)
                    split_gu(a + 1, (1,))
                if ssm:
                    if not nxt:
                        add_y(b + 1, e, 6)
                    add_y(b + 1, e, 7)
                    if nxt:
                        dbu(b + 1, e + 1, 0, ring)
                        dbu(b + 1, e + 1, 1, ring)

            v.memset(pad[:, 5:6], 0.0).then_inc(pool_dbu, 8)
            v.memset(pad[:, 6:7], 0.0).then_inc(y_added, PRIME_Y)
            split_ctx(0)
            split_x_dt(0)
            u_lo(0)
            scale_r(0)
            with pool.Fori(0, NF) as e:
                for j in range(8):
                    dbu(0, e, j, ring_0)

            def batch(b, last, ssm, pre, proj):
                body(b, 0, last, True, True, ssm, proj=proj)
                with pool.Fori(1, NF - 1) as e:
                    body(b, e, last, True, True, ssm)
                body(b, NF - 1, last, True, False, ssm)
                body(b, NF, last, False, False, False)
                if pre:
                    split_ctx(b + 2)
                body(b, NF + 1, last, False, False, False)
                if pre:
                    split_x_dt(b + 2)
                    u_lo(b + 2)
                if not last:
                    scale_d(b + 1, 0)

            split_gu(0)
            split_ctx(1)
            split_x_dt(1)
            u_lo(1)
            scale_d(0, 0)
            with pool.Fori(0, B - 2) as b:
                batch(b, False, True, True, True)
            batch(B - 2, False, True, False, True)
            batch(B - 1, True, False, False, False)

        @block.vector
        def _(dve):
            v = nc.vector
            tt_ = v.tensor_tensor

            def stt(out_, a, s_, b_, op0, op1):
                return v.scalar_tensor_tensor(out=out_, in0=a, scalar=s_, in1=b_, op0=op0, op1=op1)

            def lo(out_, whole, hi):
                return tt_(out_, whole, hi.bitcast(F32), ALU.subtract)

            def chain(s_, base):
                done = [0]

                def step(ins, wait=True):
                    done[0] += 1
                    ins.then_inc(s_, 1)
                    if wait:
                        dve.wait_ge(s_, base + done[0])
                return step

            def carrier(k):
                return v.memset(pad[:, 12 + k:13 + k], 0.0)

            def selectors(nb, e, ks):
                for k in ks:
                    v.tensor_scalar(sel[:, k, :], ones[:], col(cs, 2 * e + (C_E + (k % 2) * NS + k // 2)), None,
                                    ALU.mult).then_inc(dve_sel, 1)

            def tile(nb, e, j, ring):
                t = ssm_tile(nb, e, j)
                w = ring[j % len(ring)]
                dve.wait_ge(act_da, t + 1)
                dve.wait_ge(pool_dbu, t + 9)
                v.tensor_tensor_scan(w, dA[:, j % 2, :], w, 0.0, ALU.mult, ALU.add).then_inc(dve_scan, 1)
                if j % 4 == 0:
                    dve.wait_ge(act_rep, ssm_rep(nb, e, j // 2 + 1) + 2)
                dve.wait_ge(dve_scan, t + 3)
                tt_(w, w, c_rep[:, j // 4, :], ALU.mult).then_inc(dve_p, 1)

            def stats(u, src, half):
                row_sums(u, src)
                scales(u, half)

            def row_sums(u, src):
                step = chain(dve_stat, STAT_STEPS * u)
                step(carrier(0), False)
                for c in range(LC):
                    step(v.bn_stats(bst[:, c, :], src[:, c, :]), c == LC - 1)

            def scales(u, half):
                step = chain(dve_stat, STAT_STEPS * u + 1 + LC)
                step(carrier(1), False)
                for c in range(LC):
                    step(v.bn_aggr(mv[:, c, :], bst[:, c, :]), c == LC - 1)
                step(v.tensor_scalar(st[:, 0, :], mv[:, :, 1], EPS, None, ALU.add))
                dve.wait_ge(act_sqrt, u + 1)
                step(v.reciprocal(st[:, 2, :], st[:, 1, :]))
                step(tt_(st[:, 3, :], st[:, 0, :], st[:, 2, :], ALU.mult))
                step(tt_(st[:, 4, :], st[:, 1, :], st[:, 3, :], ALU.add))
                step(v.reciprocal(st[:, 5, :], st[:, 4, :]))
                step(v.tensor_scalar(st[:, 6, :], st[:, 5, :], 1.0 if half else 2.0, None, ALU.mult))
                step(stt(st[:, 7, :], mv[:, :, 0], -1.0, st[:, 6, :], ALU.mult, ALU.mult))

            def normed(dst, src, c):
                return v.tensor_scalar(dst[:, c, :], src[:, c, :], st[:, 6, c:c + 1], st[:, 7, c:c + 1],
                                       ALU.mult, ALU.add)

            def split_in(nb):
                dve.wait_ge(act_hi_in, nb + 1)
                lo(d_l[:, 0:PRE_XP], raw_d[:, 0:PRE_XP], d_h[:, 0:PRE_XP]).then_inc(dve_lo_in, 1)

            def conv(nb, pairs=range(HC // 2)):
                for pair in pairs:
                    for j in range(TAPS - 1):
                        k = TAPS - 2 - j
                        for m in (2 * pair, 2 * pair + 1):
                            w = cwh[:, m * TAPS + k:m * TAPS + k + 1]
                            src = yx[:, m, k:k + L]
                            if j == 0:
                                dve.wait_ge(act_cv, HC * nb + m + 1)
                                dve.wait_ge(act_xs, HC * nb + m + 1)
                            else:
                                dve.wait_ge(dve_cv, 12 * nb + 6 * pair + 2 * (j - 1) + m % 2 + 1)
                            stt(delta[:, m, :], src, w, delta[:, m, :], ALU.mult, ALU.add).then_inc(dve_cv, 1)

            def make_u(nb, ms=range(HC)):
                if not (isinstance(nb, int) and nb == 0):
                    dve.wait_ge(act_x1, nb)
                for m in ms:
                    dve.wait_ge(act_tc, HC * nb + m + 1)
                    stt(xu[:, m, :], du[:, m, :], 1.0, delta[:, m, :], ALU.add, ALU.mult).then_inc(dve_u, 1)

            def lo_state(nb):
                dve.wait_ge(act_rnd, nb + 1)
                dve.wait_ge(act_s, nb + 1)
                lo(s_st[HALF:P, :], b_s[HALF:P, :], rnd[HALF:P, :]).then_inc(dve_s, 1)

            def one_plus(nb):
                dve.wait_ge(act_ev, nb + 1)
                for q in range(2):
                    v.tensor_scalar(w_e[q][:], du[:, 2 * q:2 * q + 2, :], 1.0, None, ALU.add).then_inc(dve_w, 1)

            half = [slice(0, 2), slice(2, 4)]

            def rest_of_w(nb):
                for q in range(2):
                    dve.wait_ge(act_ln, 2 * nb + q + 1)
                    stt(w_e[q][:], w_e[q][:], 1.0, du[:, half[q], :], ALU.subtract, ALU.subtract).then_inc(dve_w, 1)

            def softplus(nb):
                for q in range(2):
                    dve.wait_ge(dve_w, 8 * nb + 2 + q + 1)
                    tt_(w_e[q][:], y[:, half[q], :], w_e[q][:], ALU.subtract).then_inc(dve_w, 1)
                dve.wait_ge(act_relu, HC * (nb + 1))
                for q in range(2):
                    dve.wait_ge(dve_w, 8 * nb + 4 + q + 1)
                    tt_(delta[:, half[q], :], delta[:, half[q], :], w_e[q][:], ALU.add).then_inc(dve_w, 1)
                dve.wait_ge(dve_w, 8 * nb + 8)
                tt_(du[:], delta[:], xu[:], ALU.mult).then_inc(dve_y, 1)

            def norm_z(b):
                for c in range(LC):
                    normed(xnT, xu, c).then_inc(dve_zh, 1)

            def gate_z(b):
                dve.wait_ge(act_tz, b + 1)
                tanh_half = z_0 if isinstance(b, int) and b == 0 else delta[:]
                stt(xnT[:], tanh_half, 1.0, xnT[:], ALU.add, ALU.mult).then_inc(dve_z, 1)

            def y_gated(b):
                dve.wait_ge(dve_z, b + 1)
                dve.wait_ge(y_added, PRIME_Y + 64 * (b + 1))
                tt_(du[:], y, xnT[:], ALU.mult).then_inc(dve_y3, 1)

            def add_ssm(b, lc):
                dve.wait_ge(pe_yt, LC * b + lc + 1)
                stt(xu[:, lc, :], bt[lc % 2][:], tgx[:], xu[:, lc, :], ALU.mult, ALU.add).then_inc(dve_x1, 1)

            def norm_x1(b):
                for c in range(LC):
                    normed(delta, xu, c).then_inc(dve_xn, 1)

            def route(b):
                step = chain(dve_rt, ROUTE_STEPS * b)
                lg = b_q[:, 0:LC * NE].rearrange("p (c n) -> p c n", c=LC)
                s_ = sc[:, :, 0:NE]
                dve.wait_ge(pe_lg, b + 1)
                step(v.tensor_reduce(mx[:], lg, AX_X, ALU.max))
                step(tt_(s_, lg, mx[:].unsqueeze(2).broadcast_to([P, LC, NE]), ALU.subtract))
                dve.wait_ge(act_ex, b + 1)
                step(v.tensor_reduce(mx[:], s_, AX_X, ALU.add))
                step(v.reciprocal(mx[:], mx[:]))
                step(tt_(s_, s_, mx[:].unsqueeze(2).broadcast_to([P, LC, NE]), ALU.mult))
                step(carrier(2), False)
                for c in range(LC):
                    step(v.max(m8[:, c, :], s_[:, c, :]), c == LC - 1)
                step(v.memset(m8[:, :, TOPK:8], -1.0))
                step(carrier(3), False)
                for c in range(LC):
                    step(v.match_replace(rep[:, c, :], m8[:, c, :], sc[:, c, :], 0.0), c == LC - 1)
                step(tt_(wd, s_, rep[:, :, 0:NE], ALU.subtract))

            def flat_weights(b):
                step = chain(dve_ft, FLAT_STEPS * b)
                dve.wait_ge(pe_fl, b + 1)
                fv = fz.rearrange("p g k -> p (g k)")
                bc = [P, LC * NF, NK]
                step(v.tensor_copy(flat.rearrange("p g k -> p (g k)"), b_q[:, 0:LC * NE]))
                step(v.tensor_scalar(fz, flat, 0.0, -1e9, ALU.is_equal, ALU.mult))
                step(tt_(fz, fz, flat, ALU.add))
                step(v.tensor_reduce(g1[:], fz, AX_X, ALU.max))
                step(tt_(fz, fz, g1[:].unsqueeze(2).broadcast_to(bc), ALU.subtract))
                dve.wait_ge(act_fe, b + 1)
                step(v.tensor_reduce(g1[:], fz, AX_X, ALU.add))
                step(v.reciprocal(g1[:], g1[:]))
                step(v.tensor_reduce(g2[:], flat, AX_X, ALU.add))
                step(v.tensor_scalar(scal[:].rearrange("p c f -> p (c f)"), g2[:], tgf[:], None, ALU.mult))
                step(tt_(fz, fz, g1[:].unsqueeze(2).broadcast_to(bc), ALU.mult))
                step(v.tensor_copy(soft2, fv.rearrange("p (c n) -> p c n", c=LC).unsqueeze(2)
                                   .broadcast_to([P, LC, 2, NE])))

            def lo_soft(b):
                dve.wait_ge(act_sr, b + 1)
                dve.wait_ge(act_sT, b + 1)
                lo(soft_s[HALF:P, :], b_s[HALF:P, :], rnd[HALF:P, :]).then_inc(dve_sT, 1)

            def bridge(b, pre):
                if pre:
                    split_in(b + 1)
                flat_weights(b)
                if pre:
                    conv(b + 1, (0,))
                lo_soft(b)
                if pre:
                    conv(b + 1, (1,))
                ws_lo(r_(b, 0))
                if pre:
                    make_u(b + 1, (0, 1))
                xe_sum(b, 0, r_(b, 0), 0)
                xe(b, 0, r_(b, 0))
                if pre:
                    make_u(b + 1, (2, 3))
                dve.wait_ge(act_x1, b + 1)

            def split_r(k):
                dve.wait_ge(act_hi_r, k + 1)
                lo(r_l[:], raw_r[:, 0:R_SPLIT], r_h[:]).then_inc(dve_lo_r, 1)

            def ws_lo(r):
                dve.wait_ge(act_ws, 3 * r + 3)
                lo(ws[HALF:P, :], b_q[HALF:P, :], rnd[HALF:P, :]).then_inc(dve_ws, 1)

            def split_d(split_count, routed):
                dve.wait_ge(act_hi_d, split_count)
                n = D_SPLIT if routed else IC * H
                lo(d_l[:, 0:n], raw_d[:, 0:n], d_h[:, 0:n]).then_inc(lo_of_d, 1)

            def mask_up(k, first):
                dve.wait_ge(act_mu, 2 * k + 2)
                if not first:
                    dve.wait_ge(pe_xe, HC * k)
                stt(mu[:], rnd[:].bitcast(F32), cs[:, C_MA:C_MA + 1], raw_r[:, R_MU:R_MU + H], ALU.mult, ALU.add
                    ).then_inc(dve_mu, 1)

            def xe(b, e, r):
                for c in range(1, HC):
                    xe_sum(b, e, r, c)
                    xe_lo(b, e, c - 1)
                xe_lo(b, e, HC - 1)

            def xe_shared(b, c):
                dve.wait_ge(act_xe, HC * x_(b, NF) + c + 1)
                lo(xe_l[:, c, :], xnT[:, c, :], xe_h[:, c, :]).then_inc(dve_xe, 1)

            def xe_sum(b, e, r, c):
                dve.wait_ge(pe_xe, HC * r + c + 1)
                if c >= 2:
                    dve.wait_ge(dve_xe, HC * x_(b, e) + c - 1)
                tt_(xt[:, c % 2, :], bx[c][:], xnT[:, c, :], ALU.add).then_inc(dve_xt, 1)

            def xe_lo(b, e, c):
                dve.wait_ge(act_xe, HC * x_(b, e) + c + 1)
                lo(xe_l[:, c, :], xt[:, c % 2, :], xe_h[:, c, :]).then_inc(dve_xe, 1)

            def body(b, e, last, routed, nxt, ssm, start=False, proj=False):
                a, r = a_(b, e), (r_(b, e) if routed else None)
                if routed:
                    dve.wait_ge(pe_qa, r + 1)
                    dve.wait_ge(act_wrc, r + 1)
                    tt_(aw[:], b_q[:], wr_c[:], ALU.mult).then_inc(dve_aw, 1)
                    dve.wait_ge(act_aw, r + 1)
                    lo(aw_l[:], aw[:], aw_h[:]).then_inc(dve_awl, 1)
                more_r = routed and not (last and not nxt)
                if routed and start:
                    dve.wait_ge(dma_x, 16 * (b + 2))
                    stats(2 * (b + 1), xu, True)

                def hidden(m):
                    w = IW[m]
                    t = tt[0:w, m % 2, :]
                    dve.wait_ge(act_tanh, IC * a + m + 1)
                    stt(t, t, 1.0, bg[m][0:w, :], ALU.add, ALU.mult).then_inc(dve_g2, 1)
                    dve.wait_ge(dve_g2, IC * a + m + 1)
                    stt(t, t, 0.5, bu[m][0:w, :], ALU.mult, ALU.mult).then_inc(dve_h, 1)
                    if m > 0 and start and e == NF:
                        add_ssm(b + 1, 2 * m - 2)
                    dve.wait_ge(act_hh, IC * a + m + 1)
                    lo(hl[0:w, m, :], t, hh[0:w, m, :]).then_inc(dve_hl, 1)
                    if m > 0 and start and e == NF:
                        add_ssm(b + 1, 2 * m - 1)

                def tiles(*js):
                    if ssm and not proj:
                        for j in js:
                            tile(b + 1, e, j, ring)

                def add_down(tc):
                    dve.wait_ge(pe_dn, LC * a + tc + 2)
                    s_ = col(scal[:].rearrange("p c f -> p (c f)"), tc * NF + e) if routed else tgf[:]
                    stt(x1[:, tc, :], bd[tc][:], s_, x1[:, tc, :], ALU.mult, ALU.add).then_inc(dve_dn, 1)

                if start and e == NF:
                    gate_z(b + 1)
                tiles(0)
                if proj:
                    lo_state(b + 1)
                    selectors(b + 1, e, range(4))
                elif ssm:
                    selectors(b + 1, e, (2, 3))
                    if nxt:
                        selectors(b + 1, e + 1, (0, 1))
                tiles(1)
                hidden(0)
                if proj:
                    one_plus(b + 1)
                    mask_up(r + 1, False)
                    rest_of_w(b + 1)
                    softplus(b + 1)
                if start and e == NF:
                    y_gated(b + 1)
                if not proj:
                    split_d(a_(b, e) + 1, routed)
                if more_r and not proj:
                    mask_up(r + 1, False)
                tiles(2, 3)
                if proj:
                    ws_lo(r + 1)
                hidden(1)
                if nxt and not proj:
                    ws_lo(r + 1)
                if proj:
                    tile(b + 1, e, 0, ring)
                    tile(b + 1, e, 1, ring)
                tiles(4, 5)
                if nxt:
                    xe_sum(b, e + 1, r + 1, 0)
                    xe_sum(b, e + 1, r + 1, 1)
                hidden(2)
                if nxt:
                    xe_lo(b, e + 1, 0)
                    xe_sum(b, e + 1, r + 1, 2)
                    xe_lo(b, e + 1, 1)
                    if proj:
                        tile(b + 1, e, 2, ring)
                elif routed:
                    xe_shared(b, 0)
                    xe_shared(b, 1)
                if routed:
                    dve.wait_ge(pe_dqa, r + 1)
                    tt_(aw[:], b_q[:], wr_c[:], ALU.mult).then_inc(dve_aw, 1)
                if nxt:
                    xe_sum(b, e + 1, r + 1, 3)
                elif routed:
                    xe_shared(b, 2)
                if routed:
                    dve.wait_ge(act_daw, 2 * r + 1)
                    lo(daw_s[HALF:P, :], aw[HALF:P, :], rnd[HALF:P, :]).then_inc(dve_daw, 1)
                if nxt:
                    xe_lo(b, e + 1, 2)
                    xe_lo(b, e + 1, 3)
                elif routed:
                    xe_shared(b, 3)
                if start and e == NX - 1:
                    route(b + 1)
                tiles(6, 7)
                if more_r and nxt:
                    split_r(r + 1)
                if proj:
                    for j in range(3, 8):
                        tile(b + 1, e, j, ring)
                        if j == 3:
                            selectors(b + 1, e + 1, (0, 1))
                            add_down(0)
                            add_down(1)
                        elif j == 4:
                            add_down(2)
                            add_down(3)
                    return
                if start and e == NF:
                    dve.wait_ge(dve_x1, LC * (b + 2))
                    row_sums(2 * (b + 1) + 1, xu)
                add_down(0)
                add_down(1)
                add_down(2)
                add_down(3)
                if start and routed:
                    norm_z(b + 1)
                elif start and e == NF:
                    scales(2 * (b + 1) + 1, False)
                if more_r and not nxt:
                    split_r(r + 1)
                if start and e == NF:
                    norm_x1(b + 1)

            v.memset(yx[:], 0.0).then_inc(set_dve, 1)
            v.memset(ones[:], 1.0).then_inc(set_dve, 1)
            v.memset(sc[:], -1.0).then_inc(set_dve, 1)
            v.memset(pad[:, 7:8], 0.0).then_inc(dve_scan, PRIME)
            v.memset(pad[:, 8:9], 0.0).then_inc(dve_p, 8)
            v.memset(pad[:, 9:10], 0.0).then_inc(dve_dn, 1)
            v.memset(pad[:, 0:1], 0.0).then_inc(pe_dn, 1)
            v.memset(pad[:, 1:2], 0.0).then_inc(dve_daw, 1)
            v.memset(pad[:, 10:11], 0.0).then_inc(dma_out, 16)
            v.memset(pad[:, 11:12], 0.0).then_inc(set_dve, 1)
            dve.wait_ge(dma_cst, 32)
            v.tensor_scalar(cwh[:], cs[:, C_CW:C_CW + HC * TAPS], 0.5, None, ALU.mult).then_inc(set_dve, 1)
            v.tensor_scalar(cbh[:], cs[:, C_CB:C_CB + HC], 0.5, None, ALU.mult).then_inc(set_dve, 1)
            v.tensor_copy(inv_f[:], inv_i[:]).then_inc(set_dve, 1)
            dve.wait_ge(set_dve, 7)
            v.tensor_scalar(pm[:], inv_f[:], cs[0:NE, C_IO:C_IO + 1], None, ALU.is_equal).then_inc(set_dve, 1)
            dve.wait_ge(set_act, 3)
            v.tensor_scalar(a_neg[:], a_neg[:], -1.0, None, ALU.mult).then_inc(set_dve, 1)
            split_in(0)
            conv(0)
            make_u(0)
            dve.wait_ge(dma_x0, 16)
            stats(0, x1, True)
            for c in range(LC):
                normed(xnT, x1, c).then_inc(dve_zh, 1)
            lo_state(0)
            selectors(0, 0, (0, 1))
            one_plus(0)
            gate_z(0)
            rest_of_w(0)
            softplus(0)

            def tiles_0(e, more):
                for j in range(8):
                    tile(0, e, j, ring_0)
                    if j == 0:
                        selectors(0, e, (2, 3))
                        if more:
                            selectors(0, e + 1, (0, 1))

            with dve.Fori(0, NF - 1) as e:
                tiles_0(e, True)
            tiles_0(NF - 1, False)

            def batch(b, last, ssm, proj):
                body(b, 0, last, True, True, ssm, proj=proj)
                with dve.Fori(1, NF - 1) as e:
                    body(b, e, last, True, True, ssm)
                body(b, NF - 1, last, True, False, ssm, not last)
                body(b, NF, last, False, False, False, not last)
                body(b, NF + 1, last, False, False, False, not last)

            dve.wait_ge(dve_z, 1)
            dve.wait_ge(y_added, PRIME_Y + 64)
            for dc in range(HC):
                i = tt_(du[:, dc, :], four[dc][:], xnT[:, dc, :], ALU.mult)
            i.then_inc(dve_y3, 1)
            dve.wait_ge(dma_x, 16)
            for lc in range(LC):
                add_ssm(0, lc)
            dve.wait_ge(dve_x1, LC)
            stats(1, xu, False)
            norm_x1(0)
            mask_up(0, True)
            split_r(0)
            route(0)
            bridge(0, True)
            with dve.Fori(0, B - 2) as b:
                batch(b, False, True, True)
                bridge(b + 1, True)
            batch(B - 2, False, True, True)
            bridge(B - 1, False)
            batch(B - 1, True, False, False)


def kernel(**inputs):
    import numpy as np
    import concourse.bacc as bacc
    from concourse.bass_utils import run_bass_kernel_spmd

    def get(n):
        return np.asarray(inputs[n])

    def chunks(w, pad=0):
        k, n = w.shape
        if pad:
            w = np.concatenate([w, np.zeros((pad, n), w.dtype)])
        return w.reshape(-1, P, n).transpose(1, 0, 2).reshape(P, -1)

    x = np.ascontiguousarray(get("x"))
    f32 = x.dtype
    ctxT = np.stack([chunks(c.T) for c in get("ctx_1024")])
    w = {n: get("L0_ffn_" + n) for n in ("mask_up_W", "gate_W", "gate_qa", "gate_qb", "gate_scale", "up_W", "up_qa",
                                         "up_qb", "up_scale", "down_W", "down_qa", "down_qb", "down_scale",
                                         "sh_gate_W", "sh_up_W", "sh_down_W", "gate_weight", "inv_mapping")}
    m = {n: get("L0_xattn_" + n) for n in ("in_proj_w", "conv_w", "conv_b", "x_proj_w", "dt_proj_w", "dt_proj_b",
                                           "A_log", "D")}
    gu, dd, rr = [], [], []
    pad = IC * P - I
    for f in range(NF):
        gu.append(np.concatenate([chunks(w["gate_W"][f].T), chunks(w["up_W"][f].T)], 1))
        qa = w["down_qa"][f].reshape(KR, I).T
        qb = w["down_qb"][f].transpose(0, 2, 1).reshape(KR, H)
        dd.append(np.concatenate([chunks(w["down_W"][f].T, pad), chunks(np.concatenate([qa, qa], 1), pad),
                                  np.concatenate([qb, qb]), np.broadcast_to(w["down_scale"][f], (P, H))], 1))
        qa = np.concatenate([w["gate_qa"][f].reshape(KR, H), w["up_qa"][f].reshape(KR, H)])
        qb = np.concatenate([w[n][f].transpose(0, 2, 1).reshape(KR, I) for n in ("gate_qb", "up_qb")])
        qs = np.concatenate([np.broadcast_to(w[n][f], (HALF, I)) for n in ("gate_scale", "up_scale")])
        mup = np.repeat(w["mask_up_W"][f].T, NR, 0)
        p_, c_ = np.arange(P)[:, None] % HALF, np.arange(P)[None, :] % HALF
        selr = (p_ == f * NK + c_ // NR).astype(f32)
        rr.append(np.concatenate([chunks(qa.T), qb, qs, np.concatenate([mup, mup]), selr], 1))
    for s in range(2):
        rows = slice(s * I, (s + 1) * I)
        gu.append(np.concatenate([chunks(w["sh_gate_W"][rows].T), chunks(w["sh_up_W"][rows].T)], 1))
        d = chunks(w["sh_down_W"][:, rows].T, pad)
        dd.append(np.concatenate([d, np.zeros((P, D_ALL - IC * H), f32)], 1))
    xp = np.zeros((H, P), f32)
    xp[:, 0:DR + 2 * NS] = xp[:, HALF:HALF + DR + 2 * NS] = m["x_proj_w"].T
    dt = np.zeros((P, H), f32)
    dt[0:DR] = dt[HALF:HALF + DR] = m["dt_proj_w"].T
    pre = np.concatenate([chunks(m["in_proj_w"].T), chunks(xp), dt], 1)
    i = np.arange(P)[:, None]
    j = np.arange(2 * NS)[None, :]
    cst = np.concatenate([
        np.eye(P), 1 * (i % NR == 0) - 1 * ((i < HALF) & (i % NR == 1)), (i < HALF) & (i % NR == 1), i % HALF == DR + j,
        chunks(m["A_log"]), chunks(m["conv_w"]), chunks(m["conv_b"][:, None]), chunks(m["dt_proj_b"][:, None]),
        chunks(m["D"][:, None]), chunks(w["gate_weight"].T), np.broadcast_to(get("g_xattn"), (P, 1)),
        np.broadcast_to(get("g_ffn"), (P, 1)), i], 1).astype(f32)
    arrays = {"x": x, "ctxT": ctxT, "gu": np.stack(gu), "dd": np.stack(dd), "pre": pre, "rr": np.stack(rr),
              "cst": cst, "inv": w["inv_mapping"].reshape(-1)}
    nc = bacc.Bacc("TRN2", target_bir_lowering=False, num_devices=1)
    args, feed = [], {}
    for n, a in arrays.items():
        a = np.ascontiguousarray(a)
        feed[f"in_{n}"] = a
        args.append(nc.dram_tensor(f"in_{n}", a.shape, mybir.dt.from_np(a.dtype), kind="ExternalInput").ap())
    args.append(nc.dram_tensor("out_0", x.shape, F32, kind="ExternalOutput").ap())
    gated_ssm_moe(nc, *args)
    r = run_bass_kernel_spmd(nc, [feed], core_ids=[0])
    return r.results[0]["out_0"]
```
